# Optimizing a Trainium2 kernel written in Bass

```python
import numpy as np
import jax
import jax.numpy as jnp

def _softmax(x, axis=-1):
    return jax.nn.softmax(x, axis=axis)

def _gelu(x):
    return jax.nn.gelu(x, approximate=True)

def _silu(x):
    return jax.nn.silu(x)

def _sigmoid(x):
    return jax.nn.sigmoid(x)

def _layernorm(x, axis=-1, eps=1e-05):
    m = jnp.mean(x, axis=axis, keepdims=True)
    v = jnp.var(x, axis=axis, keepdims=True)
    return (x - m) / jnp.sqrt(v + eps)

def _scatter_add(tgt, idx, src, axis=0):
    return tgt.at[idx].add(src)

def _segment_sum(src, seg, n):
    return jax.ops.segment_sum(src, seg, n)
kernel_name = 'mk_lm_tower_d2_tok_ids1024_r4_d6eb86'

def setup_inputs(seed: int=0):
    np.random.seed(seed)
    _w = jnp.asarray

    def _rec_inputs():
        import jax
        import jax.numpy as jnp
        _rk = jax.random.key(seed)
        x = jax.random.randint(jax.random.fold_in(_rk, 1), (4, 1024), 0, 50226, jnp.int32)
        return x
    x = _rec_inputs()

    def _L0_tok_setup():
        import jax, jax.numpy as jnp
        import numpy as np
        import math
        V, D, B, S = (50257, 256, 16, 128)
        EPS = 1e-06

        def _pos_enc(seq_len: int, dim: int) -> jnp.ndarray:
            position = jnp.arange(seq_len, dtype=jnp.float32)[:, None]
            div_term = jnp.exp(jnp.arange(0, dim, 2, dtype=jnp.float32) * (-math.log(10000.0) / dim))
            ang = position * div_term
            return jnp.stack([jnp.sin(ang), jnp.cos(ang)], axis=-1).reshape(seq_len, dim)
        key = jax.random.key(seed)
        k1, k2 = jax.random.split(key)
        x = jax.random.randint(k1, (B, S), 0, V, dtype=jnp.int32)
        emb = jax.random.normal(k2, (V, D), dtype=jnp.float32)
        alpha = jnp.ones((D,), dtype=jnp.float32)
        beta = jnp.zeros((D,), dtype=jnp.float32)
        return {'x': x, 'emb': emb, 'alpha': alpha, 'beta': beta}
    _L0_tok_all = _L0_tok_setup()
    _L0_tok_in = {k: v for k, v in _L0_tok_all.items() if k in ('emb', 'alpha', 'beta')}
    del _L0_tok_all

    def _L0_attn_setup():
        import jax, jax.numpy as jnp
        import numpy as np
        import math
        D_MODEL = 256
        LAYER_ID = 6
        NUM_LAYERS = 12
        B, T = (8, 512)
        MIN_P = -1e+38

        def _init_params():
            C = D_MODEL
            r01 = LAYER_ID / (NUM_LAYERS - 1)
            r1a0 = 1.0 - LAYER_ID / NUM_LAYERS
            h = np.arange(C, dtype=np.float32)
            decay_speed = -5.0 + 8.0 * (h / (C - 1)) ** (0.7 + 1.3 * r01)
            zigzag = ((np.arange(C) + 1) % 3 - 1).astype(np.float32) * 0.5
            U = np.float32(math.log(0.3)) + zigzag
            xx = (np.arange(C, dtype=np.float32) / C).reshape(1, 1, C)
            tmk = xx ** r1a0
            tmv = xx ** r1a0 + 0.3 * r01
            tmr = xx ** (0.5 * r1a0)
            return (jnp.asarray(decay_speed), jnp.asarray(U), jnp.asarray(tmk, jnp.float32), jnp.asarray(tmv, jnp.float32), jnp.asarray(tmr, jnp.float32))

        def _wkv(W, U, k, v):
            w = -jnp.exp(W)
            Bb, Tt, Cc = k.shape
            aa0 = jnp.zeros((Bb, Cc), k.dtype)
            bb0 = jnp.zeros((Bb, Cc), k.dtype)
            pp0 = jnp.full((Bb, Cc), MIN_P, k.dtype)

            def step(carry, kv_t):
                aa, bb, pp = carry
                kt, vt = kv_t
                ww = U + kt
                p = jnp.maximum(pp, ww)
                e1 = jnp.exp(pp - p)
                e2 = jnp.exp(ww - p)
                y = (e1 * aa + e2 * vt) / (e1 * bb + e2)
                ww2 = pp + w
                p2 = jnp.maximum(ww2, kt)
                e1b = jnp.exp(ww2 - p2)
                e2b = jnp.exp(kt - p2)
                return ((e1b * aa + e2b * vt, e1b * bb + e2b, p2), y)
            kT = jnp.swapaxes(k, 0, 1)
            vT = jnp.swapaxes(v, 0, 1)
            _, yT = jax.lax.scan(step, (aa0, bb0, pp0), (kT, vT))
            return jnp.swapaxes(yT, 0, 1)

        def _reference_tuple_inner(x, W, U, time_mix_k, time_mix_v, time_mix_r, Wk, Wv, Wr, Wo):
            xs = jnp.pad(x, ((0, 0), (1, 0), (0, 0)))[:, :-1]
            xk = x * time_mix_k + xs * (1.0 - time_mix_k)
            xv = x * time_mix_v + xs * (1.0 - time_mix_v)
            xr = x * time_mix_r + xs * (1.0 - time_mix_r)
            K = jnp.einsum('btc,dc->btd', xk, Wk)
            V = jnp.einsum('btc,dc->btd', xv, Wv)
            R = jnp.einsum('btc,dc->btd', xr, Wr)
            wkv = _wkv(W, U, K, V)
            hidden = jax.lax.stop_gradient(wkv[:, -1, :])
            rwkv = jax.nn.sigmoid(R) * wkv
            output = jnp.einsum('btc,dc->btd', rwkv, Wo)
            return (output, hidden)
        key = jax.random.key(seed)
        k0, k1, k2, k3, k4 = jax.random.split(key, 5)
        W, U, tmk, tmv, tmr = _init_params()
        C = D_MODEL
        s = 1.0 / math.sqrt(C)
        return {'x': jax.random.normal(k0, (B, T, C), jnp.float32), 'W': W, 'U': U, 'time_mix_k': tmk, 'time_mix_v': tmv, 'time_mix_r': tmr, 'Wk': jax.random.normal(k1, (C, C), jnp.float32) * s, 'Wv': jax.random.normal(k2, (C, C), jnp.float32) * s, 'Wr': jax.random.normal(k3, (C, C), jnp.float32) * s, 'Wo': jax.random.normal(k4, (C, C), jnp.float32) * s}
    _L0_attn_all = _L0_attn_setup()
    _L0_attn_in = {k: v for k, v in _L0_attn_all.items() if k in ('W', 'U', 'time_mix_k', 'time_mix_v', 'time_mix_r', 'Wk', 'Wv', 'Wr', 'Wo')}
    del _L0_attn_all

    def _L0_ffn_setup():
        import jax, jax.numpy as jnp
        import numpy as np
        B, T, D, E, K = (2, 512, 256, 8, 2)
        H = 2 * D
        key = jax.random.key(seed)
        ks = jax.random.split(key, 5)
        s = 0.02
        return {'x': jax.random.normal(ks[0], (B, T, D), jnp.float32), 'Wr': jax.random.normal(ks[1], (D, E), jnp.float32) * s, 'br': jnp.zeros((E,), jnp.float32), 'W1': jax.random.normal(ks[2], (E, D, H), jnp.float32) * s, 'b1': jnp.zeros((E, H), jnp.float32), 'W2': jax.random.normal(ks[3], (E, H, D), jnp.float32) * s, 'b2': jnp.zeros((E, D), jnp.float32)}
    _L0_ffn_all = _L0_ffn_setup()
    _L0_ffn_in = {k: v for k, v in _L0_ffn_all.items() if k in ('Wr', 'br', 'W1', 'b1', 'W2', 'b2')}
    del _L0_ffn_all

    def _L1_attn_setup():
        import jax, jax.numpy as jnp
        import numpy as np
        HIDDEN = 256
        HEADS = 16
        HEAD_DIM = HIDDEN // HEADS
        BLOCK = 256
        B, S = (1, 1024)

        def _ring_attention(q, k, v, block, scale):
            b, h, s, d = q.shape
            nb = s // block
            kb = jnp.moveaxis(k.reshape(b, h, nb, block, d), 2, 0)
            vb = jnp.moveaxis(v.reshape(b, h, nb, block, d), 2, 0)

            def step(carry, kv):
                num, den = carry
                k_blk, v_blk = kv
                s_blk = jnp.einsum('bhqd,bhkd->bhqk', q, k_blk) * scale
                m = jnp.max(s_blk, axis=-1, keepdims=True)
                e = jnp.exp(s_blk - m)
                num = num + jnp.einsum('bhqk,bhkd->bhqd', e, v_blk)
                den = den + jnp.sum(e, axis=-1, keepdims=True)
                return ((num, den), None)
            init = (jnp.zeros_like(q), jnp.zeros((b, h, s, 1), dtype=q.dtype))
            (num, den), _ = jax.lax.scan(step, init, (kb, vb))
            return num / den
        key = jax.random.key(seed)
        k0, k1, k2, k3, k4 = jax.random.split(key, 5)
        w_scale = 0.02
        return {'hidden_states': jax.random.normal(k0, (B, S, HIDDEN), dtype=jnp.float32), 'w_q': jax.random.normal(k1, (HIDDEN, HIDDEN), dtype=jnp.float32) * w_scale, 'w_k': jax.random.normal(k2, (HIDDEN, HIDDEN), dtype=jnp.float32) * w_scale, 'w_v': jax.random.normal(k3, (HIDDEN, HIDDEN), dtype=jnp.float32) * w_scale, 'w_o': jax.random.normal(k4, (HIDDEN, HIDDEN), dtype=jnp.float32) * w_scale}
    _L1_attn_all = _L1_attn_setup()
    _L1_attn_in = {k: v for k, v in _L1_attn_all.items() if k in ('w_q', 'w_k', 'w_v', 'w_o')}
    del _L1_attn_all

    def _L1_ffn_setup():
        import jax, jax.numpy as jnp
        import numpy as np
        key = jax.random.key(seed)
        k0, k1, k2, k3 = jax.random.split(key, 4)
        B, S, D, F, E = (8, 512, 256, 512, 8)
        x = jax.random.normal(k0, (B, S, D), dtype=jnp.float32)
        Wg = jax.random.normal(k1, (D, E), dtype=jnp.float32) * 0.02
        W1 = jax.random.normal(k2, (E, D, F), dtype=jnp.float32) * 0.02
        W2 = jax.random.normal(k3, (E, F, D), dtype=jnp.float32) * 0.02
        return {'x': x, 'Wg': Wg, 'W1': W1, 'W2': W2}
    _L1_ffn_all = _L1_ffn_setup()
    _L1_ffn_in = {k: v for k, v in _L1_ffn_all.items() if k in ('Wg', 'W1', 'W2')}
    del _L1_ffn_all
    return {'x': x, 'L0_tok_emb': _L0_tok_in['emb'], 'L0_tok_alpha': _L0_tok_in['alpha'], 'L0_tok_beta': _L0_tok_in['beta'], 'L0_attn_W': _L0_attn_in['W'], 'L0_attn_U': _L0_attn_in['U'], 'L0_attn_time_mix_k': _L0_attn_in['time_mix_k'], 'L0_attn_time_mix_v': _L0_attn_in['time_mix_v'], 'L0_attn_time_mix_r': _L0_attn_in['time_mix_r'], 'L0_attn_Wk': _L0_attn_in['Wk'], 'L0_attn_Wv': _L0_attn_in['Wv'], 'L0_attn_Wr': _L0_attn_in['Wr'], 'L0_attn_Wo': _L0_attn_in['Wo'], 'L0_ffn_Wr': _L0_ffn_in['Wr'], 'L0_ffn_br': _L0_ffn_in['br'], 'L0_ffn_W1': _L0_ffn_in['W1'], 'L0_ffn_b1': _L0_ffn_in['b1'], 'L0_ffn_W2': _L0_ffn_in['W2'], 'L0_ffn_b2': _L0_ffn_in['b2'], 'L1_attn_w_q': _L1_attn_in['w_q'], 'L1_attn_w_k': _L1_attn_in['w_k'], 'L1_attn_w_v': _L1_attn_in['w_v'], 'L1_attn_w_o': _L1_attn_in['w_o'], 'L1_ffn_Wg': _L1_ffn_in['Wg'], 'L1_ffn_W1': _L1_ffn_in['W1'], 'L1_ffn_W2': _L1_ffn_in['W2']}

def reference(x, L0_tok_emb, L0_tok_alpha, L0_tok_beta, L0_attn_W, L0_attn_U, L0_attn_time_mix_k, L0_attn_time_mix_v, L0_attn_time_mix_r, L0_attn_Wk, L0_attn_Wv, L0_attn_Wr, L0_attn_Wo, L0_ffn_Wr, L0_ffn_br, L0_ffn_W1, L0_ffn_b1, L0_ffn_W2, L0_ffn_b2, L1_attn_w_q, L1_attn_w_k, L1_attn_w_v, L1_attn_w_o, L1_ffn_Wg, L1_ffn_W1, L1_ffn_W2):
    import jax
    import jax.numpy as jnp

    def _L0_tok_ref(x, emb, alpha, beta):
        import jax, jax.numpy as jnp
        import numpy as np
        import math
        V, D, B, S = (50257, 256, 16, 128)
        EPS = 1e-06

        def _pos_enc(seq_len: int, dim: int) -> jnp.ndarray:
            position = jnp.arange(seq_len, dtype=jnp.float32)[:, None]
            div_term = jnp.exp(jnp.arange(0, dim, 2, dtype=jnp.float32) * (-math.log(10000.0) / dim))
            ang = position * div_term
            return jnp.stack([jnp.sin(ang), jnp.cos(ang)], axis=-1).reshape(seq_len, dim)
        seq_len = x.shape[1]
        y = emb[x] + _pos_enc(seq_len, emb.shape[1])[None, :, :]
        mean = jnp.mean(y, axis=-1, keepdims=True)
        sigma = jnp.std(y, axis=-1, keepdims=True, ddof=1) + EPS
        return alpha * ((y - mean) / sigma + beta)

    def _L0_attn_ref(x, W, U, time_mix_k, time_mix_v, time_mix_r, Wk, Wv, Wr, Wo):
        import jax, jax.numpy as jnp
        import numpy as np
        import math
        D_MODEL = 256
        LAYER_ID = 6
        NUM_LAYERS = 12
        B, T = (8, 512)
        MIN_P = -1e+38

        def _init_params():
            C = D_MODEL
            r01 = LAYER_ID / (NUM_LAYERS - 1)
            r1a0 = 1.0 - LAYER_ID / NUM_LAYERS
            h = np.arange(C, dtype=np.float32)
            decay_speed = -5.0 + 8.0 * (h / (C - 1)) ** (0.7 + 1.3 * r01)
            zigzag = ((np.arange(C) + 1) % 3 - 1).astype(np.float32) * 0.5
            U = np.float32(math.log(0.3)) + zigzag
            xx = (np.arange(C, dtype=np.float32) / C).reshape(1, 1, C)
            tmk = xx ** r1a0
            tmv = xx ** r1a0 + 0.3 * r01
            tmr = xx ** (0.5 * r1a0)
            return (jnp.asarray(decay_speed), jnp.asarray(U), jnp.asarray(tmk, jnp.float32), jnp.asarray(tmv, jnp.float32), jnp.asarray(tmr, jnp.float32))

        def _wkv(W, U, k, v):
            w = -jnp.exp(W)
            Bb, Tt, Cc = k.shape
            aa0 = jnp.zeros((Bb, Cc), k.dtype)
            bb0 = jnp.zeros((Bb, Cc), k.dtype)
            pp0 = jnp.full((Bb, Cc), MIN_P, k.dtype)

            def step(carry, kv_t):
                aa, bb, pp = carry
                kt, vt = kv_t
                ww = U + kt
                p = jnp.maximum(pp, ww)
                e1 = jnp.exp(pp - p)
                e2 = jnp.exp(ww - p)
                y = (e1 * aa + e2 * vt) / (e1 * bb + e2)
                ww2 = pp + w
                p2 = jnp.maximum(ww2, kt)
                e1b = jnp.exp(ww2 - p2)
                e2b = jnp.exp(kt - p2)
                return ((e1b * aa + e2b * vt, e1b * bb + e2b, p2), y)
            kT = jnp.swapaxes(k, 0, 1)
            vT = jnp.swapaxes(v, 0, 1)
            _, yT = jax.lax.scan(step, (aa0, bb0, pp0), (kT, vT))
            return jnp.swapaxes(yT, 0, 1)

        def _reference_tuple_inner(x, W, U, time_mix_k, time_mix_v, time_mix_r, Wk, Wv, Wr, Wo):
            xs = jnp.pad(x, ((0, 0), (1, 0), (0, 0)))[:, :-1]
            xk = x * time_mix_k + xs * (1.0 - time_mix_k)
            xv = x * time_mix_v + xs * (1.0 - time_mix_v)
            xr = x * time_mix_r + xs * (1.0 - time_mix_r)
            K = jnp.einsum('btc,dc->btd', xk, Wk)
            V = jnp.einsum('btc,dc->btd', xv, Wv)
            R = jnp.einsum('btc,dc->btd', xr, Wr)
            wkv = _wkv(W, U, K, V)
            hidden = jax.lax.stop_gradient(wkv[:, -1, :])
            rwkv = jax.nn.sigmoid(R) * wkv
            output = jnp.einsum('btc,dc->btd', rwkv, Wo)
            return (output, hidden)
        return _reference_tuple_inner(x, W, U, time_mix_k, time_mix_v, time_mix_r, Wk, Wv, Wr, Wo)[0]

    def _L0_ffn_ref(x, Wr, br, W1, b1, W2, b2):
        import jax, jax.numpy as jnp
        import numpy as np
        B, T, D, E, K = (2, 512, 256, 8, 2)
        H = 2 * D
        logits = jnp.einsum('btd,de->bte', x, Wr) + br
        topv, topi = jax.lax.top_k(logits, K)
        sel_mask = jax.nn.one_hot(topi, E, dtype=logits.dtype).sum(-2) > 0
        neg_inf = jnp.finfo(logits.dtype).min
        gates = jax.nn.softmax(jnp.where(sel_mask, logits, neg_inf), axis=-1)
        h = jax.nn.relu(jnp.einsum('btd,edh->bteh', x, W1) + b1)
        out = jnp.einsum('bte,bteh,ehd->btd', gates, h, W2)
        out = out + jnp.einsum('bte,ed->btd', gates, b2)
        return out

    def _L1_attn_ref(hidden_states, w_q, w_k, w_v, w_o):
        import jax, jax.numpy as jnp
        import numpy as np
        HIDDEN = 256
        HEADS = 16
        HEAD_DIM = HIDDEN // HEADS
        BLOCK = 256
        B, S = (1, 1024)

        def _ring_attention(q, k, v, block, scale):
            b, h, s, d = q.shape
            nb = s // block
            kb = jnp.moveaxis(k.reshape(b, h, nb, block, d), 2, 0)
            vb = jnp.moveaxis(v.reshape(b, h, nb, block, d), 2, 0)

            def step(carry, kv):
                num, den = carry
                k_blk, v_blk = kv
                s_blk = jnp.einsum('bhqd,bhkd->bhqk', q, k_blk) * scale
                m = jnp.max(s_blk, axis=-1, keepdims=True)
                e = jnp.exp(s_blk - m)
                num = num + jnp.einsum('bhqk,bhkd->bhqd', e, v_blk)
                den = den + jnp.sum(e, axis=-1, keepdims=True)
                return ((num, den), None)
            init = (jnp.zeros_like(q), jnp.zeros((b, h, s, 1), dtype=q.dtype))
            (num, den), _ = jax.lax.scan(step, init, (kb, vb))
            return num / den
        b, s, _ = hidden_states.shape
        q = (hidden_states @ w_q).reshape(b, s, HEADS, HEAD_DIM).transpose(0, 2, 1, 3)
        k = (hidden_states @ w_k).reshape(b, s, HEADS, HEAD_DIM).transpose(0, 2, 1, 3)
        v = (hidden_states @ w_v).reshape(b, s, HEADS, HEAD_DIM).transpose(0, 2, 1, 3)
        scale = HEAD_DIM ** (-0.5)
        out = _ring_attention(q, k, v, BLOCK, scale)
        out = out.transpose(0, 2, 1, 3).reshape(b, s, HIDDEN)
        return out @ w_o

    def _L1_ffn_ref(x, Wg, W1, W2):
        import jax, jax.numpy as jnp
        import numpy as np
        B, S, D = x.shape
        E = Wg.shape[1]
        T = B * S
        cap = max(1, T // E)
        xt = x.reshape(T, D)
        logits = xt @ Wg
        probs = jax.nn.softmax(logits, axis=-1)
        pT = probs.T
        _, top_idx = jax.lax.top_k(pT, cap)
        sel = jnp.zeros((E, T), dtype=bool).at[jnp.arange(E)[:, None], top_idx].set(True)
        masked = jnp.where(sel, pT, -jnp.inf)
        assigned = sel.any(axis=0)
        tok2exp = jnp.where(assigned, jnp.argmax(masked, axis=0), jnp.argmax(pT, axis=0))
        weights = jnp.take_along_axis(probs, tok2exp[:, None], axis=1)[:, 0]
        out = jnp.zeros_like(xt)
        for e in range(E):
            gate = jnp.where(tok2exp == e, weights, 0.0)
            h = jax.nn.gelu(xt @ W1[e], approximate=False) @ W2[e]
            out = out + gate[:, None] * h
        return out.reshape(B, S, D)
    h = _L0_tok_ref(x, L0_tok_emb, L0_tok_alpha, L0_tok_beta)
    h = h + _L0_attn_ref(_layernorm(h, axis=-1), L0_attn_W, L0_attn_U, L0_attn_time_mix_k, L0_attn_time_mix_v, L0_attn_time_mix_r, L0_attn_Wk, L0_attn_Wv, L0_attn_Wr, L0_attn_Wo)
    h = h + _L0_ffn_ref(_layernorm(h, axis=-1), L0_ffn_Wr, L0_ffn_br, L0_ffn_W1, L0_ffn_b1, L0_ffn_W2, L0_ffn_b2)
    h = h + _L1_attn_ref(_layernorm(h, axis=-1), L1_attn_w_q, L1_attn_w_k, L1_attn_w_v, L1_attn_w_o)
    h = h + _L1_ffn_ref(_layernorm(h, axis=-1), L1_ffn_Wg, L1_ffn_W1, L1_ffn_W2)
    return h

_drawn_inputs = setup_inputs


def setup_inputs(seed=0):
    import zlib

    import numpy as np

    out = dict(_drawn_inputs(seed))
    spreads = {'L0_tok_alpha': (1.0, 0.2),
     'L0_tok_beta': (0.0, 0.1),
     'L0_ffn_br': (0.0, 0.1),
     'L0_ffn_b1': (0.0, 0.395),
     'L0_ffn_b2': (0.0, 0.1)}
    factors = {'L1_attn_w_q': 8.0,
     'L1_attn_w_k': 8.0,
     'L1_ffn_Wg': 4.394,
     'L1_ffn_W1': 4.126,
     'L1_ffn_W2': 4.046}
    for name, (base, spread) in spreads.items():
        noise = np.random.default_rng([zlib.crc32(name.encode()), seed]).standard_normal(out[name].shape)
        drawn = base * np.exp(spread * noise) if base else spread * noise
        out[name] = jnp.asarray(drawn.astype(out[name].dtype))
    for name, factor in factors.items():
        out[name] = (out[name] * factor).astype(out[name].dtype)
    return out
```

```python
from contextlib import ExitStack

import concourse.bass as bass
import numpy as np
from concourse import mybir

F32 = mybir.dt.float32
BF16 = mybir.dt.bfloat16
I32 = mybir.dt.int32
U16 = mybir.dt.uint16
ALU = mybir.AluOpType
ACT = mybir.ActivationFunctionType
AX_X = mybir.AxisListType.X

P = 128
B, S, D = 4, 1024, 256
T = B * S
NT = T // P
TB = S // P
C = D // P
CHUNK = 512
NC = S // CHUNK
E = 8
HID = 512
HC = HID // P
FAR = -1e38
LN_EPS = 1e-5
ds = bass.ds


def allocators(nc, ctx):
    sems = []

    def sem(name):
        sems.append(nc.alloc_semaphore(name))
        return sems[-1]

    def clear():
        nc.clear_and_free_semaphores(sems)
        nc.all_engine_barrier()

    ctx.callback(clear)
    return (lambda name, shape, dt: ctx.enter_context(nc.sbuf_tensor(name, shape, dt)),
            lambda name, shape, dt: ctx.enter_context(nc.psum_tensor(name, shape, dt)), sem)


def need(eng, s, count):
    if isinstance(count, int) and count <= 0:
        return
    eng.wait_ge(s, count)


def over_sequences(eng, sequence):
    sequence(0)
    with eng.Fori(1, B) as b:
        sequence(b)


class Steps:

    def __init__(self, eng, sem, base=0):
        self.eng, self.sem, self.base, self.n = eng, sem, base, 0

    def mark(self, ins):
        ins.then_inc(self.sem, 1)
        self.n += 1
        return self.n

    def wait(self, n=None):
        self.eng.wait_ge(self.sem, self.base + (self.n if n is None else n))

    def step(self, ins):
        self.mark(ins)
        self.wait()


def embed(nc, st, tok_ids, emb, pos, alpha, beta):
    h, ident = st["h"], st["ident"]
    with ExitStack() as ctx:
        sb, pb, sem = allocators(nc, ctx)
        tok_idx = sb("tok_idx", [P, NT], I32)
        pos_sb = sb("pos_sb", [P, TB * D], F32)
        alpha_all = sb("alpha_all", [P, D], F32)
        beta_all = sb("beta_all", [P, D], F32)
        stats = sb("em_stats", [P, NT * 6], F32)
        mv = sb("em_mv", [P, NT * 2], F32)
        dev = sb("em_dev", [P, NT], F32)
        rec = sb("em_rec", [P, NT], F32)
        idx_in = sem("em_idx_in")
        const_in = sem("em_const_in")
        rows0 = sem("em_rows0")
        rows1 = sem("em_rows1")
        rows2 = sem("em_rows2")
        rows3 = sem("em_rows3")
        own = sem("em_own")
        ident0 = sem("em_ident0")
        mv_ready = sem("em_mv_ready")
        dev_ready = sem("em_dev_ready")
        block = ctx.enter_context(nc.Block())
        rows_in = [rows0, rows1, rows2, rows3]

        @block.sync
        def _(sp):
            sp.dma_start(tok_idx[:, :], tok_ids).then_inc(idx_in, 16)
            sp.dma_start(pos_sb[:, :].rearrange("p (n d) -> p n d", d=D), pos.rearrange("(n p) d -> p n d", p=P)).then_inc(const_in, 16)
            sp.dma_start(alpha_all[:, :], alpha.partition_broadcast(P)).then_inc(const_in, 16)
            sp.dma_start(beta_all[:, :], beta.partition_broadcast(P)).then_inc(const_in, 16)

        @block.gpsimd
        def _(pool):
            pool.memset(ident[:, :], 0.0).then_inc(ident0, 1)
            pool.wait_ge(ident0, 1)
            pool.affine_select(out=ident[:, :], in_=ident[:, :], compare_op=ALU.not_equal, fill=1.0, base=0,
                               pattern=[[-1, P]], channel_multiplier=1).then_inc(ident0, 1)
            pool.wait_ge(idx_in, 16)
            for n in range(NT):
                pool.indirect_dma_start(out=h[:, n * D:(n + 1) * D], out_offset=None, in_=emb,
                                        in_offset=bass.IndirectOffsetOnAxis(ap=tok_idx[:, n:n + 1], axis=0),
                                        ).then_inc(rows_in[n // TB], 16)

        @block.scalar
        def _(act):
            act.wait_ge(mv_ready, 1)
            act.activation(dev[:, :], mv[:, 1::2], ACT.Sqrt, scale=D / (D - 1.0)).then_inc(dev_ready, 1)

        @block.vector
        def _(dve):
            s = Steps(dve, own)
            dve.wait_ge(const_in, 48)
            for b in range(B):
                dve.wait_ge(rows_in[b], 16 * TB)
                hb = h[:, b * TB * D:(b + 1) * TB * D]
                s.step(dve.tensor_tensor(hb, hb, pos_sb[:, :], ALU.add))
                for n in range(b * TB, (b + 1) * TB):
                    dve.bn_stats(stats[:, n * 6:(n + 1) * 6], h[:, n * D:(n + 1) * D])
            dve.drain()
            for n in range(NT):
                dve.bn_aggr(mv[:, n * 2:(n + 1) * 2], stats[:, n * 6:(n + 1) * 6])
            dve.drain()
            dve.nop().then_inc(mv_ready, 1)
            dve.wait_ge(dev_ready, 1)
            s.step(dve.tensor_scalar_add(dev[:, :], dev[:, :], 1e-6))
            s.step(dve.reciprocal(rec[:, :], dev[:, :]))
            with dve.Fori(0, B) as b:
                for k in range(TB):
                    n = b * TB + k
                    hn = h[:, ds(n * D, D)]
                    dve.tensor_scalar(hn, hn, mv[:, ds(n * 2, 1)], rec[:, ds(n, 1)], ALU.subtract, ALU.mult)
            dve.drain()
            every = h[:, :].rearrange("p (n d) -> p n d", d=D)
            s.step(dve.tensor_tensor(every, every, beta_all[:, :].unsqueeze(1).to_broadcast([P, NT, D]), ALU.add))
            s.step(dve.tensor_tensor(every, every, alpha_all[:, :].unsqueeze(1).to_broadcast([P, NT, D]), ALU.mult))


def layer_norm(nc, st, tag, after_stats=None):
    h, mv, rstd = st["h"], st["mv"], st["rstd"]
    with ExitStack() as ctx:
        sb, pb, sem = allocators(nc, ctx)
        stats = sb(tag + "_stats", [P, NT * 6], F32)
        var = sb(tag + "_var", [P, NT], F32)
        dev = sb(tag + "_dev", [P, NT], F32)
        var_ready = sem(tag + "_var_ready")
        dev_ready = sem(tag + "_dev_ready")
        own = sem(tag + "_own")
        block = ctx.enter_context(nc.Block())

        @block.scalar
        def _(act):
            act.wait_ge(var_ready, 1)
            act.activation(dev[:, :], var[:, :], ACT.Sqrt).then_inc(dev_ready, 1)

        @block.vector
        def _(dve):
            with dve.Fori(0, B) as b:
                for n in range(TB):
                    dve.bn_stats(stats[:, ds((b * TB + n) * 6, 6)], h[:, ds((b * TB + n) * D, D)])
            dve.drain()
            for n in range(NT):
                dve.bn_aggr(mv[:, n * 2:(n + 1) * 2], stats[:, n * 6:(n + 1) * 6])
            dve.drain()
            dve.tensor_scalar_add(var[:, :], mv[:, 1::2], LN_EPS).then_inc(var_ready, 1)
            dve.wait_ge(dev_ready, 1)
            dve.reciprocal(rstd[:, :], dev[:, :]).then_inc(own, 1)
            dve.wait_ge(own, 1)


def rwkv(nc, st, decay, bonus, mix_k, mix_v, mix_r, wk, wv, wr, wo):
    h, mv, rstd, ident = st["h"], st["mv"], st["rstd"], st["ident"]
    with ExitStack() as ctx:
        sb, pb, sem = allocators(nc, ctx)
        w_sb = sb("rw_w", [P, 4 * C * D], F32)
        cols = sb("rw_cols", [P, 5 * C], F32)
        neg_w = sb("rw_nw", [P, C], F32)
        xn = sb("rw_xn", [P, TB * D], F32)
        xt = sb("rw_xt", [P, C * (S + 1)], F32)
        dif = sb("rw_dif", [P, C * S], F32)
        mix = sb("rw_mix", [P, 3 * C * S], F32)
        kvr = sb("rw_kvr", [P, 3 * C * S], F32)
        run_max = sb("rw_max", [P, S + 1], F32)
        aa = sb("rw_aa", [P, S + 1], F32)
        bb = sb("rw_bb", [P, S + 1], F32)
        expo = sb("rw_f", [P, 4 * S], F32)
        ex = sb("rw_e", [P, 4 * S], F32)
        tmp = sb("rw_t", [P, 3 * S], F32)
        gated = sb("rw_out", [P, C * S], F32)
        ps_t = pb("rw_pt", [P, 2 * CHUNK], F32)
        ps_p = pb("rw_pp", [P, 4 * CHUNK], F32)
        ps_o = pb("rw_po", [P, 2 * CHUNK], F32)
        w_in = sem("rw_in")
        zeroed = sem("rw_zero")
        decay_ready = sem("rw_decay")
        own = sem("rw_own")
        xn_ready = sem("rw_xn_ready")
        turned = sem("rw_turned")
        xt_ready = sem("rw_xt_ready")
        mix_ready = sem("rw_mix_ready")
        projected = sem("rw_proj")
        kvr_ready = sem("rw_kvr_ready")
        arg_ready = sem("rw_arg")
        exp_ready = sem("rw_exp")
        relu_ready = sem("rw_relu")
        gated_ready = sem("rw_gated")
        out_ready = sem("rw_outp")
        added = sem("rw_added")
        block = ctx.enter_context(nc.Block())
        W = C * D

        def weight(i, c, lo, n):
            return w_sb[:, i * W + c * D + lo:i * W + c * D + lo + n]

        def col(i, c):
            return cols[:, i * C + c:i * C + c + 1]

        def xt_now(c):
            return xt[:, c * (S + 1) + 1:(c + 1) * (S + 1)]

        def xt_before(c):
            return xt[:, c * (S + 1):(c + 1) * (S + 1) - 1]

        def mixed(i, c, lo=0, n=S):
            return mix[:, (i * C + c) * S + lo:(i * C + c) * S + lo + n]

        def chan(i, d, lo=0, n=S):
            return kvr[:, (i * C + d) * S + lo:(i * C + d) * S + lo + n]

        def row(t, i, n=S):
            return t[:, i * S:i * S + n]

        def wkv_exps(act, b, d):
            at = b * (4 * C) + 4 * d
            act.wait_ge(arg_ready, at + 1)
            act.activation(row(ex, 0), row(expo, 0), ACT.Exp).then_inc(exp_ready, 1)
            act.wait_ge(arg_ready, at + 2)
            act.activation(row(ex, 1), row(expo, 1), ACT.Exp).then_inc(exp_ready, 1)
            act.wait_ge(arg_ready, at + 3)
            act.activation(row(tmp, 2), row(expo, 2), ACT.Relu).then_inc(relu_ready, 1)
            act.wait_ge(relu_ready, b * C + d + 1)
            act.activation(row(ex, 2), row(tmp, 2), ACT.Exp, scale=-1.0).then_inc(exp_ready, 1)
            act.wait_ge(arg_ready, at + 4)
            act.activation(row(ex, 3), row(expo, 3), ACT.Exp).then_inc(exp_ready, 1)

        @block.sync
        def _(sp):
            for i, w in enumerate((wk, wv, wr, wo)):
                sp.dma_start(w_sb[:, i * W:(i + 1) * W].rearrange("p (c n) -> p c n", c=C),
                             w.rearrange("(c p) n -> p c n", p=P)).then_inc(w_in, 16)
            for i, v in enumerate((mix_k, mix_v, mix_r, bonus, decay)):
                sp.dma_start(cols[:, i * C:(i + 1) * C], v.rearrange("p c -> p c")).then_inc(w_in, 16)

        @block.gpsimd
        def _(pool):
            for c in range(C):
                pool.memset(xt[:, c * (S + 1):c * (S + 1) + 1], 0.0).then_inc(zeroed, 1)
            pool.memset(run_max[:, 0:1], FAR).then_inc(zeroed, 1)
            pool.memset(aa[:, 0:1], 0.0).then_inc(zeroed, 1)
            pool.memset(bb[:, 0:1], 0.0).then_inc(zeroed, 1)

        @block.tensor
        def _(pe):
            pe.wait_ge(w_in, 16 * 9)
            with pe.Fori(0, B) as b:
                for q in range(C * NC):
                    c, half = q // NC, q % NC
                    if q == 0:
                        pe.wait_ge(xn_ready, b + 1)
                    if q >= 2:
                        pe.wait_ge(xt_ready, b * (C * NC) + q - 1)
                    for j in range(TB // NC):
                        n = half * (TB // NC) + j
                        last = pe.transpose(ps_t[:, (q % 2) * CHUNK + j * P:(q % 2) * CHUNK + (j + 1) * P],
                                            xn[:, n * D + c * P:n * D + (c + 1) * P], ident[:, :])
                    last.then_inc(turned, 1)
                k = 0
                for d in range(C):
                    for i in range(3):
                        if d == 0:
                            pe.wait_ge(mix_ready, b * 3 + i + 1)
                        for m in range(NC):
                            if k >= 4:
                                pe.wait_ge(kvr_ready, b * (3 * C * NC) + k - 3)
                            for c in range(C):
                                last = pe.matmul(ps_p[:, (k % 4) * CHUNK:(k % 4 + 1) * CHUNK], weight(i, c, d * P, P),
                                                 mixed(i, c, m * CHUNK, CHUNK), start=(c == 0), stop=(c == C - 1))
                            last.then_inc(projected, 1)
                            k += 1
                pe.wait_ge(gated_ready, (b + 1) * C)
                for g in range(TB // 2):
                    if g >= 2:
                        pe.wait_ge(added, b * (TB // 2) + g - 1)
                    for j in range(2):
                        n = 2 * g + j
                        for d in range(C):
                            last = pe.matmul(ps_o[:, (g % 2) * CHUNK + j * D:(g % 2) * CHUNK + (j + 1) * D],
                                             gated[:, d * S + n * P:d * S + (n + 1) * P], weight(3, d, 0, D),
                                             start=(d == 0), stop=(d == C - 1))
                    last.then_inc(out_ready, 1)

        @block.scalar
        def _(act):
            act.wait_ge(w_in, 16 * 9)
            act.activation(neg_w[:, :], cols[:, 4 * C:5 * C], ACT.Exp).then_inc(decay_ready, 1)
            with act.Fori(0, B) as b:
                for q in range(C * NC):
                    c, half = q // NC, q % NC
                    act.wait_ge(turned, b * (C * NC) + q + 1)
                    act.activation(xt[:, c * (S + 1) + 1 + half * CHUNK:c * (S + 1) + 1 + (half + 1) * CHUNK],
                                   ps_t[:, (q % 2) * CHUNK:(q % 2 + 1) * CHUNK], ACT.Copy).then_inc(xt_ready, 1)
                k = 0
                for d in range(C):
                    for i in range(3):
                        for m in range(NC):
                            act.wait_ge(projected, b * (3 * C * NC) + k + 1)
                            src = ps_p[:, (k % 4) * CHUNK:(k % 4 + 1) * CHUNK]
                            if i < 2:
                                act.activation(chan(i, d, m * CHUNK, CHUNK), src, ACT.Copy).then_inc(kvr_ready, 1)
                            else:
                                act.activation(chan(i, d, m * CHUNK, CHUNK), src, ACT.Exp, scale=-1.0).then_inc(kvr_ready, 1)
                            k += 1
                    if d == 0:
                        continue
                    wkv_exps(act, b, 0)
                    wkv_exps(act, b, 1)

        @block.vector
        def _(dve):
            dve.wait_ge(decay_ready, 1)
            dve.wait_ge(zeroed, C + 3)
            dve.tensor_scalar_mul(neg_w[:, :], neg_w[:, :], -1.0).then_inc(decay_ready, 1)
            dve.wait_ge(decay_ready, 2)
            STEPS = 1 + 12 * C
            with dve.Fori(0, B) as b:
                s = Steps(dve, own, b * STEPS)
                for n in range(TB):
                    t = b * TB + n
                    last = dve.tensor_scalar(xn[:, n * D:(n + 1) * D], h[:, ds(t * D, D)], mv[:, ds(t * 2, 1)],
                                             rstd[:, ds(t, 1)], ALU.subtract, ALU.mult)
                last.then_inc(xn_ready, 1)
                dve.wait_ge(xt_ready, (b + 1) * (C * NC))
                for c in range(C):
                    last = dve.tensor_tensor(dif[:, c * S:(c + 1) * S], xt_now(c), xt_before(c), ALU.subtract)
                s.step(last)
                for i in range(3):
                    for c in range(C):
                        last = dve.scalar_tensor_tensor(out=mixed(i, c), in0=dif[:, c * S:(c + 1) * S], scalar=col(i, c),
                                                        in1=xt_before(c), op0=ALU.mult, op1=ALU.add)
                    last.then_inc(mix_ready, 1)
                for d in range(C):
                    k, v, er = chan(0, d), chan(1, d), chan(2, d)
                    w1, u1 = neg_w[:, d:d + 1], col(3, d)
                    ex_at = b * (4 * C) + 4 * d
                    dve.wait_ge(kvr_ready, b * (3 * C * NC) + (d + 1) * 3 * NC)
                    s.step(dve.tensor_tensor_scan(run_max[:, 1:S + 1], w1.to_broadcast([P, S]), k, FAR, ALU.add, ALU.max))
                    dve.scalar_tensor_tensor(out=row(expo, 0), in0=run_max[:, 0:S], scalar=w1, in1=run_max[:, 1:S + 1],
                                             op0=ALU.add, op1=ALU.subtract).then_inc(arg_ready, 1)
                    dve.tensor_tensor(row(expo, 1), k, run_max[:, 1:S + 1], ALU.subtract).then_inc(arg_ready, 1)
                    s.mark(dve.scalar_tensor_tensor(out=row(expo, 2), in0=k, scalar=u1, in1=run_max[:, 0:S],
                                                    op0=ALU.add, op1=ALU.subtract))
                    s.wait()
                    dve.tensor_scalar_min(row(expo, 3), row(expo, 2), 0.0).then_inc(arg_ready, 2)
                    dve.wait_ge(exp_ready, ex_at + 2)
                    s.step(dve.tensor_tensor(row(tmp, 0), row(ex, 1), v, ALU.mult))
                    s.step(dve.tensor_tensor_scan(aa[:, 1:S + 1], row(ex, 0), row(tmp, 0), 0.0, ALU.mult, ALU.add))
                    s.step(dve.tensor_tensor_scan(bb[:, 1:S + 1], row(ex, 0), row(ex, 1), 0.0, ALU.mult, ALU.add))
                    dve.wait_ge(exp_ready, ex_at + 4)
                    s.mark(dve.tensor_tensor(row(tmp, 0), row(ex, 2), aa[:, 0:S], ALU.mult))
                    s.step(dve.tensor_tensor(row(tmp, 1), row(ex, 3), v, ALU.mult))
                    s.mark(dve.tensor_tensor(row(gated, d), row(tmp, 0), row(tmp, 1), ALU.add))
                    s.step(dve.tensor_tensor(row(ex, 2), row(ex, 2), bb[:, 0:S], ALU.mult))
                    s.step(dve.tensor_tensor(row(tmp, 1), row(ex, 2), row(ex, 3), ALU.add))
                    s.mark(dve.scalar_tensor_tensor(out=row(tmp, 0), in0=er, scalar=1.0, in1=row(tmp, 1),
                                                    op0=ALU.add, op1=ALU.mult))
                    s.wait()
                    s.step(dve.reciprocal(row(tmp, 1), row(tmp, 0)))
                    dve.tensor_tensor(row(gated, d), row(gated, d), row(tmp, 1), ALU.mult).then_inc(gated_ready, 1)
                for g in range(TB // 2):
                    dve.wait_ge(out_ready, b * (TB // 2) + g + 1)
                    hg = h[:, ds((b * TB + 2 * g) * D, 2 * D)]
                    dve.tensor_tensor(hg, hg, ps_o[:, (g % 2) * CHUNK:(g % 2 + 1) * CHUNK], ALU.add).then_inc(added, 1)
                assert s.n == STEPS


def first_of_max(dve, s, vals, top, eq, rev, cmax, onehot):
    s.step(dve.tensor_reduce(top, vals, AX_X, ALU.max))
    s.step(dve.tensor_tensor(eq, vals, top.unsqueeze(2).to_broadcast([P, NT, E]), ALU.is_equal))
    s.step(dve.tensor_tensor(eq, eq, rev.unsqueeze(1).to_broadcast([P, NT, E]), ALU.mult))
    s.step(dve.tensor_reduce(cmax, eq, AX_X, ALU.max))
    s.step(dve.tensor_tensor(onehot, eq, cmax.unsqueeze(2).to_broadcast([P, NT, E]), ALU.is_equal))


def slots_of(dve, s, t, marks, ps_rank, n_slot_tiles):
    rank, total = t["rank"], t["total"]
    s.mark(dve.tensor_copy(rank, ps_rank[:, 0:NT * E]))
    s.step(dve.tensor_copy(total, ps_rank[:, NT * E:2 * NT * E]))
    by = lambda a: a.rearrange("p (n e) -> p n e", e=E)
    for e in range(E):
        s.mark(dve.tensor_tensor_scan(t["incl"][:, e::E], t["one"].to_broadcast([P, NT]), total[:, e::E],
                                      0.0, ALU.mult, ALU.add))
    s.wait()
    s.mark(dve.tensor_tensor(rank, rank, t["incl"], ALU.add))
    s.step(dve.tensor_scalar_add(t["cnt_i"], t["incl"][:, (NT - 1) * E:], float(P - 1)))
    s.step(dve.tensor_single_scalar(t["cnt_i"], t["cnt_i"], -P, ALU.bitwise_and))
    s.step(dve.tensor_copy(t["padded"], t["cnt_i"]))
    s.step(dve.tensor_tensor_scan(t["ends"], t["one"].to_broadcast([P, E]), t["padded"], 0.0, ALU.mult, ALU.add))
    s.step(dve.tensor_tensor(t["base"], t["ends"], t["padded"], ALU.subtract))
    s.step(dve.tensor_tensor(rank, rank, total, ALU.subtract))
    s.step(dve.tensor_tensor(by(rank), by(rank), t["base"].unsqueeze(1).to_broadcast([P, NT, E]), ALU.add))
    J = n_slot_tiles
    ge = t["ge"][0:1, 0:J * E].rearrange("p (j e) -> p j e", e=E)
    s.step(dve.tensor_tensor(ge, t["starts"][0:1, 0:J].unsqueeze(2).to_broadcast([1, J, E]),
                             t["ends"][0:1, :].unsqueeze(1).to_broadcast([1, J, E]), ALU.is_ge))
    s.step(dve.tensor_reduce(t["tile_e"][0:1, 0:J], ge, AX_X, ALU.add))
    s.step(dve.tensor_scalar_min(t["tile_ei"][0:1, 0:J], t["tile_e"][0:1, 0:J], float(E - 1)))


def routing_tables(sb, tag, st):
    t = {}
    for name, n, dt in (("rank", NT * E, F32), ("total", NT * E, F32), ("incl", NT * E, F32), ("padded", E, F32),
                        ("ends", E, F32), ("base", E, F32), ("cnt_i", E, I32), ("ge", 72 * E, F32), ("tile_e", 72, F32)):
        t[name] = sb(tag + "_" + name, [P, n], dt)[:, :]
    t["one"] = st["ones"][:, 0:1]
    t["starts"] = st["starts"][:, :]
    t["tile_ei"] = st["tile_ei"][:, :]
    return t


def logits_phase(nc, st, tag, w_router, bias):
    h, mv, rstd, ident, xn_all, logits = (st[k] for k in ("h", "mv", "rstd", "ident", "xn_all", "logits"))
    with ExitStack() as ctx:
        sb, pb, sem = allocators(nc, ctx)
        w_sb = sb(tag + "_w", [P, C * E], F32)
        b_sb = sb(tag + "_b", [P, E], F32)
        xn = sb(tag + "_xn", [P, TB * D], F32)
        xt = sb(tag + "_xt", [P, C * S], F32)
        ps_t = pb(tag + "_pt", [P, 4 * CHUNK], F32)
        ps_l = pb(tag + "_pl", [P, CHUNK], F32)
        w_in = sem(tag + "_in")
        xn_ready = sem(tag + "_xn_ready")
        xn_kept = sem(tag + "_xn_kept")
        turned = sem(tag + "_turned")
        xt_ready = sem(tag + "_xt_ready")
        logit_done = sem(tag + "_logit_done")
        logit_read = sem(tag + "_logit_read")
        block = ctx.enter_context(nc.Block())
        Q = C * NC
        n_in = 32 if bias is not None else 16

        @block.sync
        def _(sp):
            sp.dma_start(w_sb[:, :].rearrange("p (c n) -> p c n", c=C), w_router.rearrange("(c p) n -> p c n", p=P)).then_inc(w_in, 16)
            if bias is not None:
                sp.dma_start(b_sb[:, :], bias.partition_broadcast(P)).then_inc(w_in, 16)

        @block.vector
        def _(dve):
            dve.wait_ge(w_in, n_in)
            with dve.Fori(0, B) as b:
                for n in range(TB):
                    t = b * TB + n
                    last = dve.tensor_scalar(xn[:, n * D:(n + 1) * D], h[:, ds(t * D, D)], mv[:, ds(t * 2, 1)],
                                             rstd[:, ds(t, 1)], ALU.subtract, ALU.mult)
                last.then_inc(xn_ready, 1)
                dve.wait_ge(logit_done, b + 1)
                lb = logits[:, ds(b * TB * E, TB * E)]
                if bias is not None:
                    dve.tensor_tensor(lb.rearrange("p (n e) -> p n e", e=E), ps_l[:, 0:TB * E].rearrange("p (n e) -> p n e", e=E),
                                      b_sb[:, :].unsqueeze(1).to_broadcast([P, TB, E]), ALU.add).then_inc(logit_read, 1)
                else:
                    dve.tensor_copy(lb, ps_l[:, 0:TB * E]).then_inc(logit_read, 1)
                dve.wait_ge(xn_kept, b + 1)
            dve.wait_ge(logit_read, B)

        @block.scalar
        def _(act):
            with act.Fori(0, B) as b:
                act.wait_ge(xn_ready, b + 1)
                act.activation(xn_all[:, ds(b * TB * D, TB * D)], xn[:, :], ACT.Copy).then_inc(xn_kept, 1)
                for q in range(Q):
                    c, half = q // NC, q % NC
                    act.wait_ge(turned, b * Q + q + 1)
                    act.activation(xt[:, c * S + half * CHUNK:c * S + (half + 1) * CHUNK],
                                   ps_t[:, q * CHUNK:(q + 1) * CHUNK], ACT.Copy).then_inc(xt_ready, 1)
                act.wait_ge(logit_done, b + 1)
            act.wait_ge(xn_kept, B)

        @block.tensor
        def _(pe):
            pe.wait_ge(w_in, n_in)
            with pe.Fori(0, B) as b:
                pe.wait_ge(xn_ready, b + 1)
                for q in range(Q):
                    c, half = q // NC, q % NC
                    for j in range(TB // NC):
                        n = half * (TB // NC) + j
                        last = pe.transpose(ps_t[:, q * CHUNK + j * P:q * CHUNK + (j + 1) * P],
                                            xn[:, n * D + c * P:n * D + (c + 1) * P], ident[:, :])
                    last.then_inc(turned, 1)
                pe.wait_ge(xt_ready, (b + 1) * Q)
                for n in range(TB):
                    for c in range(C):
                        last = pe.matmul(ps_l[:, n * E:(n + 1) * E], xt[:, c * S + n * P:c * S + (n + 1) * P],
                                         w_sb[:, c * E:(c + 1) * E], start=(c == 0), stop=(c == C - 1))
                last.then_inc(logit_done, 1)
                pe.wait_ge(logit_read, b + 1)


def scatter_rows(pool, st, pos, sorted_x, done):
    for n in range(NT):
        pool.indirect_dma_start(out=sorted_x, out_offset=bass.IndirectOffsetOnAxis(ap=pos[:, n:n + 1], axis=0),
                                in_=st["xn_all"][:, n * D:(n + 1) * D], in_offset=None).then_inc(done, 16)


def dispatch_top2(nc, st, sorted_x):
    logits, gates, pos1, pos2, xn_all = (st[k] for k in ("logits", "gates", "pos1", "pos2", "xn_all"))
    with ExitStack() as ctx:
        sb, pb, sem = allocators(nc, ctx)
        t = routing_tables(sb, "d0", st)
        rev = st["rev"][:, :]
        vals2 = sb("d0_vals2", [P, NT * E], F32)[:, :]
        eq = sb("d0_eq", [P, NT * E], F32)[:, :]
        oh1 = sb("d0_oh1", [P, NT * E], F32)[:, :]
        oh2 = sb("d0_oh2", [P, NT * E], F32)[:, :]
        marks = sb("d0_marks", [P, NT * E], F32)[:, :]
        top1 = sb("d0_top1", [P, NT], F32)[:, :]
        top2 = sb("d0_top2", [P, NT], F32)[:, :]
        cmax = sb("d0_cmax", [P, NT], F32)[:, :]
        dif = sb("d0_dif", [P, NT], F32)[:, :]
        ps_rank = pb("d0_ps", [P, 2 * NT * E], F32)
        own = sem("d0_own")
        dif_ready = sem("d0_dif_ready")
        exp_ready = sem("d0_exp_ready")
        marks_ready = sem("d0_marks_ready")
        ranked = sem("d0_ranked")
        pos_ready = sem("d0_pos_ready")
        scattered = sem("d0_scattered")
        block = ctx.enter_context(nc.Block())
        by = lambda a: a.rearrange("p (n e) -> p n e", e=E)

        @block.vector
        def _(dve):
            s = Steps(dve, own)
            first_of_max(dve, s, by(logits[:, :]), top1, by(eq), rev, cmax, by(oh1))
            s.step(dve.scalar_tensor_tensor(out=vals2, in0=oh1, scalar=-3e38, in1=logits[:, :], op0=ALU.mult, op1=ALU.add))
            first_of_max(dve, s, by(vals2), top2, by(eq), rev, cmax, by(oh2))
            dve.tensor_tensor(marks, oh1, oh2, ALU.add).then_inc(marks_ready, 1)
            dve.tensor_tensor(dif, top2, top1, ALU.subtract).then_inc(dif_ready, 1)
            dve.wait_ge(exp_ready, 1)
            s.step(dve.tensor_scalar_add(top2, dif, 1.0))
            s.step(dve.reciprocal(gates[:, 0:NT], top2))
            s.step(dve.tensor_tensor(gates[:, NT:2 * NT], gates[:, 0:NT], dif, ALU.mult))
            dve.wait_ge(ranked, 1)
            slots_of(dve, s, t, marks, ps_rank, 72)
            for oh, pos in ((oh1, pos1), (oh2, pos2)):
                s.step(dve.tensor_tensor(oh, oh, t["rank"], ALU.mult))
                s.step(dve.tensor_reduce(cmax, by(oh), AX_X, ALU.add))
                dve.tensor_copy(pos[:, :], cmax).then_inc(pos_ready, 1)
                dve.wait_ge(pos_ready, 1 if pos is pos1 else 2)

        @block.scalar
        def _(act):
            act.wait_ge(dif_ready, 1)
            act.activation(dif, dif, ACT.Exp).then_inc(exp_ready, 1)

        @block.tensor
        def _(pe):
            pe.wait_ge(marks_ready, 1)
            pe.matmul(ps_rank[:, 0:NT * E], st["before"][:, :], marks, start=True, stop=True)
            pe.matmul(ps_rank[:, NT * E:2 * NT * E], st["ones"][:, :], marks, start=True, stop=True).then_inc(ranked, 1)

        @block.gpsimd
        def _(pool):
            pool.wait_ge(pos_ready, 1)
            scatter_rows(pool, st, pos1, sorted_x, scattered)
            pool.wait_ge(pos_ready, 2)
            scatter_rows(pool, st, pos2, sorted_x, scattered)
            pool.wait_ge(scattered, 2 * NT * 16)


def experts(nc, st, tag, n_tiles, sorted_x, sorted_y, b1, b2, func, weights_in):
    ident, w1_sb, w2_sb, tile_ei = st["ident"], st["w1_sb"], st["w2_sb"], st["tile_ei"]
    X4 = 4
    with ExitStack() as ctx:
        sb, pb, sem = allocators(nc, ctx)
        xin = sb(tag + "_xin", [P, X4 * D], F32)
        xt = sb(tag + "_xt", [P, 2 * D], F32)
        hid = sb(tag + "_hid", [P, 2 * HID], F32)
        hidt = sb(tag + "_hidt", [P, 2 * HID], F32)
        yout = sb(tag + "_yout", [P, X4 * D], F32)
        b1_all = sb(tag + "_b1", [P, E * HID], F32) if b1 is not None else None
        b2_all = sb(tag + "_b2", [P, E * D], F32) if b2 is not None else None
        ps_x = pb(tag + "_px", [P, 2 * CHUNK], F32)
        ps_h = pb(tag + "_ph", [P, 2 * HID], F32)
        ps_t = pb(tag + "_pt", [P, 2 * HID], F32)
        ps_y = pb(tag + "_py", [P, 2 * CHUNK], F32)
        bias_in = sem(tag + "_bias_in")
        x_in = [sem(f"{tag}_x_in{k}") for k in range(X4)]
        y_out = [sem(f"{tag}_y_out{k}") for k in range(X4)]
        x_turned = sem(tag + "_x_turned")
        xt_ready = sem(tag + "_xt_ready")
        first_done = sem(tag + "_first_done")
        hid_ready = sem(tag + "_hid_ready")
        hid_turned = sem(tag + "_hid_turned")
        hidt_ready = sem(tag + "_hidt_ready")
        second_done = sem(tag + "_second_done")
        y_ready = sem(tag + "_y_ready")
        block = ctx.enter_context(nc.Block())
        LOOPS = n_tiles // 8 - 1
        assert n_tiles == 8 * LOOPS + 8

        def over_tiles(eng, step):
            for c in range(5):
                step(0, c)
            with eng.Fori(0, LOOPS) as i:
                for c in range(5, 13):
                    step(i, c)
            for c in range(5, 8):
                step(LOOPS, c)

        def need(eng, s, i, c):
            if isinstance(i, int) and 8 * i + c <= 0:
                return
            eng.wait_ge(s, i * 8 + c)

        def slot(t, c, n, w):
            return t[:, (c % n) * w:(c % n + 1) * w]

        def pick(eng, i, c):
            return eng.value_load(tile_ei[0:1, ds(i * 8 + c, 1)], min_val=0, max_val=E - 1)

        @block.sync
        def _(sp):
            if b1 is not None:
                sp.dma_start(b1_all[:, :], b1.rearrange("e n -> (e n)").partition_broadcast(P)).then_inc(bias_in, 16)
                sp.dma_start(b2_all[:, :], b2.rearrange("e n -> (e n)").partition_broadcast(P)).then_inc(bias_in, 16)
            for c in range(X4):
                sp.dma_start(slot(xin, c, X4, D), sorted_x[c * P:(c + 1) * P, :]).then_inc(x_in[c], 16)
            with sp.Fori(0, n_tiles // X4 - 1) as i:
                for c in range(X4):
                    sp.wait_ge(x_turned, i * X4 + c + 1)
                    sp.dma_start(slot(xin, c, X4, D), sorted_x[ds((i * X4 + X4 + c) * P, P), :]).then_inc(x_in[c], 16)

        @block.gpsimd
        def _(pool):
            with pool.Fori(0, n_tiles // X4) as i:
                for c in range(X4):
                    pool.wait_ge(y_ready, i * X4 + c + 1)
                    pool.dma_start(sorted_y[ds((i * X4 + c) * P, P), :], slot(yout, c, X4, D)).then_inc(y_out[c], 16)
            for c in range(X4):
                pool.wait_ge(y_out[c], 16 * (n_tiles // X4))

        @block.tensor
        def _(pe):
            pe.wait_ge(weights_in, 2 * E * 16)

            def turn_x(i, c):
                pe.wait_ge(x_in[c % X4], i * 32 + (c // X4 + 1) * 16)
                need(pe, xt_ready, i, c - 1)
                for k in range(C):
                    last = pe.transpose(ps_x[:, (c % 2) * CHUNK + k * P:(c % 2) * CHUNK + (k + 1) * P],
                                        xin[:, (c % X4) * D + k * P:(c % X4) * D + (k + 1) * P], ident[:, :])
                last.then_inc(x_turned, 1)

            def turn_hidden(i, c):
                need(pe, hid_ready, i, c + 1)
                need(pe, hidt_ready, i, c - 1)
                for k in range(HC):
                    last = pe.transpose(ps_t[:, (c % 2) * HID + k * P:(c % 2) * HID + (k + 1) * P],
                                        hid[:, (c % 2) * HID + k * P:(c % 2) * HID + (k + 1) * P], ident[:, :])
                last.then_inc(hid_turned, 1)

            def first(i, c):
                e = pick(pe, i, c)
                need(pe, xt_ready, i, c + 1)
                need(pe, hid_ready, i, c - 1)
                for k in range(C):
                    last = pe.matmul(slot(ps_h, c, 2, HID), xt[:, (c % 2) * D + k * P:(c % 2) * D + (k + 1) * P],
                                     w1_sb[:, ds(e * (C * HID) + k * HID, HID)], start=(k == 0), stop=(k == C - 1))
                last.then_inc(first_done, 1)

            def second(i, c):
                e = pick(pe, i, c)
                need(pe, hidt_ready, i, c + 1)
                need(pe, y_ready, i, c - 1)
                for k in range(HC):
                    last = pe.matmul(ps_y[:, (c % 2) * CHUNK:(c % 2) * CHUNK + D],
                                     hidt[:, (c % 2) * HID + k * P:(c % 2) * HID + (k + 1) * P],
                                     w2_sb[:, ds(e * (HC * D) + k * D, D)], start=(k == 0), stop=(k == HC - 1))
                last.then_inc(second_done, 1)

            turn_x(0, 0)

            def tile(i, c):
                head = isinstance(i, int) and 8 * i + c == 0
                tail = isinstance(i, int) and 8 * i + c == n_tiles - 1
                if not head:
                    turn_hidden(i, c - 1)
                if not tail:
                    turn_x(i, c + 1)
                first(i, c)
                if not head:
                    second(i, c - 1)

            over_tiles(pe, tile)
            turn_hidden(LOOPS, 7)
            second(LOOPS, 7)

        @block.vector
        def _(dve):
            if b1 is not None:
                dve.wait_ge(bias_in, 32)

            def take_x(i, c):
                need(dve, x_turned, i, c + 1)
                need(dve, first_done, i, c - 1)
                dve.tensor_copy(slot(xt, c, 2, D), ps_x[:, (c % 2) * CHUNK:(c % 2) * CHUNK + D]).then_inc(xt_ready, 1)

            def take_hidden(i, c):
                if b1 is not None:
                    e = pick(dve, i, c)
                need(dve, first_done, i, c + 1)
                need(dve, hid_turned, i, c - 1)
                if b1 is not None:
                    dve.tensor_tensor(slot(hid, c, 2, HID), slot(ps_h, c, 2, HID), b1_all[:, ds(e * HID, HID)],
                                      ALU.add).then_inc(hid_ready, 1)
                else:
                    dve.tensor_copy(slot(hid, c, 2, HID), slot(ps_h, c, 2, HID)).then_inc(hid_ready, 1)

            def take_y(i, c):
                if b2 is not None:
                    e = pick(dve, i, c)
                need(dve, second_done, i, c + 1)
                if not (isinstance(i, int) and 8 * i + c < X4):
                    dve.wait_ge(y_out[c % X4], i * 32 + (c // X4) * 16)
                y = ps_y[:, (c % 2) * CHUNK:(c % 2) * CHUNK + D]
                if b2 is not None:
                    dve.tensor_tensor(slot(yout, c, X4, D), y, b2_all[:, ds(e * D, D)], ALU.add).then_inc(y_ready, 1)
                else:
                    dve.tensor_copy(slot(yout, c, X4, D), y).then_inc(y_ready, 1)

            take_x(0, 0)

            def tile(i, c):
                if not (isinstance(i, int) and 8 * i + c == n_tiles - 1):
                    take_x(i, c + 1)
                take_hidden(i, c)
                if not (isinstance(i, int) and 8 * i + c == 0):
                    take_y(i, c - 1)

            over_tiles(dve, tile)
            take_y(LOOPS, 7)

        @block.scalar
        def _(act):
            def tile(i, c):
                need(act, hid_turned, i, c + 1)
                need(act, second_done, i, c - 1)
                act.activation(slot(hidt, c, 2, HID), slot(ps_t, c, 2, HID), func).then_inc(hidt_ready, 1)

            over_tiles(act, tile)


def combine_top2(nc, st, sorted_y):
    h, gates, pos1, pos2 = (st[k] for k in ("h", "gates", "pos1", "pos2"))
    with ExitStack() as ctx:
        sb, pb, sem = allocators(nc, ctx)
        rows = sb("c0_rows", [P, NT * D], F32)
        got = [sem(f"c0_got{k}") for k in range(2 * B)]
        added = sem("c0_added")
        block = ctx.enter_context(nc.Block())

        @block.gpsimd
        def _(pool):
            for w, pos in enumerate((pos1, pos2)):
                for n in range(NT):
                    if w and n % TB == 0:
                        pool.wait_ge(added, n // TB + 1)
                    pool.indirect_dma_start(out=rows[:, n * D:(n + 1) * D], out_offset=None, in_=sorted_y,
                                            in_offset=bass.IndirectOffsetOnAxis(ap=pos[:, n:n + 1], axis=0),
                                            ).then_inc(got[w * B + n // TB], 16)

        @block.vector
        def _(dve):
            for w in range(2):
                for b in range(B):
                    dve.wait_ge(got[w * B + b], 16 * TB)
                    if w:
                        dve.wait_ge(added, b + 1)
                    for n in range(b * TB, (b + 1) * TB):
                        hn = h[:, n * D:(n + 1) * D]
                        last = dve.scalar_tensor_tensor(out=hn, in0=rows[:, n * D:(n + 1) * D], scalar=gates[:, w * NT + n:w * NT + n + 1],
                                                        in1=hn, op0=ALU.mult, op1=ALU.add)
                    last.then_inc(added, 1)
            dve.wait_ge(added, 2 * B)


HEADS, HD = 16, 16
GH = 4
GROUPS = B * HEADS // GH
GCH = GH * HD
KEYS = 256
NB = S // KEYS
PARTS = 3
QROWS = 6 * HD
MROWS = PARTS * NB
ROWS = QROWS + MROWS


def project_qkv(nc, st, wq, wk, wv, v_ones, qk_dram, v_dram):
    h, mv, rstd, ident = (st[x] for x in ("h", "mv", "rstd", "ident"))
    with ExitStack() as ctx:
        sb, pb, sem = allocators(nc, ctx)
        VW = GROUPS // B * P
        wqk_sb = sb("qk_w", [P, 2 * C * D], F32)
        wv_sb = sb("v_w", [P, C * VW], F32)
        one_sb = sb("v_one", [P, VW], F32)
        xn = sb("qk_xn", [P, TB * D], F32)
        xt = sb("qk_xt", [P, C * S], F32)
        parts = sb("qk_parts", [P, 2 * PARTS * S], BF16)
        rest = sb("qk_rest", [P, 2 * CHUNK], F32)
        v_sb = sb("v_sb", [P, 4 * VW], F32)
        ps_t = pb("qk_pt", [P, 2 * CHUNK], F32)
        ps_q = pb("qk_pq", [P, 2 * CHUNK], F32)
        ps_v = pb("qk_pv", [P, 2 * VW], F32)
        w_in = sem("qk_w_in")
        xn_ready = sem("qk_xn_ready")
        turned = sem("qk_turned")
        xt_ready = sem("qk_xt_ready")
        projected = sem("qk_projected")
        high_ready = sem("qk_high")
        rest_ready = sem("qk_rest_ready")
        mid_ready = sem("qk_mid")
        low_ready = sem("qk_low")
        parts_out = [sem(f"qk_parts_out{k}") for k in range(2)]
        v_done = sem("qk_v_done")
        v_ready = sem("qk_v_ready")
        v_out = [sem(f"qk_v_out{k}") for k in range(4)]
        block = ctx.enter_context(nc.Block())
        Q = C * NC
        U = 2 * C * NC
        SCALE = HD ** -0.5

        def part(k, p, lo, n):
            return parts[:, (k % 2 * PARTS + p) * S + lo:(k % 2 * PARTS + p) * S + lo + n]

        @block.sync
        def _(sp):
            for i, w in enumerate((wq, wk)):
                sp.dma_start(wqk_sb[:, i * C * D:(i + 1) * C * D].rearrange("p (c n) -> p c n", c=C),
                             w.rearrange("(c p) n -> p c n", p=P)).then_inc(w_in, 16)
            sp.dma_start(wv_sb[:, :].rearrange("p (c n) -> p c n", c=C), wv.rearrange("(c p) n -> p c n", p=P)).then_inc(w_in, 16)
            sp.dma_start(one_sb[:, :], v_ones.partition_broadcast(P)).then_inc(w_in, 16)
            with sp.Fori(0, B) as b:
                for k in range(2 * C):
                    i, d = k // C, k % C
                    sp.wait_ge(low_ready, b * U + (k + 1) * NC)
                    for half in range(2):
                        sp.dma_start(qk_dram[ds(b * (GROUPS // B) + d * 2 + half, 1), i].rearrange("o p c t -> c (o p) t"),
                                     parts[half * GCH:(half + 1) * GCH, (k % 2) * PARTS * S:(k % 2 + 1) * PARTS * S]
                                     .rearrange("c (p t) -> c p t", p=PARTS)).then_inc(parts_out[k % 2], 16)
            for k in range(2):
                sp.wait_ge(parts_out[k], B * C * 32)

        @block.gpsimd
        def _(pool):
            with pool.Fori(0, B) as b:
                for n in range(TB):
                    pool.wait_ge(v_ready, b * TB + n + 1)
                    pool.dma_start(v_dram[ds(b * (GROUPS // B), GROUPS // B), n * P:(n + 1) * P, :].rearrange("g t c -> t g c"),
                                   v_sb[:, (n % 4) * VW:(n % 4 + 1) * VW].rearrange("p (g c) -> p g c", g=GROUPS // B)
                                   ).then_inc(v_out[n % 4], 16)
            for k in range(4):
                pool.wait_ge(v_out[k], B * TB // 4 * 16)

        @block.tensor
        def _(pe):
            pe.wait_ge(w_in, 64)
            with pe.Fori(0, B) as b:
                pe.wait_ge(xn_ready, b + 1)
                for q in range(Q):
                    c, half = q // NC, q % NC
                    if q >= 2:
                        pe.wait_ge(xt_ready, b * Q + q - 1)
                    for j in range(TB // NC):
                        n = half * (TB // NC) + j
                        last = pe.transpose(ps_t[:, (q % 2) * CHUNK + j * P:(q % 2) * CHUNK + (j + 1) * P],
                                            xn[:, n * D + c * P:n * D + (c + 1) * P], ident[:, :])
                    last.then_inc(turned, 1)
                pe.wait_ge(xt_ready, (b + 1) * Q)
                for u in range(U):
                    i, d, m = u // (C * NC), u // NC % C, u % NC
                    if u >= 2:
                        pe.wait_ge(rest_ready, b * U + u - 1)
                    for c in range(C):
                        last = pe.matmul(ps_q[:, (u % 2) * CHUNK:(u % 2 + 1) * CHUNK],
                                         wqk_sb[:, (i * C + c) * D + d * P:(i * C + c) * D + (d + 1) * P],
                                         xt[:, c * S + m * CHUNK:c * S + (m + 1) * CHUNK], start=(c == 0), stop=(c == C - 1))
                    last.then_inc(projected, 1)
                    n = u
                    if n >= 2:
                        pe.wait_ge(v_ready, b * TB + n - 1)
                    for c in range(C):
                        last = pe.matmul(ps_v[:, (n % 2) * VW:(n % 2 + 1) * VW], xt[:, c * S + n * P:c * S + (n + 1) * P],
                                         wv_sb[:, c * VW:(c + 1) * VW], start=(c == 0), stop=(c == C - 1))
                    last.then_inc(v_done, 1)

        @block.scalar
        def _(act):
            def sequence(b):
                for q in range(Q):
                    c, half = q // NC, q % NC
                    act.wait_ge(turned, b * Q + q + 1)
                    act.activation(xt[:, c * S + half * CHUNK:c * S + (half + 1) * CHUNK],
                                   ps_t[:, (q % 2) * CHUNK:(q % 2 + 1) * CHUNK], ACT.Copy).then_inc(xt_ready, 1)
                for u in range(U):
                    k, m = u // NC, u % NC
                    if m == 0:
                        need(act, parts_out[k % 2], b * (C * 32) + k // 2 * 32)
                    act.wait_ge(projected, b * U + u + 1)
                    act.activation(part(k, 0, m * CHUNK, CHUNK), ps_q[:, (u % 2) * CHUNK:(u % 2 + 1) * CHUNK], ACT.Copy,
                                   scale=SCALE if k < C else 1.0).then_inc(high_ready, 1)
                    act.wait_ge(rest_ready, b * U + u + 1)
                    act.activation(part(k, 1, m * CHUNK, CHUNK), rest[:, (u % 2) * CHUNK:(u % 2 + 1) * CHUNK],
                                   ACT.Copy).then_inc(mid_ready, 1)
                act.wait_ge(v_done, (b + 1) * TB)

            over_sequences(act, sequence)

        @block.vector
        def _(dve):
            dve.wait_ge(w_in, 64)

            def sequence(b):
                for n in range(TB):
                    t = b * TB + n
                    last = dve.tensor_scalar(xn[:, n * D:(n + 1) * D], h[:, ds(t * D, D)], mv[:, ds(t * 2, 1)],
                                             rstd[:, ds(t, 1)], ALU.subtract, ALU.mult)
                last.then_inc(xn_ready, 1)
                for u in range(U):
                    k, m = u // NC, u % NC
                    r = rest[:, (u % 2) * CHUNK:(u % 2 + 1) * CHUNK]
                    dve.wait_ge(high_ready, b * U + u + 1)
                    if u > 0:
                        dve.wait_ge(low_ready, b * U + u)
                    dve.scalar_tensor_tensor(out=r, in0=ps_q[:, (u % 2) * CHUNK:(u % 2 + 1) * CHUNK],
                                             scalar=SCALE if k < C else 1.0, in1=part(k, 0, m * CHUNK, CHUNK),
                                             op0=ALU.mult, op1=ALU.subtract).then_inc(rest_ready, 1)
                    n = u
                    dve.wait_ge(v_done, b * TB + n + 1)
                    need(dve, v_out[n % 4], b * 32 + n // 4 * 16)
                    dve.tensor_tensor(v_sb[:, (n % 4) * VW:(n % 4 + 1) * VW], ps_v[:, (n % 2) * VW:(n % 2 + 1) * VW],
                                      one_sb[:, :], ALU.add).then_inc(v_ready, 1)
                    dve.wait_ge(rest_ready, b * U + u + 1)
                    dve.wait_ge(mid_ready, b * U + u + 1)
                    dve.tensor_tensor(part(k, 2, m * CHUNK, CHUNK), r, part(k, 1, m * CHUNK, CHUNK),
                                      ALU.subtract).then_inc(low_ready, 1)
                dve.wait_ge(low_ready, (b + 1) * U)

            over_sequences(dve, sequence)


def attention(nc, st, qk_dram, v_dram, block_rows, ident_bits):
    ctx_all = st["ctx_all"]
    with ExitStack() as ctx:
        sb, pb, sem = allocators(nc, ctx)
        NU = 3
        qs = [sb(f"at_q{u}", [ROWS, GH * S], BF16) for u in range(NU)]
        ks = [sb(f"at_k{u}", [ROWS, GH * S], BF16) for u in range(NU)]
        vs = [sb(f"at_v{u}", [P, TB * P], F32) for u in range(NU)]
        identb = sb("at_identb", [P, P], BF16)
        ex = sb("at_ex", [P, 2 * GH * CHUNK], F32)
        raw = sb("at_raw", [P, CHUNK], F32)
        den = sb("at_den", [P, GH * GH], F32)
        mx = sb("at_mx", [P, GH * TB * NB], F32)
        neg = sb("at_neg", [P, TB * NB], F32)
        zero = sb("at_zero", [P, TB * NB], F32)
        rem = sb("at_rem", [P, TB * NB], F32)
        mp = sb("at_mp", [P, GH * TB * MROWS], BF16)
        ps_k = pb("at_pk", [P, 4 * CHUNK], F32)
        ps_s = pb("at_ps", [P, 2 * CHUNK], F32)
        ps_v = pb("at_pv", [P, CHUNK], F32)
        ps_m = pb("at_pm", [P, CHUNK], F32)
        ps_mb = ps_m[:, :].bitcast(BF16)
        set_up = sem("at_set_up")
        zero_set = sem("at_zero_set")
        in_k = [sem(f"at_in{u}") for u in range(NU)]
        scored = sem("at_scored")
        maxed = sem("at_maxed")
        own = sem("at_own")
        split = sem("at_split")
        rows_turned = sem("at_rows_turned")
        rows_copied = sem("at_rows_copied")
        keyed = sem("at_keyed")
        exp_done = sem("at_exp_done")
        pv_done = sem("at_pv_done")
        pv_copied = sem("at_pv_copied")
        ctx_turned = sem("at_ctx_turned")
        den_ready = sem("at_den_ready")
        ctx_read = sem("at_ctx_read")
        block = ctx.enter_context(nc.Block())
        N_IN = (2 * 6 + 1) * 16
        STEPS = 2 * TB
        UNITS = GH * TB * 2
        FROM = [5 * s for s in range(5)] + [4 * s + 4 for s in range(5, STEPS)] + [UNITS]
        TURN_ROWS = {5: 0, 8: 1, 12: 2, STEPS - 1: GH - 1}
        LOOPS = (GROUPS - 4) // NU

        def over_groups(eng, group):
            group(0, 0)
            with eng.Fori(0, LOOPS) as i:
                for v in (1, 2, 3):
                    group(i, v)
            for v in (1, 2, 3):
                group(LOOPS, v)

        def need(eng, s, i, v, per, c):
            if isinstance(i, int) and per * (NU * i + v) + c <= 0:
                return
            eng.wait_ge(s, i * (per * NU) + (per * v + c))

        def is_first(i, v):
            return isinstance(i, int) and NU * i + v == 0

        def is_last(i, v):
            return isinstance(i, int) and NU * i + v == GROUPS - 1

        @block.sync
        def _(sp):
            for u in range(NU):
                sp.dma_start(ks[u][QROWS:ROWS, :].bitcast(U16), block_rows).then_inc(set_up, 16)
            sp.dma_start(identb[:, :].bitcast(U16), ident_bits).then_inc(set_up, 16)

            def load(i, v):
                if not (isinstance(i, int) and NU * i + v < NU):
                    need(sp, pv_done, i, v, STEPS, -2 * STEPS)
                u, g = v % NU, (i * NU + v)
                for t, i_qk, order in ((qs, 0, (0, 1, 2, 0, 1, 0)), (ks, 1, (0, 0, 0, 1, 1, 2))):
                    for r, p in enumerate(order):
                        src = qk_dram[ds(g, 1), i_qk, p] if not isinstance(g, int) else qk_dram[g:g + 1, i_qk, p]
                        sp.dma_start(t[u][r * HD:(r + 1) * HD, :].rearrange("c (j t) -> c j t", j=GH),
                                     src.rearrange("o (j c) t -> c (o j) t", c=HD)).then_inc(in_k[u], 16)
                src = v_dram[ds(g, 1)] if not isinstance(g, int) else v_dram[g:g + 1]
                sp.dma_start(vs[u][:, :].rearrange("p (n c) -> p n c", c=P),
                             src.rearrange("o (n p) c -> p (o n) c", p=P)).then_inc(in_k[u], 16)

            for v in range(NU):
                load(0, v)
            with sp.Fori(0, LOOPS) as i:
                for v in range(NU, 2 * NU):
                    load(i, v)
            load(LOOPS, NU)

        @block.gpsimd
        def _(pool):
            pool.memset(zero[:, :], 0.0).then_inc(zero_set, 1)
            pool.wait_ge(zero_set, 1)

            def splits(i, v):
                for j in range(GH):
                    base = i * (4 * GH * NU) + 4 * (GH * v + j)
                    m = mx[:, j * TB * NB:(j + 1) * TB * NB]
                    by = mp[:, j * TB * MROWS:(j + 1) * TB * MROWS].rearrange("p (n k) -> p n k", k=PARTS)
                    as3 = lambda a: a.unsqueeze(2)
                    need(pool, maxed, i, v, UNITS, (j + 1) * 2 * TB)
                    need(pool, rows_turned, i, v, GH, j + 1 - GH)
                    need(pool, split, i, v, GH, j)
                    pool.tensor_tensor(neg[:, :], zero[:, :], m, ALU.subtract).then_inc(own, 1)
                    pool.wait_ge(own, base + 1)
                    pool.tensor_tensor(by[:, :, 0:1], as3(neg[:, :]), as3(zero[:, :]), ALU.add).then_inc(own, 1)
                    pool.wait_ge(own, base + 2)
                    pool.tensor_tensor(as3(rem[:, :]), as3(neg[:, :]), by[:, :, 0:1], ALU.subtract).then_inc(own, 1)
                    pool.wait_ge(own, base + 3)
                    pool.tensor_tensor(by[:, :, 1:2], as3(rem[:, :]), as3(zero[:, :]), ALU.add).then_inc(own, 1)
                    pool.wait_ge(own, base + 4)
                    pool.tensor_tensor(by[:, :, 2:3], as3(rem[:, :]), by[:, :, 1:2], ALU.subtract).then_inc(split, 1)

            over_groups(pool, splits)

        @block.tensor
        def _(pe):
            pe.wait_ge(set_up, (NU + 1) * 16)

            def score(i, v, n):
                j, t, half, u = n // (2 * TB), n % (2 * TB) // 2, n % 2, v % NU
                if n == 0:
                    pe.wait_ge(in_k[u], i * N_IN + (v // NU + 1) * N_IN)
                need(pe, maxed, i, v, UNITS, n - 1)
                pe.matmul(ps_s[:, (n % 2) * CHUNK:(n % 2 + 1) * CHUNK], qs[u][0:QROWS, j * S + t * P:j * S + (t + 1) * P],
                          ks[u][0:QROWS, j * S + half * CHUNK:j * S + (half + 1) * CHUNK],
                          start=True, stop=True).then_inc(scored, 1)

            def turn_rows(i, v, j):
                need(pe, split, i, v, GH, j + 1)
                need(pe, rows_copied, i, v, GH, j)
                for t in range(TB):
                    last = pe.transpose(ps_mb[QROWS:ROWS, t * P:(t + 1) * P],
                                        mp[:, (j * TB + t) * MROWS:(j * TB + t + 1) * MROWS], identb[:, :])
                last.then_inc(rows_turned, 1)

            def key_scores(i, v, s, pair):
                half, kt, u = s // TB, s % TB, v % NU
                need(pe, exp_done, i, v, 2 * STEPS, 2 * s + pair - 1)
                for j in (2 * pair, 2 * pair + 1):
                    last = pe.matmul(ps_k[:, j * CHUNK:(j + 1) * CHUNK], ks[u][:, j * S + kt * P:j * S + (kt + 1) * P],
                                     qs[u][:, j * S + half * CHUNK:j * S + (half + 1) * CHUNK], start=True, stop=True)
                last.then_inc(keyed, 1)

            def values(i, v, s):
                half, kt, u = s // TB, s % TB, v % NU
                need(pe, exp_done, i, v, 2 * STEPS, 2 * s + 2)
                if kt == 0:
                    need(pe, pv_copied, i, v, 2, half)
                for j in range(GH):
                    last = pe.matmul(ps_v[32 * j:32 * j + 32, :], vs[u][:, kt * P + 32 * j:kt * P + 32 * j + 32],
                                     ex[:, (s % 2) * GH * CHUNK + j * CHUNK:(s % 2) * GH * CHUNK + (j + 1) * CHUNK],
                                     start=(kt == 0), stop=(kt == TB - 1), skip_group_check=True)
                last.then_inc(pv_done, 1)

            def turn_ctx(i, v, half):
                need(pe, pv_copied, i, v, 2, half + 1)
                need(pe, ctx_read, i, v, 2, half)
                for t in range(CHUNK // P):
                    last = pe.transpose(ps_m[:, t * P:(t + 1) * P], raw[:, t * P:(t + 1) * P], st["ident"][:, :])
                last.then_inc(ctx_turned, 1)

            for n in range(UNITS):
                score(0, 0, n)
                if n % (2 * TB) == 8 and n >= 2 * TB:
                    turn_rows(0, 0, n // (2 * TB) - 1)
            turn_rows(0, 0, GH - 1)

            def group(i, v):
                for s in range(STEPS):
                    more = [] if is_last(i, v) else list(range(FROM[s], FROM[s + 1]))
                    if s == 0:
                        need(pe, rows_copied, i, v, GH, 2)
                    for n in more[:1]:
                        score(i, v + 1, n)
                    key_scores(i, v, s, 0)
                    for n in more[1:-2]:
                        score(i, v + 1, n)
                    if s == 0:
                        need(pe, rows_copied, i, v, GH, GH)
                    key_scores(i, v, s, 1)
                    for n in more[-2:] if len(more) > 2 else more[1:]:
                        score(i, v + 1, n)
                    if s > 0:
                        values(i, v, s - 1)
                    elif not is_first(i, v):
                        values(i, v - 1, STEPS - 1)
                    if s == 2 and not is_first(i, v):
                        turn_ctx(i, v - 1, 1)
                    if s in TURN_ROWS and not is_last(i, v):
                        if s == 5:
                            need(pe, ctx_read, i, v, 2, 0)
                        if s == 12:
                            need(pe, ctx_read, i, v, 2, 1)
                        turn_rows(i, v + 1, TURN_ROWS[s])
                    if s == 10:
                        if not is_last(i, v):
                            need(pe, rows_copied, i, v, GH, GH + 2)
                        turn_ctx(i, v, 0)

            over_groups(pe, group)
            values(LOOPS, NU, STEPS - 1)
            pe.wait_ge(ctx_read, 2 * GROUPS - 1)
            turn_ctx(LOOPS, NU, 1)

        @block.scalar
        def _(act):
            def copy_rows(i, v, j):
                u = v % NU
                need(act, rows_turned, i, v, GH, j + 1)
                act.activation(qs[u][QROWS:ROWS, j * S:(j + 1) * S], ps_mb[QROWS:ROWS, :], ACT.Copy).then_inc(rows_copied, 1)

            def exps(i, v, s, pair):
                need(act, keyed, i, v, 2 * STEPS, 2 * s + pair + 1)
                need(act, pv_done, i, v, STEPS, s - 1)
                at = (s % 2) * GH * CHUNK + pair * 2 * CHUNK
                act.activation(ex[:, at:at + 2 * CHUNK], ps_k[:, pair * 2 * CHUNK:(pair + 1) * 2 * CHUNK],
                               ACT.Exp).then_inc(exp_done, 1)

            def copy_ctx(i, v, half):
                need(act, pv_done, i, v, STEPS, (half + 1) * TB)
                need(act, ctx_turned, i, v, 2, half)
                act.activation(raw[:, :], ps_v[:, :], ACT.Copy).then_inc(pv_copied, 1)

            for j in range(GH):
                copy_rows(0, 0, j)

            def group(i, v):
                for s in range(STEPS):
                    exps(i, v, s, 0)
                    exps(i, v, s, 1)
                    if s == 0 and not is_first(i, v):
                        copy_ctx(i, v - 1, 1)
                    if s == TB:
                        copy_ctx(i, v, 0)
                    if s in TURN_ROWS and not is_last(i, v):
                        copy_rows(i, v + 1, TURN_ROWS[s])

            over_groups(act, group)
            copy_ctx(LOOPS, NU, 1)

        @block.vector
        def _(dve):
            def largest(i, v, n):
                j, t, half = n // (2 * TB), n % (2 * TB) // 2, n % 2
                if n % (2 * TB) == 0:
                    need(dve, split, i, v, GH, j + 1 - GH)
                need(dve, scored, i, v, UNITS, n + 1)
                at = (j * TB + t) * NB + half * 2
                dve.tensor_reduce(mx[:, at:at + 2], ps_s[:, (n % 2) * CHUNK:(n % 2 + 1) * CHUNK]
                                  .rearrange("p (k c) -> p k c", c=KEYS), AX_X, ALU.max).then_inc(maxed, 1)

            def divide(i, v, half):
                need(dve, ctx_turned, i, v, 2, half + 1)
                need(dve, ctx_read, i, v, 2, half)
                strips = ps_m[:, :].rearrange("p (t j c) -> p (t j) c", j=GH, c=32)
                dve.reciprocal(den[:, :].unsqueeze(2), strips[:, :, HD:HD + 1]).then_inc(den_ready, 1)
                need(dve, den_ready, i, v, 2, half + 1)
                at = i * (NU * TB * GCH) + (v * TB + half * TB // 2) * GCH
                dve.tensor_tensor(ctx_all[:, ds(at, CHUNK // P * GCH)].rearrange("p (t c) -> p t c", c=HD),
                                  strips[:, :, 0:HD], den[:, :].unsqueeze(2).to_broadcast([P, GH * GH, HD]),
                                  ALU.mult).then_inc(ctx_read, 1)

            for n in range(UNITS):
                largest(0, 0, n)

            def group(i, v):
                for s in range(STEPS):
                    if not is_last(i, v):
                        for n in range(FROM[s], FROM[s + 1]):
                            largest(i, v + 1, n)
                    if s == 2 and not is_first(i, v):
                        divide(i, v - 1, 1)
                    if s == 10:
                        divide(i, v, 0)

            over_groups(dve, group)
            divide(LOOPS, NU, 1)
            dve.wait_ge(ctx_read, 2 * GROUPS)


def attention_out(nc, st, wo):
    h, ident, ctx_all = (st[x] for x in ("h", "ident", "ctx_all"))
    with ExitStack() as ctx:
        sb, pb, sem = allocators(nc, ctx)
        w_sb = sb("ao_w", [P, C * D], F32)
        stage = sb("ao_stage", [P, TB * D], F32)
        ct = sb("ao_ct", [P, C * S], F32)
        ps_t = pb("ao_pt", [P, 4 * CHUNK], F32)
        ps_o = pb("ao_po", [P, 2 * CHUNK], F32)
        w_in = sem("ao_w_in")
        staged = sem("ao_staged")
        turned = sem("ao_turned")
        ct_ready = sem("ao_ct_ready")
        out_ready = sem("ao_out_ready")
        added = sem("ao_added")
        block = ctx.enter_context(nc.Block())
        Q = C * NC
        G = GROUPS // B

        @block.sync
        def _(sp):
            sp.dma_start(w_sb[:, :].rearrange("p (c n) -> p c n", c=C), wo.rearrange("(c p) n -> p c n", p=P)).then_inc(w_in, 16)

        @block.tensor
        def _(pe):
            pe.wait_ge(w_in, 16)
            with pe.Fori(0, B) as b:
                pe.wait_ge(staged, b + 1)
                for q in range(Q):
                    c, half = q // NC, q % NC
                    for j in range(TB // NC):
                        n = half * (TB // NC) + j
                        last = pe.transpose(ps_t[:, q * CHUNK + j * P:q * CHUNK + (j + 1) * P],
                                            stage[:, n * D + c * P:n * D + (c + 1) * P], ident[:, :])
                    last.then_inc(turned, 1)
                pe.wait_ge(ct_ready, (b + 1) * Q)
                for g in range(TB // 2):
                    if g >= 2:
                        pe.wait_ge(added, b * (TB // 2) + g - 1)
                    for j in range(2):
                        n = 2 * g + j
                        for c in range(C):
                            last = pe.matmul(ps_o[:, (g % 2) * CHUNK + j * D:(g % 2) * CHUNK + (j + 1) * D],
                                             ct[:, c * S + n * P:c * S + (n + 1) * P], w_sb[:, c * D:(c + 1) * D],
                                             start=(c == 0), stop=(c == C - 1))
                    last.then_inc(out_ready, 1)

        @block.scalar
        def _(act):
            with act.Fori(0, B) as b:
                for q in range(Q):
                    c, half = q // NC, q % NC
                    act.wait_ge(turned, b * Q + q + 1)
                    act.activation(ct[:, c * S + half * CHUNK:c * S + (half + 1) * CHUNK],
                                   ps_t[:, q * CHUNK:(q + 1) * CHUNK], ACT.Copy).then_inc(ct_ready, 1)
                act.wait_ge(out_ready, (b + 1) * (TB // 2))

        @block.vector
        def _(dve):
            with dve.Fori(0, B) as b:
                for g in range(G):
                    last = dve.tensor_copy(stage[:, :].rearrange("p (n g c) -> p n g c", g=G, c=GCH)[:, :, g, :],
                                           ctx_all[:, ds((b * G + g) * TB * GCH, TB * GCH)].rearrange("p (n c) -> p n c", c=GCH))
                last.then_inc(staged, 1)
                for g in range(TB // 2):
                    dve.wait_ge(out_ready, b * (TB // 2) + g + 1)
                    hg = h[:, ds((b * TB + 2 * g) * D, 2 * D)]
                    dve.tensor_tensor(hg, hg, ps_o[:, (g % 2) * CHUNK:(g % 2 + 1) * CHUNK], ALU.add).then_inc(added, 1)
            dve.wait_ge(added, B * TB // 2)


CAP = T // E
BITS = 30


def dispatch_capacity(nc, st, sorted_x):
    logits, gates, pos1 = (st[k] for k in ("logits", "gates", "pos1"))
    with ExitStack() as ctx:
        sb, pb, sem = allocators(nc, ctx)
        t = routing_tables(sb, "d1", st)
        W = NT * E
        new = lambda name, n, dt=F32: sb("d1_" + name, [P, n], dt)[:, :]
        probs, cmp, sel, eq, onehot, vals = (new(x, W) for x in ("probs", "cmp", "sel", "eq", "onehot", "vals"))
        top, total, cmax = (new(x, NT) for x in ("top", "sum", "cmax"))
        counts, need, keep_f = (new(x, E) for x in ("counts", "need", "keepf"))
        level, trial, keep = (new(x, E, I32) for x in ("level", "trial", "keep"))
        bits_i = new("bits_i", BITS, I32)
        ps_rank = pb("d1_ps", [P, 2 * W], F32)
        ps_cnt = pb("d1_pc", [P, CHUNK], F32)
        own = sem("d1_own")
        shifted = sem("d1_shifted")
        exp_ready = sem("d1_exp_ready")
        counted = sem("d1_counted")
        summed = sem("d1_summed")
        eq_ready = sem("d1_eq_ready")
        ranked = sem("d1_ranked")
        pos_ready = sem("d1_pos_ready")
        scattered = sem("d1_scattered")
        block = ctx.enter_context(nc.Block())
        by = lambda a: a.rearrange("p (n e) -> p n e", e=E)
        over_tiles = lambda a: a.rearrange("p (n e) -> p e n", e=E)
        per_e = lambda a: a.unsqueeze(1).to_broadcast([P, NT, E])
        per_n = lambda a: a.unsqueeze(2).to_broadcast([P, NT, E])
        UNROLL = 5
        BIT_STEPS = 5

        @block.tensor
        def _(pe):
            with pe.Fori(0, BITS // UNROLL) as i:
                for k in range(UNROLL):
                    pe.wait_ge(counted, i * UNROLL + k + 1)
                    pe.matmul(ps_cnt[:, 0:E], st["ones"][:, :], counts, start=True, stop=True).then_inc(summed, 1)
            pe.wait_ge(counted, BITS + 1)
            pe.matmul(ps_cnt[:, 0:E], st["ones"][:, :], counts, start=True, stop=True).then_inc(summed, 1)
            for k in range(2):
                pe.wait_ge(eq_ready, k + 1)
                src = eq if k == 0 else onehot
                pe.matmul(ps_rank[:, 0:W], st["before"][:, :], src, start=True, stop=True)
                pe.matmul(ps_rank[:, W:2 * W], st["ones"][:, :], src, start=True, stop=True).then_inc(ranked, 1)

        @block.scalar
        def _(act):
            act.wait_ge(shifted, 1)
            act.activation(vals, vals, ACT.Exp).then_inc(exp_ready, 1)

        @block.vector
        def _(dve):
            s = Steps(dve, own)
            s.step(dve.tensor_reduce(top, by(logits[:, :]), AX_X, ALU.max))
            dve.tensor_tensor(by(vals), by(logits[:, :]), per_n(top), ALU.subtract).then_inc(shifted, 1)
            s.step(dve.memset(level, 0))
            s.step(dve.tensor_copy(bits_i, st["bits"][:, :]))
            dve.wait_ge(exp_ready, 1)
            s.step(dve.tensor_reduce(total, by(vals), AX_X, ALU.add))
            s.step(dve.reciprocal(cmax, total))
            s.step(dve.tensor_tensor(by(probs), by(vals), per_n(cmax), ALU.mult))
            before = s.n
            with dve.Fori(0, BITS // UNROLL) as i:
                s = Steps(dve, own, i * (UNROLL * BIT_STEPS) + before)
                for k in range(UNROLL):
                    b = i * UNROLL + k
                    s.step(dve.tensor_tensor(trial, level, bits_i[:, ds(b, 1)].to_broadcast([P, E]), ALU.bitwise_or))
                    s.step(dve.tensor_tensor(by(cmp), by(probs), per_e(trial.bitcast(F32)), ALU.is_ge))
                    dve.tensor_reduce(counts, over_tiles(cmp), AX_X, ALU.add).then_inc(counted, 1)
                    dve.wait_ge(summed, b + 1)
                    s.step(dve.tensor_scalar(keep_f, ps_cnt[:, 0:E], CAP - 0.5, None, ALU.is_ge))
                    s.step(dve.tensor_tensor(keep, keep_f, st["bits"][:, ds(b, 1)].to_broadcast([P, E]), ALU.mult))
                    s.step(dve.tensor_tensor(level, level, keep, ALU.bitwise_or))
                assert s.n == UNROLL * BIT_STEPS
            s = Steps(dve, own, before + BITS * BIT_STEPS)
            level_f = level.bitcast(F32)
            s.step(dve.tensor_tensor(by(sel), by(probs), per_e(level_f), ALU.is_gt))
            dve.tensor_reduce(counts, over_tiles(sel), AX_X, ALU.add).then_inc(counted, 1)
            dve.tensor_tensor(by(eq), by(probs), per_e(level_f), ALU.is_equal).then_inc(eq_ready, 1)
            dve.wait_ge(summed, BITS + 1)
            s.step(dve.tensor_scalar(need, ps_cnt[:, 0:E], -1.0, float(CAP), ALU.mult, ALU.add))
            dve.wait_ge(ranked, 1)
            s.mark(dve.tensor_copy(t["rank"], ps_rank[:, 0:W]))
            s.step(dve.tensor_copy(t["total"], ps_rank[:, W:2 * W]))
            for e in range(E):
                s.mark(dve.tensor_tensor_scan(t["incl"][:, e::E], t["one"].to_broadcast([P, NT]), t["total"][:, e::E],
                                              0.0, ALU.mult, ALU.add))
            s.wait()
            s.step(dve.tensor_tensor(t["rank"], t["rank"], t["incl"], ALU.add))
            s.step(dve.tensor_tensor(t["rank"], t["rank"], t["total"], ALU.subtract))
            s.step(dve.tensor_tensor(by(cmp), by(t["rank"]), per_e(need), ALU.is_lt))
            dve.wait_ge(eq_ready, 1)
            s.step(dve.tensor_tensor(cmp, cmp, eq, ALU.mult))
            s.step(dve.tensor_tensor(sel, sel, cmp, ALU.add))
            s.step(dve.tensor_reduce(top, by(sel), AX_X, ALU.max))
            s.step(dve.tensor_scalar(top, top, -1.0, 1.0, ALU.mult, ALU.add))
            s.step(dve.tensor_tensor(by(sel), by(sel), per_n(top), ALU.max))
            s.step(dve.tensor_tensor(cmp, probs, sel, ALU.mult))
            s.step(dve.scalar_tensor_tensor(out=vals, in0=sel, scalar=-1.0, in1=cmp, op0=ALU.add, op1=ALU.add))
            first_of_max(dve, s, by(vals), top, by(cmp), st["rev"][:, :], cmax, by(onehot))
            dve.nop().then_inc(eq_ready, 1)
            s.step(dve.tensor_tensor(cmp, probs, onehot, ALU.mult))
            s.step(dve.tensor_reduce(gates[:, 0:NT], by(cmp), AX_X, ALU.add))
            dve.wait_ge(ranked, 2)
            slots_of(dve, s, t, onehot, ps_rank, T // P + E)
            s.step(dve.tensor_tensor(onehot, onehot, t["rank"], ALU.mult))
            s.step(dve.tensor_reduce(cmax, by(onehot), AX_X, ALU.add))
            dve.tensor_copy(pos1[:, :], cmax).then_inc(pos_ready, 1)
            dve.wait_ge(pos_ready, 1)

        @block.gpsimd
        def _(pool):
            pool.wait_ge(pos_ready, 1)
            scatter_rows(pool, st, pos1, sorted_x, scattered)
            pool.wait_ge(scattered, NT * 16)


def combine_top1(nc, st, sorted_y, out):
    h, gates, pos1 = (st[k] for k in ("h", "gates", "pos1"))
    with ExitStack() as ctx:
        sb, pb, sem = allocators(nc, ctx)
        rows = sb("c1_rows", [P, NT * D], F32)
        got = [sem(f"c1_got{k}") for k in range(B)]
        added = sem("c1_added")
        stored = sem("c1_stored")
        block = ctx.enter_context(nc.Block())

        @block.gpsimd
        def _(pool):
            for n in range(NT):
                pool.indirect_dma_start(out=rows[:, n * D:(n + 1) * D], out_offset=None, in_=sorted_y,
                                        in_offset=bass.IndirectOffsetOnAxis(ap=pos1[:, n:n + 1], axis=0),
                                        ).then_inc(got[n // TB], 16)

        @block.vector
        def _(dve):
            for b in range(B):
                dve.wait_ge(got[b], 16 * TB)
                for n in range(b * TB, (b + 1) * TB):
                    hn = h[:, n * D:(n + 1) * D]
                    last = dve.scalar_tensor_tensor(out=hn, in0=rows[:, n * D:(n + 1) * D], scalar=gates[:, n:n + 1],
                                                    in1=hn, op0=ALU.mult, op1=ALU.add)
                last.then_inc(added, 1)

        @block.sync
        def _(sp):
            for b in range(B):
                sp.wait_ge(added, b + 1)
                sp.dma_start(out[b].rearrange("(n p) d -> p n d", p=P),
                             h[:, b * TB * D:(b + 1) * TB * D].rearrange("p (n d) -> p n d", d=D)).then_inc(stored, 16)
            sp.wait_ge(stored, 16 * B)


def load_experts(nc, st, w1, w2, arrived):
    with nc.Block() as block:

        @block.sync
        def _(sp):
            for e in range(E):
                sp.dma_start(st["w1_sb"][:, e * C * HID:(e + 1) * C * HID].rearrange("p (c n) -> p c n", c=C),
                             w1[e].rearrange("(c p) n -> p c n", p=P)).then_inc(arrived, 16)
                sp.dma_start(st["w2_sb"][:, e * HC * D:(e + 1) * HC * D].rearrange("p (c n) -> p c n", c=HC),
                             w2[e].rearrange("(c p) n -> p c n", p=P)).then_inc(arrived, 16)


CONSTS = (("before", P), ("ones", P), ("rev", E), ("starts", 2 * NT + E), ("bits", BITS))


def set_up(nc, st, a, slots0, slots1):
    with ExitStack() as ctx:
        sb, pb, sem = allocators(nc, ctx)
        PIECES = 8
        width = slots0.shape[0] * D // (P * PIECES)
        zeros = sb("su_zeros", [P, width], F32)
        zeroed = sem("su_zeroed")
        filled = sem("su_filled")
        const_in = sem("su_const_in")
        block = ctx.enter_context(nc.Block())

        @block.gpsimd
        def _(pool):
            pool.memset(zeros[:, :], 0.0).then_inc(zeroed, 1)

        @block.sync
        def _(sp):
            for name, _ in CONSTS:
                sp.dma_start(st[name][:, :], a["c_" + name]).then_inc(const_in, 16)
            sp.wait_ge(zeroed, 1)
            for slots in (slots0, slots1):
                rows = slots.shape[0] // PIECES
                with sp.Fori(0, PIECES) as i:
                    sp.dma_start(slots[ds(i * rows, rows), :].rearrange("(p n) d -> p (n d)", p=P),
                                 zeros[:, 0:rows * D // P]).then_inc(filled, 16)
            sp.wait_ge(const_in, 16 * len(CONSTS))
            sp.wait_ge(filled, 2 * 16 * PIECES)


def tower(nc, a, out):
    SLOTS0 = 2 * T + E * P
    SLOTS1 = T + E * P
    sorted_x0, sorted_y0 = (nc.dram_tensor(n, [SLOTS0, D], F32).ap() for n in ("sorted_x0", "sorted_y0"))
    sorted_x1, sorted_y1 = (nc.dram_tensor(n, [SLOTS1, D], F32).ap() for n in ("sorted_x1", "sorted_y1"))
    qk_dram = nc.dram_tensor("qk_groups", [GROUPS, 2, PARTS, GCH, S], BF16).ap()
    v_dram = nc.dram_tensor("v_groups", [GROUPS, S, P], F32).ap()
    with ExitStack() as ctx:
        sb, pb, sem = allocators(nc, ctx)
        st = {"h": sb("h", [P, NT * D], F32), "ident": sb("ident", [P, P], F32), "mv": sb("mv", [P, 2 * NT], F32),
              "rstd": sb("rstd", [P, NT], F32), "logits": sb("logits", [P, NT * E], F32),
              "gates": sb("gates", [P, 2 * NT], F32), "pos1": sb("pos1", [P, NT], I32), "pos2": sb("pos2", [P, NT], I32),
              "tile_ei": sb("tile_ei", [P, 2 * NT + E], I32)}
        for name, n in CONSTS:
            st[name] = sb(name, [P, n], F32)
        experts0_in = sem("experts0_in")
        experts1_in = sem("experts1_in")

        set_up(nc, st, a, sorted_x0, sorted_x1)
        embed(nc, st, a["tok"], a["L0_tok_emb"], a["c_pos"], a["L0_tok_alpha"], a["L0_tok_beta"])
        layer_norm(nc, st, "n0")
        rwkv(nc, st, *(a["L0_attn_" + n] for n in ("W", "U", "time_mix_k", "time_mix_v", "time_mix_r", "Wk", "Wv", "Wr", "Wo")))
        with ExitStack() as moe:
            for n in ("w1_sb", "w2_sb"):
                st[n] = moe.enter_context(nc.sbuf_tensor("l0_" + n, [P, E * C * HID], F32))
            load_experts(nc, st, a["L0_ffn_W1"], a["L0_ffn_W2"], experts0_in)
            with nc.sbuf_tensor("xn_all0", [P, NT * D], F32) as st["xn_all"]:
                layer_norm(nc, st, "n1")
                logits_phase(nc, st, "g0", a["L0_ffn_Wr"], a["L0_ffn_br"])
                dispatch_top2(nc, st, sorted_x0)
            experts(nc, st, "x0", 2 * NT + E, sorted_x0, sorted_y0, a["L0_ffn_b1"], a["L0_ffn_b2"], ACT.Relu, experts0_in)
        combine_top2(nc, st, sorted_y0)
        layer_norm(nc, st, "n2")
        with nc.sbuf_tensor("ctx_all", [P, NT * D], F32) as st["ctx_all"]:
            project_qkv(nc, st, a["L1_attn_w_q"], a["L1_attn_w_k"], a["L1_attn_w_v"], a["c_v_ones"], qk_dram, v_dram)
            attention(nc, st, qk_dram, v_dram, a["c_block_rows"], a["c_ident_bits"])
            attention_out(nc, st, a["L1_attn_w_o"])
        with ExitStack() as moe:
            for n in ("w1_sb", "w2_sb"):
                st[n] = moe.enter_context(nc.sbuf_tensor("l1_" + n, [P, E * C * HID], F32))
            load_experts(nc, st, a["L1_ffn_W1"], a["L1_ffn_W2"], experts1_in)
            with nc.sbuf_tensor("xn_all1", [P, NT * D], F32) as st["xn_all"]:
                layer_norm(nc, st, "n3")
                logits_phase(nc, st, "g1", a["L1_ffn_Wg"], None)
                dispatch_capacity(nc, st, sorted_x1)
            experts(nc, st, "x1", NT + E, sorted_x1, sorted_y1, None, None, ACT.Gelu, experts1_in)
        combine_top1(nc, st, sorted_y1, out)


def shape_constants():
    position = np.arange(S, dtype=np.float32)[:, None]
    step = np.arange(0, D, 2, dtype=np.float32) * np.float32(-np.log(10000.0) / D)
    angle = (position * np.exp(step.astype(np.float64)).astype(np.float32)).astype(np.float64)
    BF16_ONE = 0x3F80
    rows = np.zeros((MROWS, GH, S), np.uint16)
    for k in range(NB):
        rows[k * PARTS:(k + 1) * PARTS, :, k * KEYS:(k + 1) * KEYS] = BF16_ONE
    ones = np.zeros((HEADS, 32), np.float32)
    ones[:, HD] = 1.0
    spread = lambda v: np.ascontiguousarray(np.broadcast_to(v.astype(np.float32), (P, v.size)))
    return {
        "c_pos": np.stack([np.sin(angle), np.cos(angle)], axis=-1).reshape(S, D).astype(np.float32),
        "c_before": np.triu(np.ones((P, P), np.float32), 1),
        "c_ones": np.ones((P, P), np.float32),
        "c_rev": spread(E - np.arange(E)),
        "c_starts": spread(P * np.arange(2 * NT + E)),
        "c_bits": spread(2.0 ** np.arange(BITS - 1, -1, -1)),
        "c_block_rows": rows.reshape(MROWS, GH * S),
        "c_ident_bits": np.eye(P, dtype=np.uint16) * np.uint16(BF16_ONE),
        "c_v_ones": ones.reshape(-1),
    }


def laid_out(inputs):
    a = {n: np.ascontiguousarray(v) for n, v in inputs.items() if n != "x"}
    a["tok"] = np.ascontiguousarray(inputs["x"].reshape(NT, P).T)
    for n in ("Wk", "Wv", "Wr", "Wo"):
        a["L0_attn_" + n] = np.ascontiguousarray(a["L0_attn_" + n].T)
    for n in ("W", "U", "time_mix_k", "time_mix_v", "time_mix_r"):
        a["L0_attn_" + n] = np.ascontiguousarray(a["L0_attn_" + n].reshape(C, P).T)
    wv = np.zeros((D, HEADS, 32), a["L1_attn_w_v"].dtype)
    wv[:, :, :HD] = a["L1_attn_w_v"].reshape(D, HEADS, HD)
    a["L1_attn_w_v"] = wv.reshape(D, HEADS * 32)
    return a


def kernel(**inputs):
    import concourse.bacc as bacc
    from concourse.bass_utils import run_bass_kernel_spmd

    nc = bacc.Bacc("TRN2", target_bir_lowering=False, num_devices=1)
    arrays = {**laid_out({n: np.asarray(v) for n, v in inputs.items()}), **shape_constants()}
    a = {n: nc.dram_tensor("in_" + n, list(v.shape), mybir.dt.from_np(v.dtype), kind="ExternalInput").ap()
         for n, v in arrays.items()}
    out = nc.dram_tensor("out_h", [B, S, D], F32, kind="ExternalOutput").ap()
    tower(nc, a, out)
    r = run_bass_kernel_spmd(nc, [{"in_" + n: v for n, v in arrays.items()}], core_ids=[0])
    return r.results[0]["out_h"]
```

```python
from contextlib import ExitStack

import concourse.bass as bass
import numpy as np
from concourse import mybir

F32 = mybir.dt.float32
BF16 = mybir.dt.bfloat16
I32 = mybir.dt.int32
U16 = mybir.dt.uint16
ALU = mybir.AluOpType
ACT = mybir.ActivationFunctionType
AX_X = mybir.AxisListType.X

P = 128
B, S, D = 4, 1024, 256
T = B * S
NT = T // P
TB = S // P
C = D // P
CHUNK = 512
NC = S // CHUNK
E = 8
HID = 512
HC = HID // P
FAR = -1e38
LN_EPS = 1e-5
ds = bass.ds


def allocators(nc, ctx):
    sems = []

    def sem(name):
        sems.append(nc.alloc_semaphore(name))
        return sems[-1]

    def clear():
        nc.clear_and_free_semaphores(sems)
        nc.all_engine_barrier()

    ctx.callback(clear)
    return (lambda name, shape, dt: ctx.enter_context(nc.sbuf_tensor(name, shape, dt)),
            lambda name, shape, dt: ctx.enter_context(nc.psum_tensor(name, shape, dt)), sem)


def need(eng, s, count):
    if isinstance(count, int) and count <= 0:
        return
    eng.wait_ge(s, count)


def over_sequences(eng, sequence):
    sequence(0)
    with eng.Fori(1, B) as b:
        sequence(b)


class Steps:

    def __init__(self, eng, sem, base=0):
        self.eng, self.sem, self.base, self.n = eng, sem, base, 0

    def mark(self, ins):
        ins.then_inc(self.sem, 1)
        self.n += 1
        return self.n

    def wait(self, n=None):
        self.eng.wait_ge(self.sem, self.base + (self.n if n is None else n))

    def step(self, ins):
        self.mark(ins)
        self.wait()


def embed(nc, st, tok_ids, emb, pos, alpha, beta):
    h, ident = st["h"], st["ident"]
    with ExitStack() as ctx:
        sb, pb, sem = allocators(nc, ctx)
        tok_idx = sb("tok_idx", [P, NT], I32)
        pos_sb = sb("pos_sb", [P, TB * D], F32)
        alpha_all = sb("alpha_all", [P, D], F32)
        beta_all = sb("beta_all", [P, D], F32)
        stats = sb("em_stats", [P, NT * 6], F32)
        mv = sb("em_mv", [P, NT * 2], F32)
        dev = sb("em_dev", [P, NT], F32)
        rec = sb("em_rec", [P, NT], F32)
        idx_in = sem("em_idx_in")
        const_in = sem("em_const_in")
        rows0 = sem("em_rows0")
        rows1 = sem("em_rows1")
        rows2 = sem("em_rows2")
        rows3 = sem("em_rows3")
        own = sem("em_own")
        ident0 = sem("em_ident0")
        mv_ready = sem("em_mv_ready")
        dev_ready = sem("em_dev_ready")
        block = ctx.enter_context(nc.Block())
        rows_in = [rows0, rows1, rows2, rows3]

        @block.sync
        def _(sp):
            sp.dma_start(tok_idx[:, :], tok_ids).then_inc(idx_in, 16)
            sp.dma_start(pos_sb[:, :].rearrange("p (n d) -> p n d", d=D), pos.rearrange("(n p) d -> p n d", p=P)).then_inc(const_in, 16)
            sp.dma_start(alpha_all[:, :], alpha.partition_broadcast(P)).then_inc(const_in, 16)
            sp.dma_start(beta_all[:, :], beta.partition_broadcast(P)).then_inc(const_in, 16)

        @block.gpsimd
        def _(pool):
            pool.memset(ident[:, :], 0.0).then_inc(ident0, 1)
            pool.wait_ge(ident0, 1)
            pool.affine_select(out=ident[:, :], in_=ident[:, :], compare_op=ALU.not_equal, fill=1.0, base=0,
                               pattern=[[-1, P]], channel_multiplier=1).then_inc(ident0, 1)
            pool.wait_ge(idx_in, 16)
            for n in range(NT):
                pool.indirect_dma_start(out=h[:, n * D:(n + 1) * D], out_offset=None, in_=emb,
                                        in_offset=bass.IndirectOffsetOnAxis(ap=tok_idx[:, n:n + 1], axis=0),
                                        ).then_inc(rows_in[n // TB], 16)

        @block.scalar
        def _(act):
            act.wait_ge(mv_ready, 1)
            act.activation(dev[:, :], mv[:, 1::2], ACT.Sqrt, scale=D / (D - 1.0)).then_inc(dev_ready, 1)

        @block.vector
        def _(dve):
            s = Steps(dve, own)
            dve.wait_ge(const_in, 48)
            for b in range(B):
                dve.wait_ge(rows_in[b], 16 * TB)
                hb = h[:, b * TB * D:(b + 1) * TB * D]
                s.step(dve.tensor_tensor(hb, hb, pos_sb[:, :], ALU.add))
                for n in range(b * TB, (b + 1) * TB):
                    dve.bn_stats(stats[:, n * 6:(n + 1) * 6], h[:, n * D:(n + 1) * D])
            dve.drain()
            for n in range(NT):
                dve.bn_aggr(mv[:, n * 2:(n + 1) * 2], stats[:, n * 6:(n + 1) * 6])
            dve.drain()
            dve.nop().then_inc(mv_ready, 1)
            dve.wait_ge(dev_ready, 1)
            s.step(dve.tensor_scalar_add(dev[:, :], dev[:, :], 1e-6))
            s.step(dve.reciprocal(rec[:, :], dev[:, :]))
            with dve.Fori(0, B) as b:
                for k in range(TB):
                    n = b * TB + k
                    hn = h[:, ds(n * D, D)]
                    dve.tensor_scalar(hn, hn, mv[:, ds(n * 2, 1)], rec[:, ds(n, 1)], ALU.subtract, ALU.mult)
            dve.drain()
            every = h[:, :].rearrange("p (n d) -> p n d", d=D)
            s.step(dve.tensor_tensor(every, every, beta_all[:, :].unsqueeze(1).to_broadcast([P, NT, D]), ALU.add))
            s.step(dve.tensor_tensor(every, every, alpha_all[:, :].unsqueeze(1).to_broadcast([P, NT, D]), ALU.mult))


def layer_norm(nc, st, tag, after_stats=None):
    h, mv, rstd = st["h"], st["mv"], st["rstd"]
    with ExitStack() as ctx:
        sb, pb, sem = allocators(nc, ctx)
        stats = sb(tag + "_stats", [P, NT * 6], F32)
        var = sb(tag + "_var", [P, NT], F32)
        dev = sb(tag + "_dev", [P, NT], F32)
        var_ready = sem(tag + "_var_ready")
        dev_ready = sem(tag + "_dev_ready")
        own = sem(tag + "_own")
        block = ctx.enter_context(nc.Block())

        @block.scalar
        def _(act):
            act.wait_ge(var_ready, 1)
            act.activation(dev[:, :], var[:, :], ACT.Sqrt).then_inc(dev_ready, 1)

        @block.vector
        def _(dve):
            with dve.Fori(0, B) as b:
                for n in range(TB):
                    dve.bn_stats(stats[:, ds((b * TB + n) * 6, 6)], h[:, ds((b * TB + n) * D, D)])
            dve.drain()
            for n in range(NT):
                dve.bn_aggr(mv[:, n * 2:(n + 1) * 2], stats[:, n * 6:(n + 1) * 6])
            dve.drain()
            dve.tensor_scalar_add(var[:, :], mv[:, 1::2], LN_EPS).then_inc(var_ready, 1)
            dve.wait_ge(dev_ready, 1)
            dve.reciprocal(rstd[:, :], dev[:, :]).then_inc(own, 1)
            dve.wait_ge(own, 1)


def rwkv(nc, st, decay, bonus, mix_k, mix_v, mix_r, wk, wv, wr, wo):
    h, mv, rstd, ident = st["h"], st["mv"], st["rstd"], st["ident"]
    with ExitStack() as ctx:
        sb, pb, sem = allocators(nc, ctx)
        w_sb = sb("rw_w", [P, 4 * C * D], F32)
        cols = sb("rw_cols", [P, 5 * C], F32)
        neg_w = sb("rw_nw", [P, C], F32)
        xn = sb("rw_xn", [P, TB * D], F32)
        xt = sb("rw_xt", [P, C * (S + 1)], F32)
        dif = sb("rw_dif", [P, C * S], F32)
        mix = sb("rw_mix", [P, 3 * C * S], F32)
        kvr = sb("rw_kvr", [P, 3 * C * S], F32)
        run_max = sb("rw_max", [P, S + 1], F32)
        aa = sb("rw_aa", [P, S + 1], F32)
        bb = sb("rw_bb", [P, S + 1], F32)
        expo = sb("rw_f", [P, 4 * S], F32)
        ex = sb("rw_e", [P, 4 * S], F32)
        tmp = sb("rw_t", [P, 3 * S], F32)
        numer = sb("rw_numer", [P, 2 * S], F32)
        gated = sb("rw_out", [P, C * S], F32)
        ps_t = pb("rw_pt", [P, 2 * CHUNK], F32)
        ps_p = pb("rw_pp", [P, 2 * CHUNK], F32)
        ps_o = pb("rw_po", [P, 4 * CHUNK], F32)
        w_in = sem("rw_in")
        zeroed = sem("rw_zero")
        decay_ready = sem("rw_decay")
        own = sem("rw_own")
        xn_ready = sem("rw_xn_ready")
        turned = sem("rw_turned")
        xt_ready = sem("rw_xt_ready")
        dif_ready = sem("rw_dif_ready")
        mix_ready = sem("rw_mix_ready")
        projected = sem("rw_proj")
        kvr_ready = sem("rw_kvr_ready")
        arg_ready = sem("rw_arg")
        exp_ready = sem("rw_exp")
        relu_ready = sem("rw_relu")
        aa_ready = sem("rw_aa_ready")
        products = sem("rw_products")
        numer_ready = sem("rw_numer_ready")
        gated_ready = sem("rw_gated")
        out_ready = sem("rw_outp")
        added = sem("rw_added")
        block = ctx.enter_context(nc.Block())
        W = C * D
        Q = C * NC
        U = 3 * NC
        G = TB // 2

        def over_turns(eng, turn):
            turn(0, False)
            with eng.Fori(1, B - 1) as b:
                turn(b, False)
            turn(B - 1, True)

        def weight(i, c, lo, n):
            return w_sb[:, i * W + c * D + lo:i * W + c * D + lo + n]

        def col(i, c):
            return cols[:, i * C + c:i * C + c + 1]

        def xt_now(c):
            return xt[:, c * (S + 1) + 1:(c + 1) * (S + 1)]

        def xt_before(c):
            return xt[:, c * (S + 1):(c + 1) * (S + 1) - 1]

        def mixed(i, c, lo=0, n=S):
            return mix[:, (i * C + c) * S + lo:(i * C + c) * S + lo + n]

        def chan(i, d, lo=0, n=S):
            return kvr[:, (i * C + d) * S + lo:(i * C + d) * S + lo + n]

        def row(t, i, n=S):
            return t[:, i * S:i * S + n]

        def wkv_exps(act, b, d):
            at = b * (4 * C) + 4 * d
            act.wait_ge(arg_ready, at + 1)
            act.activation(row(ex, 0), row(expo, 0), ACT.Exp).then_inc(exp_ready, 1)
            act.wait_ge(arg_ready, at + 2)
            act.activation(row(ex, 1), row(expo, 1), ACT.Exp).then_inc(exp_ready, 1)
            act.wait_ge(arg_ready, at + 3)
            act.activation(row(tmp, 2), row(expo, 2), ACT.Relu).then_inc(relu_ready, 1)
            act.wait_ge(relu_ready, b * C + d + 1)
            act.activation(row(ex, 2), row(tmp, 2), ACT.Exp, scale=-1.0).then_inc(exp_ready, 1)
            act.wait_ge(arg_ready, at + 4)
            act.activation(row(ex, 3), row(expo, 3), ACT.Exp).then_inc(exp_ready, 1)

        @block.sync
        def _(sp):
            for i, w in enumerate((wk, wv, wr, wo)):
                sp.dma_start(w_sb[:, i * W:(i + 1) * W].rearrange("p (c n) -> p c n", c=C),
                             w.rearrange("(c p) n -> p c n", p=P)).then_inc(w_in, 16)
            for i, v in enumerate((mix_k, mix_v, mix_r, bonus, decay)):
                sp.dma_start(cols[:, i * C:(i + 1) * C], v.rearrange("p c -> p c")).then_inc(w_in, 16)

        @block.gpsimd
        def _(pool):
            for c in range(C):
                pool.memset(xt[:, c * (S + 1):c * (S + 1) + 1], 0.0).then_inc(zeroed, 1)
            pool.memset(run_max[:, 0:1], FAR).then_inc(zeroed, 1)
            pool.memset(aa[:, 0:1], 0.0).then_inc(zeroed, 1)
            pool.memset(bb[:, 0:1], 0.0).then_inc(zeroed, 1)
            pool.wait_ge(zeroed, C + 3)

            def difference(b):
                need(pool, mix_ready, b * 3)
                pool.wait_ge(xt_ready, (b + 1) * Q)
                pool.tensor_tensor(dif[:, 0:S], xt_now(0), xt_before(0), ALU.subtract).then_inc(dif_ready, 1)

            def numerator(b, d):
                pool.wait_ge(exp_ready, b * (4 * C) + 4 * d + 4)
                pool.tensor_tensor(row(numer, 0), row(ex, 3), chan(1, d), ALU.mult).then_inc(products, 1)
                pool.wait_ge(aa_ready, b * C + d + 1)
                pool.tensor_tensor(row(numer, 1), row(ex, 2), aa[:, 0:S], ALU.mult).then_inc(products, 1)
                need(pool, out_ready, b * G)
                pool.wait_ge(products, b * (2 * C) + 2 * d + 2)
                pool.tensor_tensor(row(gated, d), row(numer, 0), row(numer, 1), ALU.add).then_inc(numer_ready, 1)

            difference(0)

            def turn(b, last):
                numerator(b, 0)
                if not last:
                    difference(b + 1)
                numerator(b, 1)

            over_turns(pool, turn)

        @block.tensor
        def _(pe):
            pe.wait_ge(w_in, 16 * 9)

            def turn_in(b):
                pe.wait_ge(xn_ready, b + 1)
                for q in range(Q):
                    c, half = q // NC, q % NC
                    need(pe, xt_ready, b * Q + q - 1)
                    for j in range(TB // NC):
                        n = half * (TB // NC) + j
                        last = pe.transpose(ps_t[:, (q % 2) * CHUNK + j * P:(q % 2) * CHUNK + (j + 1) * P],
                                            xn[:, n * D + c * P:n * D + (c + 1) * P], ident[:, :])
                    last.then_inc(turned, 1)

            def project(b, d):
                for i in range(3):
                    if d == 0:
                        pe.wait_ge(mix_ready, b * 3 + i + 1)
                    for m in range(NC):
                        k = d * U + i * NC + m
                        need(pe, kvr_ready, b * (C * U) + k - 1)
                        for c in range(C):
                            last = pe.matmul(ps_p[:, (k % 2) * CHUNK:(k % 2 + 1) * CHUNK], weight(i, c, d * P, P),
                                             mixed(i, c, m * CHUNK, CHUNK), start=(c == 0), stop=(c == C - 1))
                        last.then_inc(projected, 1)

            def output(b):
                pe.wait_ge(gated_ready, (b + 1) * C)
                for g in range(G):
                    for j in range(2):
                        n = 2 * g + j
                        for d in range(C):
                            last = pe.matmul(ps_o[:, g * CHUNK + j * D:g * CHUNK + (j + 1) * D],
                                             gated[:, d * S + n * P:d * S + (n + 1) * P], weight(3, d, 0, D),
                                             start=(d == 0), stop=(d == C - 1))
                    last.then_inc(out_ready, 1)

            turn_in(0)
            project(0, 0)

            def turn(b, last):
                if not (isinstance(b, int) and b == 0):
                    output(b - 1)
                if not last:
                    turn_in(b + 1)
                project(b, 1)
                if not last:
                    project(b + 1, 0)

            over_turns(pe, turn)
            output(B - 1)

        @block.scalar
        def _(act):
            act.wait_ge(w_in, 16 * 9)
            act.activation(neg_w[:, :], cols[:, 4 * C:5 * C], ACT.Exp).then_inc(decay_ready, 1)
            act.wait_ge(zeroed, C + 3)

            def take_turned(b):
                need(act, mix_ready, b * 3)
                for q in range(Q):
                    c, half = q // NC, q % NC
                    act.wait_ge(turned, b * Q + q + 1)
                    act.activation(xt[:, c * (S + 1) + 1 + half * CHUNK:c * (S + 1) + 1 + (half + 1) * CHUNK],
                                   ps_t[:, (q % 2) * CHUNK:(q % 2 + 1) * CHUNK], ACT.Copy).then_inc(xt_ready, 1)

            def take_projected(b, d, kinds):
                need(act, gated_ready, (b - 1) * C + d + 1)
                for i in kinds:
                    for m in range(NC):
                        k = d * U + i * NC + m
                        act.wait_ge(projected, b * (C * U) + k + 1)
                        src = ps_p[:, (k % 2) * CHUNK:(k % 2 + 1) * CHUNK]
                        if i < 2:
                            act.activation(chan(i, d, m * CHUNK, CHUNK), src, ACT.Copy).then_inc(kvr_ready, 1)
                        else:
                            act.activation(chan(i, d, m * CHUNK, CHUNK), src, ACT.Exp, scale=-1.0).then_inc(kvr_ready, 1)

            take_turned(0)
            take_projected(0, 0, (0, 1, 2))

            def turn(b, last):
                wkv_exps(act, b, 0)
                if not last:
                    take_turned(b + 1)
                take_projected(b, 1, (0, 1, 2))
                if not last:
                    take_projected(b + 1, 0, (0, 1))
                wkv_exps(act, b, 1)
                if not last:
                    take_projected(b + 1, 0, (2,))

            over_turns(act, turn)

        @block.vector
        def _(dve):
            dve.wait_ge(decay_ready, 1)
            dve.wait_ge(zeroed, C + 3)
            dve.tensor_scalar_mul(neg_w[:, :], neg_w[:, :], -1.0).then_inc(decay_ready, 1)
            dve.wait_ge(decay_ready, 2)
            STEPS = 1 + 8 * C

            def normalise(b):
                for n in range(TB):
                    t = b * TB + n
                    last = dve.tensor_scalar(xn[:, n * D:(n + 1) * D], h[:, ds(t * D, D)], mv[:, ds(t * 2, 1)],
                                             rstd[:, ds(t, 1)], ALU.subtract, ALU.mult)
                last.then_inc(xn_ready, 1)

            def mix_in(s, b):
                dve.wait_ge(xt_ready, (b + 1) * Q)
                s.step(dve.tensor_tensor(dif[:, S:2 * S], xt_now(1), xt_before(1), ALU.subtract))
                dve.wait_ge(dif_ready, b + 1)
                need(dve, projected, b * (C * U))
                for i in range(3):
                    for c in range(C):
                        last = dve.scalar_tensor_tensor(out=mixed(i, c), in0=dif[:, c * S:(c + 1) * S], scalar=col(i, c),
                                                        in1=xt_before(c), op0=ALU.mult, op1=ALU.add)
                    last.then_inc(mix_ready, 1)

            def recurrence(s, b, d):
                k, v, er = chan(0, d), chan(1, d), chan(2, d)
                w1, u1 = neg_w[:, d:d + 1], col(3, d)
                ex_at = b * (4 * C) + 4 * d
                dve.wait_ge(kvr_ready, b * (C * U) + d * U + 2 * NC)
                s.step(dve.tensor_tensor_scan(run_max[:, 1:S + 1], w1.to_broadcast([P, S]), k, FAR, ALU.add, ALU.max))
                dve.scalar_tensor_tensor(out=row(expo, 0), in0=run_max[:, 0:S], scalar=w1, in1=run_max[:, 1:S + 1],
                                         op0=ALU.add, op1=ALU.subtract).then_inc(arg_ready, 1)
                dve.tensor_tensor(row(expo, 1), k, run_max[:, 1:S + 1], ALU.subtract).then_inc(arg_ready, 1)
                s.step(dve.scalar_tensor_tensor(out=row(expo, 2), in0=k, scalar=u1, in1=run_max[:, 0:S],
                                                op0=ALU.add, op1=ALU.subtract))
                dve.tensor_scalar_min(row(expo, 3), row(expo, 2), 0.0).then_inc(arg_ready, 2)
                dve.wait_ge(exp_ready, ex_at + 2)
                s.step(dve.tensor_tensor(row(tmp, 0), row(ex, 1), v, ALU.mult))
                dve.tensor_tensor_scan(aa[:, 1:S + 1], row(ex, 0), row(tmp, 0), 0.0, ALU.mult, ALU.add).then_inc(aa_ready, 1)
                s.step(dve.tensor_tensor_scan(bb[:, 1:S + 1], row(ex, 0), row(ex, 1), 0.0, ALU.mult, ALU.add))
                dve.wait_ge(exp_ready, ex_at + 4)
                s.step(dve.tensor_tensor(row(tmp, 1), row(ex, 2), bb[:, 0:S], ALU.mult))
                s.step(dve.tensor_tensor(row(tmp, 1), row(tmp, 1), row(ex, 3), ALU.add))
                dve.wait_ge(kvr_ready, b * (C * U) + (d + 1) * U)
                dve.wait_ge(aa_ready, b * C + d + 1)
                s.step(dve.scalar_tensor_tensor(out=row(tmp, 0), in0=er, scalar=1.0, in1=row(tmp, 1),
                                                op0=ALU.add, op1=ALU.mult))
                s.step(dve.reciprocal(row(tmp, 1), row(tmp, 0)))
                dve.wait_ge(numer_ready, b * C + d + 1)
                dve.tensor_tensor(row(gated, d), row(gated, d), row(tmp, 1), ALU.mult).then_inc(gated_ready, 1)

            def add_output(b):
                for g in range(G):
                    dve.wait_ge(out_ready, b * G + g + 1)
                    hg = h[:, ds((b * TB + 2 * g) * D, 2 * D)]
                    dve.tensor_tensor(hg, hg, ps_o[:, g * CHUNK:(g + 1) * CHUNK], ALU.add).then_inc(added, 1)

            normalise(0)
            mix_in(Steps(dve, own), 0)

            def turn(b, last):
                s = Steps(dve, own, b * STEPS + 1)
                if not last:
                    normalise(b + 1)
                recurrence(s, b, 0)
                if not (isinstance(b, int) and b == 0):
                    add_output(b - 1)
                if not last:
                    mix_in(s, b + 1)
                recurrence(s, b, 1)
                assert last or s.n == STEPS, s.n

            over_turns(dve, turn)
            add_output(B - 1)
            dve.wait_ge(added, B * G)


def first_of_max(dve, s, vals, top, eq, rev, cmax, onehot):
    s.step(dve.tensor_reduce(top, vals, AX_X, ALU.max))
    s.step(dve.tensor_tensor(eq, vals, top.unsqueeze(2).to_broadcast([P, NT, E]), ALU.is_equal))
    s.step(dve.tensor_tensor(eq, eq, rev.unsqueeze(1).to_broadcast([P, NT, E]), ALU.mult))
    s.step(dve.tensor_reduce(cmax, eq, AX_X, ALU.max))
    s.step(dve.tensor_tensor(onehot, eq, cmax.unsqueeze(2).to_broadcast([P, NT, E]), ALU.is_equal))


def slots_of(dve, s, t, marks, ps_rank, n_slot_tiles):
    rank, total = t["rank"], t["total"]
    s.mark(dve.tensor_copy(rank, ps_rank[:, 0:NT * E]))
    s.step(dve.tensor_copy(total, ps_rank[:, NT * E:2 * NT * E]))
    by = lambda a: a.rearrange("p (n e) -> p n e", e=E)
    for e in range(E):
        s.mark(dve.tensor_tensor_scan(t["incl"][:, e::E], t["one"].to_broadcast([P, NT]), total[:, e::E],
                                      0.0, ALU.mult, ALU.add))
    s.wait()
    s.mark(dve.tensor_tensor(rank, rank, t["incl"], ALU.add))
    s.step(dve.tensor_scalar_add(t["cnt_i"], t["incl"][:, (NT - 1) * E:], float(P - 1)))
    s.step(dve.tensor_single_scalar(t["cnt_i"], t["cnt_i"], -P, ALU.bitwise_and))
    s.step(dve.tensor_copy(t["padded"], t["cnt_i"]))
    s.step(dve.tensor_tensor_scan(t["ends"], t["one"].to_broadcast([P, E]), t["padded"], 0.0, ALU.mult, ALU.add))
    s.step(dve.tensor_tensor(t["base"], t["ends"], t["padded"], ALU.subtract))
    s.step(dve.tensor_tensor(rank, rank, total, ALU.subtract))
    s.step(dve.tensor_tensor(by(rank), by(rank), t["base"].unsqueeze(1).to_broadcast([P, NT, E]), ALU.add))
    J = n_slot_tiles
    ge = t["ge"][0:1, 0:J * E].rearrange("p (j e) -> p j e", e=E)
    s.step(dve.tensor_tensor(ge, t["starts"][0:1, 0:J].unsqueeze(2).to_broadcast([1, J, E]),
                             t["ends"][0:1, :].unsqueeze(1).to_broadcast([1, J, E]), ALU.is_ge))
    s.step(dve.tensor_reduce(t["tile_e"][0:1, 0:J], ge, AX_X, ALU.add))
    s.step(dve.tensor_scalar_min(t["tile_ei"][0:1, 0:J], t["tile_e"][0:1, 0:J], float(E - 1)))


def routing_tables(sb, tag, st):
    t = {}
    for name, n, dt in (("rank", NT * E, F32), ("total", NT * E, F32), ("incl", NT * E, F32), ("padded", E, F32),
                        ("ends", E, F32), ("base", E, F32), ("cnt_i", E, I32), ("ge", 72 * E, F32), ("tile_e", 72, F32)):
        t[name] = sb(tag + "_" + name, [P, n], dt)[:, :]
    t["one"] = st["ones"][:, 0:1]
    t["starts"] = st["starts"][:, :]
    t["tile_ei"] = st["tile_ei"][:, :]
    return t


def load_experts(sp, st, w1, w2, arrived):
    for e in range(E):
        sp.dma_start(st["w1_sb"][:, e * C * HID:(e + 1) * C * HID].rearrange("p (c n) -> p c n", c=C),
                     w1[e].rearrange("(c p) n -> p c n", p=P)).then_inc(arrived, 16)
        sp.dma_start(st["w2_sb"][:, e * HC * D:(e + 1) * HC * D].rearrange("p (c n) -> p c n", c=HC),
                     w2[e].rearrange("(c p) n -> p c n", p=P)).then_inc(arrived, 16)


def route(nc, st, tag, w_router, bias, xn_dram, w1, w2, experts_in):
    h, ident, logits = (st[k] for k in ("h", "ident", "logits"))
    with ExitStack() as ctx:
        sb, pb, sem = allocators(nc, ctx)
        w_sb = sb(tag + "_w", [P, C * E], F32)
        b_sb = sb(tag + "_b", [P, E], F32)
        stats = sb(tag + "_stats", [P, NT * 6], F32)
        mv = sb(tag + "_mv", [P, NT * 2], F32)
        var = sb(tag + "_var", [P, NT], F32)
        dev = sb(tag + "_dev", [P, NT], F32)
        rstd = sb(tag + "_rstd", [P, NT], F32)
        xn = sb(tag + "_xn", [P, NT * D], F32)
        xt = sb(tag + "_xt", [P, 2 * C * S], F32)
        ps_t = pb(tag + "_pt", [P, 4 * CHUNK], F32)
        ps_l = pb(tag + "_pl", [P, CHUNK], F32)
        w_in = sem(tag + "_in")
        own = sem(tag + "_own")
        var_ready = sem(tag + "_var_ready")
        dev_ready = sem(tag + "_dev_ready")
        xn_ready = sem(tag + "_xn_ready")
        xn_stored = sem(tag + "_xn_stored")
        turned = sem(tag + "_turned")
        xt_ready = sem(tag + "_xt_ready")
        logit_done = sem(tag + "_logit_done")
        block = ctx.enter_context(nc.Block())
        Q = C * NC
        n_in = 32 if bias is not None else 16

        def turned_to(b, c, lo, n):
            return xt[:, (b % 2 * C + c) * S + lo:(b % 2 * C + c) * S + lo + n]

        @block.sync
        def _(sp):
            sp.dma_start(w_sb[:, :].rearrange("p (c n) -> p c n", c=C), w_router.rearrange("(c p) n -> p c n", p=P)).then_inc(w_in, 16)
            if bias is not None:
                sp.dma_start(b_sb[:, :], bias.partition_broadcast(P)).then_inc(w_in, 16)
            for b in range(B):
                sp.wait_ge(xn_ready, b + 1)
                sp.dma_start(xn_dram[b * S:(b + 1) * S, :].rearrange("(n p) d -> p n d", p=P),
                             xn[:, b * TB * D:(b + 1) * TB * D].rearrange("p (n d) -> p n d", d=D)).then_inc(xn_stored, 16)
            load_experts(sp, st, w1, w2, experts_in)
            sp.wait_ge(xn_stored, B * 16)

        @block.vector
        def _(dve):
            s = Steps(dve, own)

            def statistics(b):
                for n in range(b * TB, (b + 1) * TB):
                    last = dve.bn_stats(stats[:, n * 6:(n + 1) * 6], h[:, n * D:(n + 1) * D])
                s.step(last)
                for n in range(b * TB, (b + 1) * TB):
                    last = dve.bn_aggr(mv[:, n * 2:(n + 1) * 2], stats[:, n * 6:(n + 1) * 6])
                s.step(last)
                dve.tensor_scalar_add(var[:, b * TB:(b + 1) * TB], mv[:, b * TB * 2 + 1:(b + 1) * TB * 2:2],
                                      LN_EPS).then_inc(var_ready, 1)

            def normalise(b):
                dve.wait_ge(dev_ready, b + 1)
                s.step(dve.reciprocal(rstd[:, b * TB:(b + 1) * TB], dev[:, b * TB:(b + 1) * TB]))
                for n in range(b * TB, (b + 1) * TB):
                    last = dve.tensor_scalar(xn[:, n * D:(n + 1) * D], h[:, n * D:(n + 1) * D], mv[:, 2 * n:2 * n + 1],
                                             rstd[:, n:n + 1], ALU.subtract, ALU.mult)
                last.then_inc(xn_ready, 1)

            statistics(0)
            for b in range(B):
                if b < B - 1:
                    statistics(b + 1)
                normalise(b)
            dve.wait_ge(w_in, n_in)
            dve.wait_ge(logit_done, B)
            if bias is not None:
                s.step(dve.tensor_tensor(logits[:, :].rearrange("p (n e) -> p n e", e=E),
                                         ps_l[:, 0:NT * E].rearrange("p (n e) -> p n e", e=E),
                                         b_sb[:, :].unsqueeze(1).to_broadcast([P, NT, E]), ALU.add))
            else:
                s.step(dve.tensor_copy(logits[:, :], ps_l[:, 0:NT * E]))

        @block.scalar
        def _(act):
            def deviation(b):
                act.wait_ge(var_ready, b + 1)
                act.activation(dev[:, b * TB:(b + 1) * TB], var[:, b * TB:(b + 1) * TB], ACT.Sqrt).then_inc(dev_ready, 1)

            deviation(0)
            for b in range(B):
                if b < B - 1:
                    deviation(b + 1)
                if b >= 2:
                    act.wait_ge(logit_done, b - 1)
                for q in range(Q):
                    c, half = q // NC, q % NC
                    act.wait_ge(turned, b * Q + q + 1)
                    act.activation(turned_to(b, c, half * CHUNK, CHUNK), ps_t[:, q * CHUNK:(q + 1) * CHUNK],
                                   ACT.Copy).then_inc(xt_ready, 1)

        @block.tensor
        def _(pe):
            def turn(b):
                pe.wait_ge(xn_ready, b + 1)
                for q in range(Q):
                    c, half = q // NC, q % NC
                    if b >= 1:
                        pe.wait_ge(xt_ready, (b - 1) * Q + q + 1)
                    for j in range(TB // NC):
                        n = b * TB + half * (TB // NC) + j
                        last = pe.transpose(ps_t[:, q * CHUNK + j * P:q * CHUNK + (j + 1) * P],
                                            xn[:, n * D + c * P:n * D + (c + 1) * P], ident[:, :])
                    last.then_inc(turned, 1)

            pe.wait_ge(w_in, n_in)
            turn(0)
            for b in range(B):
                if b < B - 1:
                    turn(b + 1)
                pe.wait_ge(xt_ready, (b + 1) * Q)
                for n in range(TB):
                    for c in range(C):
                        last = pe.matmul(ps_l[:, (b * TB + n) * E:(b * TB + n + 1) * E], turned_to(b, c, n * P, P),
                                         w_sb[:, c * E:(c + 1) * E], start=(c == 0), stop=(c == C - 1))
                last.then_inc(logit_done, 1)


def slot_table(nc, st, tag, choices, n_slot_tiles):
    pos, number, slot_rows = st["pos"], st["number"], st["slot_rows"]
    with ExitStack() as ctx:
        sb, pb, sem = allocators(nc, ctx)
        W, J, R = choices * NT, n_slot_tiles, 8
        pos_i = sb(tag + "_pos_i", [P, W], I32)
        part_i = sb(tag + "_part_i", [P, 2 * W], I32)
        low = sb(tag + "_low", [P, W], F32)
        high = sb(tag + "_high", [P, W], F32)
        at_low = sb(tag + "_at_low", [P, R * P], F32)
        at_high = sb(tag + "_at_high", [P, R * J], F32)
        empty = sb(tag + "_empty", [P, J], F32)
        row = sb(tag + "_row", [P, J], F32)
        row_i = sb(tag + "_row_i", [P, J], I32)
        ps = pb(tag + "_ps", [P, CHUNK], F32)
        own = sem(tag + "_own")
        high_marked = sem(tag + "_high_marked")
        marked = sem(tag + "_marked")
        placed = sem(tag + "_placed")
        block = ctx.enter_context(nc.Block())
        FREE = 2
        F = R // FREE

        def over_rings(eng, ring):
            ring(0)
            with eng.Fori(1, W // R - 1) as i:
                ring(i)
            ring(W // R - 1)

        @block.vector
        def _(dve):
            s = Steps(dve, own)
            s.step(dve.tensor_copy(pos_i[:, :], pos[:, 0:W]))
            s.mark(dve.tensor_single_scalar(part_i[:, 0:W], pos_i[:, :], P - 1, ALU.bitwise_and))
            s.step(dve.tensor_single_scalar(part_i[:, W:2 * W], pos_i[:, :], P.bit_length() - 1, ALU.arith_shift_right))
            s.mark(dve.tensor_copy(low[:, :], part_i[:, 0:W]))
            s.step(dve.tensor_copy(high[:, :], part_i[:, W:2 * W]))

            def ring(i):
                for f in range(FREE):
                    need(dve, placed, i * FREE + f + 1 - FREE)
                    count = lambda n: st["count"][:, 0:n].unsqueeze(1).to_broadcast([P, F, n])
                    of_token = lambda a, n: a[:, ds(i * R + f * F, F)].unsqueeze(2).to_broadcast([P, F, n])
                    by_high = at_high[:, f * F * J:(f + 1) * F * J].rearrange("p (k n) -> p k n", n=J)
                    dve.tensor_tensor(by_high, count(J), of_token(high, J), ALU.is_equal).then_inc(high_marked, 1)
                    dve.tensor_tensor(at_low[:, f * F * P:(f + 1) * F * P].rearrange("p (k n) -> p k n", n=P), count(P),
                                      of_token(low, P), ALU.is_equal).then_inc(marked, 1)
                    dve.wait_ge(high_marked, i * FREE + f + 1)
                    dve.tensor_tensor(by_high, by_high, of_token(number, J), ALU.mult).then_inc(marked, 1)

            over_rings(dve, ring)
            dve.wait_ge(placed, W // R * FREE)
            s.mark(dve.tensor_single_scalar(empty[:, :], ps[:, 0:J], 0.0, ALU.is_equal))
            s.step(dve.tensor_scalar_add(row[:, :], ps[:, 0:J], -1.0))
            s.mark(dve.tensor_copy(row_i[:, :], row[:, :]))
            s.step(dve.scalar_tensor_tensor(out=empty[:, :], in0=st["slot_number"][:, 0:J], scalar=choices * T + 1.0,
                                            in1=empty[:, :], op0=ALU.add, op1=ALU.mult))
            s.mark(dve.tensor_single_scalar(slot_rows[:, 0:2 * J:2], row_i[:, :], T - 1, ALU.bitwise_and))
            s.step(dve.tensor_tensor(slot_rows[:, 1:2 * J:2], row[:, :], empty[:, :], ALU.add))

        @block.tensor
        def _(pe):
            def ring(i):
                for k in range(R):
                    if k % F == 0:
                        pe.wait_ge(marked, i * (2 * FREE) + 2 * (k // F) + 2)
                    n = i * R + k if isinstance(i, int) else None
                    last = pe.matmul(ps[:, 0:J], at_low[:, k * P:(k + 1) * P], at_high[:, k * J:(k + 1) * J],
                                     start=(n == 0), stop=(n == W - 1))
                    if k % F == F - 1:
                        last.then_inc(placed, 1)

            over_rings(pe, ring)


def dispatch_top2(nc, st):
    logits, gates, pos = (st[k] for k in ("logits", "gates", "pos"))
    with ExitStack() as ctx:
        sb, pb, sem = allocators(nc, ctx)
        t = routing_tables(sb, "d0", st)
        rev = st["rev"][:, :]
        vals2 = sb("d0_vals2", [P, NT * E], F32)[:, :]
        eq = sb("d0_eq", [P, NT * E], F32)[:, :]
        oh1 = sb("d0_oh1", [P, NT * E], F32)[:, :]
        oh2 = sb("d0_oh2", [P, NT * E], F32)[:, :]
        marks = sb("d0_marks", [P, NT * E], F32)[:, :]
        top1 = sb("d0_top1", [P, NT], F32)[:, :]
        top2 = sb("d0_top2", [P, NT], F32)[:, :]
        cmax = sb("d0_cmax", [P, NT], F32)[:, :]
        dif = sb("d0_dif", [P, NT], F32)[:, :]
        ps_rank = pb("d0_ps", [P, 2 * NT * E], F32)
        own = sem("d0_own")
        dif_ready = sem("d0_dif_ready")
        exp_ready = sem("d0_exp_ready")
        marks_ready = sem("d0_marks_ready")
        ranked = sem("d0_ranked")
        block = ctx.enter_context(nc.Block())
        by = lambda a: a.rearrange("p (n e) -> p n e", e=E)

        @block.vector
        def _(dve):
            s = Steps(dve, own)
            first_of_max(dve, s, by(logits[:, :]), top1, by(eq), rev, cmax, by(oh1))
            s.step(dve.scalar_tensor_tensor(out=vals2, in0=oh1, scalar=-3e38, in1=logits[:, :], op0=ALU.mult, op1=ALU.add))
            first_of_max(dve, s, by(vals2), top2, by(eq), rev, cmax, by(oh2))
            dve.tensor_tensor(marks, oh1, oh2, ALU.add).then_inc(marks_ready, 1)
            dve.tensor_tensor(dif, top2, top1, ALU.subtract).then_inc(dif_ready, 1)
            dve.wait_ge(exp_ready, 1)
            s.step(dve.tensor_scalar_add(top2, dif, 1.0))
            s.step(dve.reciprocal(gates[:, 0:NT], top2))
            s.step(dve.tensor_tensor(gates[:, NT:2 * NT], gates[:, 0:NT], dif, ALU.mult))
            dve.wait_ge(ranked, 1)
            slots_of(dve, s, t, marks, ps_rank, 72)
            for w, oh in enumerate((oh1, oh2)):
                s.step(dve.tensor_tensor(oh, oh, t["rank"], ALU.mult))
                s.step(dve.tensor_reduce(pos[:, w * NT:(w + 1) * NT], by(oh), AX_X, ALU.add))

        @block.scalar
        def _(act):
            act.wait_ge(dif_ready, 1)
            act.activation(dif, dif, ACT.Exp).then_inc(exp_ready, 1)

        @block.tensor
        def _(pe):
            pe.wait_ge(marks_ready, 1)
            pe.matmul(ps_rank[:, 0:NT * E], st["before"][:, :], marks, start=True, stop=True)
            pe.matmul(ps_rank[:, NT * E:2 * NT * E], st["ones"][:, :], marks, start=True, stop=True).then_inc(ranked, 1)


def experts(nc, st, tag, n_tiles, xn_dram, y_dram, b1, b2, func, weights_in):
    ident, w1_sb, w2_sb, tile_ei, slot_rows = (st[k] for k in ("ident", "w1_sb", "w2_sb", "tile_ei", "slot_rows"))
    X4, X8 = 4, 8
    with ExitStack() as ctx:
        sb, pb, sem = allocators(nc, ctx)
        rows_now = sb(tag + "_rows_now", [P, X8 * 2], I32)
        xin = sb(tag + "_xin", [P, X4 * D], F32)
        xt = sb(tag + "_xt", [P, 2 * D], F32)
        w1_now = sb(tag + "_w1_now", [P, 2 * C * HID], F32)
        hid = sb(tag + "_hid", [P, 2 * HID], F32) if b1 is not None else None
        hidt = sb(tag + "_hidt", [P, 2 * HID], F32)
        yout = sb(tag + "_yout", [P, X4 * D], F32)
        b1_all = sb(tag + "_b1", [P, E * HC], F32) if b1 is not None else None
        b2_all = sb(tag + "_b2", [P, E * D], F32) if b2 is not None else None
        ps_x = pb(tag + "_px", [P, 2 * CHUNK], F32)
        ps_h = pb(tag + "_ph", [P, 2 * HID], F32)
        ps_y = pb(tag + "_py", [P, 2 * CHUNK], F32)
        bias_in = sem(tag + "_bias_in")
        rows_ready = sem(tag + "_rows_ready")
        x_in = [sem(f"{tag}_x_in{k}") for k in range(X4)]
        y_out = [sem(f"{tag}_y_out{k}") for k in range(X4)]
        x_turned = sem(tag + "_x_turned")
        xt_ready = sem(tag + "_xt_ready")
        w1_ready = sem(tag + "_w1_ready")
        first_done = sem(tag + "_first_done")
        hid_ready = sem(tag + "_hid_ready")
        hidt_ready = sem(tag + "_hidt_ready")
        second_done = sem(tag + "_second_done")
        y_ready = sem(tag + "_y_ready")
        passed = sem(tag + "_passed")
        block = ctx.enter_context(nc.Block())
        LOOPS = n_tiles // 8 - 1
        assert n_tiles == 8 * LOOPS + 8

        def over_tiles(eng, step):
            for c in range(5):
                step(0, c)
            with eng.Fori(0, LOOPS) as i:
                for c in range(5, 13):
                    step(i, c)
            for c in range(5, 8):
                step(LOOPS, c)

        def tile_need(eng, s, i, c):
            need(eng, s, i * 8 + c)

        def y_stored(eng, i, c):
            need(eng, y_out[c % X4], i * (8 // X4 * 16) + (c // X4 + 1) * 16)

        def slot(t, c, n, w):
            return t[:, (c % n) * w:(c % n + 1) * w]

        def pick(eng, i, c):
            return eng.value_load(tile_ei[0:1, ds(i * 8 + c, 1)], min_val=0, max_val=E - 1)

        @block.sync
        def _(sp):
            if b1 is not None:
                sp.dma_start(b1_all[:, :], b1).then_inc(bias_in, 16)
                sp.dma_start(b2_all[:, :], b2.rearrange("e n -> (e n)").partition_broadcast(P)).then_inc(bias_in, 16)

        @block.gpsimd
        def _(pool):
            def gather(i, c):
                pool.wait_ge(rows_ready, i * 8 + c + 1)
                tile_need(pool, x_turned, i, c + 1 - X4)
                pool.sem_inc(passed, 1)
                pool.indirect_dma_start(out=slot(xin, c, X4, D), out_offset=None, in_=xn_dram,
                                        in_offset=bass.IndirectOffsetOnAxis(ap=rows_now[:, 2 * (c % X8):2 * (c % X8) + 1], axis=0),
                                        ).then_inc(x_in[c % X4], 16)

            def scatter(i, c):
                pool.wait_ge(y_ready, i * 8 + c + 1)
                pool.sem_inc(passed, 1)
                pool.indirect_dma_start(out=y_dram, out_offset=bass.IndirectOffsetOnAxis(
                    ap=rows_now[:, 2 * (c % X8) + 1:2 * (c % X8) + 2], axis=0),
                                        in_=slot(yout, c, X4, D), in_offset=None).then_inc(y_out[c % X4], 16)

            for c in range(X4):
                gather(0, c)
            with pool.Fori(0, LOOPS) as i:
                for c in range(8):
                    gather(i, c + X4)
                    scatter(i, c)
            for c in range(8):
                if c + X4 < 8:
                    gather(LOOPS, c + X4)
                scatter(LOOPS, c)
            for c in range(X4):
                pool.wait_ge(y_out[c], 16 * (n_tiles // X4))

        @block.tensor
        def _(pe):
            pe.wait_ge(weights_in, 2 * E * 16)

            def turn_x(i, c):
                pe.wait_ge(x_in[c % X4], i * 32 + (c // X4 + 1) * 16)
                tile_need(pe, xt_ready, i, c - 1)
                for k in range(C):
                    last = pe.transpose(ps_x[:, (c % 2) * CHUNK + k * P:(c % 2) * CHUNK + (k + 1) * P],
                                        xin[:, (c % X4) * D + k * P:(c % X4) * D + (k + 1) * P], ident[:, :])
                last.then_inc(x_turned, 1)

            def first(i, c):
                tile_need(pe, xt_ready, i, c + 1)
                tile_need(pe, w1_ready, i, c + 1)
                tile_need(pe, hid_ready if b1 is not None else hidt_ready, i, c - 1)
                for m in range(HC):
                    for k in range(C):
                        at = (c % 2) * C * HID + k * HID + m * P
                        last = pe.matmul(ps_h[:, (c % 2) * HID + m * P:(c % 2) * HID + (m + 1) * P], w1_now[:, at:at + P],
                                         xt[:, (c % 2) * D + k * P:(c % 2) * D + (k + 1) * P], start=(k == 0), stop=(k == C - 1))
                last.then_inc(first_done, 1)

            def second(i, c):
                e = pick(pe, i, c)
                tile_need(pe, hidt_ready, i, c + 1)
                tile_need(pe, y_ready, i, c - 1)
                for k in range(HC):
                    last = pe.matmul(ps_y[:, (c % 2) * CHUNK:(c % 2) * CHUNK + D],
                                     hidt[:, (c % 2) * HID + k * P:(c % 2) * HID + (k + 1) * P],
                                     w2_sb[:, ds(e * (HC * D) + k * D, D)], start=(k == 0), stop=(k == HC - 1))
                last.then_inc(second_done, 1)

            turn_x(0, 0)

            def tile(i, c):
                if not (isinstance(i, int) and 8 * i + c == n_tiles - 1):
                    turn_x(i, c + 1)
                first(i, c)
                if not (isinstance(i, int) and 8 * i + c == 0):
                    second(i, c - 1)

            over_tiles(pe, tile)
            second(LOOPS, 7)

        @block.vector
        def _(dve):
            if b1 is not None:
                dve.wait_ge(bias_in, 32)

            def take_rows(i, c):
                if not (isinstance(i, int) and 8 * i + c < X8):
                    y_stored(dve, i, c - X8)
                dve.tensor_copy(slot(rows_now, c, X8, 2), slot_rows[:, ds((i * 8 + c) * 2, 2)]).then_inc(rows_ready, 1)

            def take_x(i, c):
                tile_need(dve, x_turned, i, c + 1)
                tile_need(dve, first_done, i, c - 1)
                dve.tensor_copy(slot(xt, c, 2, D), ps_x[:, (c % 2) * CHUNK:(c % 2) * CHUNK + D]).then_inc(xt_ready, 1)

            def add_bias(i, c):
                e = pick(dve, i, c)
                tile_need(dve, first_done, i, c + 1)
                tile_need(dve, hidt_ready, i, c - 1)
                by = lambda a: a.rearrange("p (m t) -> p m t", t=P)
                dve.tensor_tensor(by(slot(hid, c, 2, HID)), by(slot(ps_h, c, 2, HID)),
                                  b1_all[:, ds(e * HC, HC)].unsqueeze(2).to_broadcast([P, HC, P]), ALU.add).then_inc(hid_ready, 1)

            def take_y(i, c):
                if b2 is not None:
                    e = pick(dve, i, c)
                tile_need(dve, second_done, i, c + 1)
                if not (isinstance(i, int) and 8 * i + c < X4):
                    y_stored(dve, i, c - X4)
                y = ps_y[:, (c % 2) * CHUNK:(c % 2) * CHUNK + D]
                if b2 is not None:
                    dve.tensor_tensor(slot(yout, c, X4, D), y, b2_all[:, ds(e * D, D)], ALU.add).then_inc(y_ready, 1)
                else:
                    dve.tensor_copy(slot(yout, c, X4, D), y).then_inc(y_ready, 1)

            AHEAD = 3
            for c in range(AHEAD):
                take_rows(0, c)
            take_x(0, 0)

            def tile(i, c):
                if not (isinstance(i, int) and 8 * i + c + AHEAD >= n_tiles):
                    take_rows(i, c + AHEAD)
                if not (isinstance(i, int) and 8 * i + c == n_tiles - 1):
                    take_x(i, c + 1)
                if b1 is not None:
                    add_bias(i, c)
                if not (isinstance(i, int) and 8 * i + c == 0):
                    take_y(i, c - 1)

            over_tiles(dve, tile)
            take_y(LOOPS, 7)

        @block.scalar
        def _(act):
            act.wait_ge(weights_in, 2 * E * 16)

            def take_w1(i, c):
                e = pick(act, i, c)
                tile_need(act, first_done, i, c - 1)
                act.activation(slot(w1_now, c, 2, C * HID), w1_sb[:, ds(e * (C * HID), C * HID)], ACT.Copy).then_inc(w1_ready, 1)

            take_w1(0, 0)

            def tile(i, c):
                if not (isinstance(i, int) and 8 * i + c == n_tiles - 1):
                    take_w1(i, c + 1)
                tile_need(act, second_done, i, c - 1)
                if b1 is not None:
                    tile_need(act, hid_ready, i, c + 1)
                    act.activation(slot(hidt, c, 2, HID), slot(hid, c, 2, HID), func).then_inc(hidt_ready, 1)
                else:
                    tile_need(act, first_done, i, c + 1)
                    act.activation(slot(hidt, c, 2, HID), slot(ps_h, c, 2, HID), func).then_inc(hidt_ready, 1)

            over_tiles(act, tile)


def combine(nc, st, tag, choices, y_dram, out=None):
    h, gates = st["h"], st["gates"]
    with ExitStack() as ctx:
        sb, pb, sem = allocators(nc, ctx)
        y = sb(tag + "_y", [P, choices * NT * D], F32)
        y_in = [sem(f"{tag}_y_in{k}") for k in range(choices * B)]
        own = sem(tag + "_own")
        added = sem(tag + "_added")
        stored = sem(tag + "_stored")
        block = ctx.enter_context(nc.Block())

        def load(eng, b, w):
            eng.dma_start(y[:, (w * NT + b * TB) * D:(w * NT + (b + 1) * TB) * D].rearrange("p (n d) -> p n d", d=D),
                          y_dram[w * T + b * S:w * T + (b + 1) * S, :].rearrange("(n p) d -> p n d", p=P)).then_inc(y_in[w * B + b], 16)

        @block.sync
        def _(sp):
            for b in range(B):
                for w in range(choices):
                    load(sp, b, w)
            if out is not None:
                for b in range(B):
                    sp.wait_ge(added, b + 1)
                    sp.dma_start(out[b].rearrange("(n p) d -> p n d", p=P),
                                 h[:, b * TB * D:(b + 1) * TB * D].rearrange("p (n d) -> p n d", d=D)).then_inc(stored, 16)
                sp.wait_ge(stored, 16 * B)

        @block.vector
        def _(dve):
            s = Steps(dve, own)
            for b in range(B):
                for w in range(choices):
                    dve.wait_ge(y_in[w * B + b], 16)
                    for n in range(b * TB, (b + 1) * TB):
                        hn = h[:, n * D:(n + 1) * D]
                        last = dve.scalar_tensor_tensor(out=hn, in0=y[:, (w * NT + n) * D:(w * NT + n + 1) * D],
                                                        scalar=gates[:, w * NT + n:w * NT + n + 1], in1=hn, op0=ALU.mult, op1=ALU.add)
                    if w < choices - 1:
                        s.step(last)
                last.then_inc(added, 1)
            dve.wait_ge(added, B)


HEADS, HD = 16, 16
GH = 4
GROUPS = B * HEADS // GH
GCH = GH * HD
KEYS = 256
NB = S // KEYS
PARTS = 3
QROWS = 6 * HD
MROWS = PARTS * NB
ROWS = QROWS + MROWS


def project_qkv(nc, st, wq, wk, wv, v_ones, qk_dram, v_dram):
    h, mv, rstd, ident = (st[x] for x in ("h", "mv", "rstd", "ident"))
    with ExitStack() as ctx:
        sb, pb, sem = allocators(nc, ctx)
        VW = GROUPS // B * P
        wqk_sb = sb("qk_w", [P, 2 * C * D], F32)
        wv_sb = sb("v_w", [P, C * D], F32)
        xn = sb("qk_xn", [P, TB * D], F32)
        xt = sb("qk_xt", [P, C * S], F32)
        parts = sb("qk_parts", [P, 2 * PARTS * S], BF16)
        rest = sb("qk_rest", [P, 2 * CHUNK], F32)
        v_sb = sb("v_sb", [P, 4 * VW], F32)
        ps_t = pb("qk_pt", [P, 2 * CHUNK], F32)
        ps_q = pb("qk_pq", [P, 2 * CHUNK], F32)
        ps_v = pb("qk_pv", [P, 2 * CHUNK], F32)
        w_in = sem("qk_w_in")
        xn_ready = sem("qk_xn_ready")
        turned = sem("qk_turned")
        xt_ready = sem("qk_xt_ready")
        projected = sem("qk_projected")
        high_ready = sem("qk_high")
        rest_ready = sem("qk_rest_ready")
        mid_ready = sem("qk_mid")
        low_ready = sem("qk_low")
        parts_out = [sem(f"qk_parts_out{k}") for k in range(2)]
        v_done = sem("qk_v_done")
        v_ready = sem("qk_v_ready")
        v_out = [sem(f"qk_v_out{k}") for k in range(4)]
        block = ctx.enter_context(nc.Block())
        Q = C * NC
        U = 2 * C * NC
        SCALE = HD ** -0.5

        def part(k, p, lo, n):
            return parts[:, (k % 2 * PARTS + p) * S + lo:(k % 2 * PARTS + p) * S + lo + n]

        @block.sync
        def _(sp):
            for i, w in enumerate((wq, wk)):
                sp.dma_start(wqk_sb[:, i * C * D:(i + 1) * C * D].rearrange("p (c n) -> p c n", c=C),
                             w.rearrange("(c p) n -> p c n", p=P)).then_inc(w_in, 16)
            sp.dma_start(wv_sb[:, :].rearrange("p (c n) -> p c n", c=C), wv.rearrange("(c p) n -> p c n", p=P)).then_inc(w_in, 16)
            for k in range(4):
                sp.dma_start(v_sb[:, k * VW:(k + 1) * VW], v_ones.partition_broadcast(P)).then_inc(w_in, 16)
            with sp.Fori(0, B) as b:
                for k in range(2 * C):
                    i, d = k // C, k % C
                    sp.wait_ge(low_ready, b * U + (k + 1) * NC)
                    for half in range(2):
                        sp.dma_start(qk_dram[ds(b * (GROUPS // B) + d * 2 + half, 1), i].rearrange("o p c t -> c (o p) t"),
                                     parts[half * GCH:(half + 1) * GCH, (k % 2) * PARTS * S:(k % 2 + 1) * PARTS * S]
                                     .rearrange("c (p t) -> c p t", p=PARTS)).then_inc(parts_out[k % 2], 16)
            for k in range(2):
                sp.wait_ge(parts_out[k], B * C * 32)

        @block.gpsimd
        def _(pool):
            with pool.Fori(0, B) as b:
                for n in range(TB):
                    pool.wait_ge(v_ready, b * TB + n + 1)
                    pool.dma_start(v_dram[ds(b * (GROUPS // B), GROUPS // B), n * P:(n + 1) * P, :].rearrange("g t c -> t g c"),
                                   v_sb[:, (n % 4) * VW:(n % 4 + 1) * VW].rearrange("p (g c) -> p g c", g=GROUPS // B)
                                   ).then_inc(v_out[n % 4], 16)
            for k in range(4):
                pool.wait_ge(v_out[k], B * TB // 4 * 16)

        @block.tensor
        def _(pe):
            pe.wait_ge(w_in, 7 * 16)
            with pe.Fori(0, B) as b:
                pe.wait_ge(xn_ready, b + 1)
                for q in range(Q):
                    c, half = q // NC, q % NC
                    if q >= 2:
                        pe.wait_ge(xt_ready, b * Q + q - 1)
                    for j in range(TB // NC):
                        n = half * (TB // NC) + j
                        last = pe.transpose(ps_t[:, (q % 2) * CHUNK + j * P:(q % 2) * CHUNK + (j + 1) * P],
                                            xn[:, n * D + c * P:n * D + (c + 1) * P], ident[:, :])
                    last.then_inc(turned, 1)
                pe.wait_ge(xt_ready, (b + 1) * Q)
                for u in range(U):
                    i, d, m = u // (C * NC), u // NC % C, u % NC
                    if u >= 2:
                        pe.wait_ge(rest_ready, b * U + u - 1)
                    for c in range(C):
                        last = pe.matmul(ps_q[:, (u % 2) * CHUNK:(u % 2 + 1) * CHUNK],
                                         wqk_sb[:, (i * C + c) * D + d * P:(i * C + c) * D + (d + 1) * P],
                                         xt[:, c * S + m * CHUNK:c * S + (m + 1) * CHUNK], start=(c == 0), stop=(c == C - 1))
                    last.then_inc(projected, 1)
                    n = u
                    if n >= 2:
                        pe.wait_ge(v_ready, b * TB + n - 1)
                    for c in range(C):
                        last = pe.matmul(ps_v[:, (n % 2) * CHUNK:(n % 2) * CHUNK + D], xt[:, c * S + n * P:c * S + (n + 1) * P],
                                         wv_sb[:, c * D:(c + 1) * D], start=(c == 0), stop=(c == C - 1))
                    last.then_inc(v_done, 1)

        @block.scalar
        def _(act):
            def sequence(b):
                for q in range(Q):
                    c, half = q // NC, q % NC
                    act.wait_ge(turned, b * Q + q + 1)
                    act.activation(xt[:, c * S + half * CHUNK:c * S + (half + 1) * CHUNK],
                                   ps_t[:, (q % 2) * CHUNK:(q % 2 + 1) * CHUNK], ACT.Copy).then_inc(xt_ready, 1)
                for u in range(U):
                    k, m = u // NC, u % NC
                    if m == 0:
                        need(act, parts_out[k % 2], b * (C * 32) + k // 2 * 32)
                    act.wait_ge(projected, b * U + u + 1)
                    act.activation(part(k, 0, m * CHUNK, CHUNK), ps_q[:, (u % 2) * CHUNK:(u % 2 + 1) * CHUNK], ACT.Copy,
                                   scale=SCALE if k < C else 1.0).then_inc(high_ready, 1)
                    act.wait_ge(rest_ready, b * U + u + 1)
                    act.activation(part(k, 1, m * CHUNK, CHUNK), rest[:, (u % 2) * CHUNK:(u % 2 + 1) * CHUNK],
                                   ACT.Copy).then_inc(mid_ready, 1)
                act.wait_ge(v_done, (b + 1) * TB)

            over_sequences(act, sequence)

        @block.vector
        def _(dve):
            dve.wait_ge(w_in, 7 * 16)

            def sequence(b):
                for n in range(TB):
                    t = b * TB + n
                    last = dve.tensor_scalar(xn[:, n * D:(n + 1) * D], h[:, ds(t * D, D)], mv[:, ds(t * 2, 1)],
                                             rstd[:, ds(t, 1)], ALU.subtract, ALU.mult)
                last.then_inc(xn_ready, 1)
                for u in range(U):
                    k, m = u // NC, u % NC
                    r = rest[:, (u % 2) * CHUNK:(u % 2 + 1) * CHUNK]
                    dve.wait_ge(high_ready, b * U + u + 1)
                    if u > 0:
                        dve.wait_ge(low_ready, b * U + u)
                    dve.scalar_tensor_tensor(out=r, in0=ps_q[:, (u % 2) * CHUNK:(u % 2 + 1) * CHUNK],
                                             scalar=SCALE if k < C else 1.0, in1=part(k, 0, m * CHUNK, CHUNK),
                                             op0=ALU.mult, op1=ALU.subtract).then_inc(rest_ready, 1)
                    n = u
                    dve.wait_ge(v_done, b * TB + n + 1)
                    need(dve, v_out[n % 4], b * 32 + n // 4 * 16)
                    dve.tensor_copy(v_sb[:, (n % 4) * VW:(n % 4 + 1) * VW].rearrange("p (j c) -> p j c", j=HEADS)[:, :, 0:HD],
                                    ps_v[:, (n % 2) * CHUNK:(n % 2) * CHUNK + D].rearrange("p (j c) -> p j c", j=HEADS)
                                    ).then_inc(v_ready, 1)
                    dve.wait_ge(rest_ready, b * U + u + 1)
                    dve.wait_ge(mid_ready, b * U + u + 1)
                    dve.tensor_tensor(part(k, 2, m * CHUNK, CHUNK), r, part(k, 1, m * CHUNK, CHUNK),
                                      ALU.subtract).then_inc(low_ready, 1)
                dve.wait_ge(low_ready, (b + 1) * U)

            over_sequences(dve, sequence)


def attention(nc, st, qk_dram, v_dram, block_rows, ident_bits):
    ctx_all = st["ctx_all"]
    with ExitStack() as ctx:
        sb, pb, sem = allocators(nc, ctx)
        NU = 3
        qs = [sb(f"at_q{u}", [ROWS, GH * S], BF16) for u in range(NU)]
        ks = [sb(f"at_k{u}", [ROWS, GH * S], BF16) for u in range(NU)]
        vs = [sb(f"at_v{u}", [P, TB * P], F32) for u in range(NU)]
        identb = sb("at_identb", [P, P], BF16)
        ex = sb("at_ex", [P, 2 * GH * CHUNK], F32)
        raw = sb("at_raw", [P, CHUNK], F32)
        den = sb("at_den", [P, GH * GH], F32)
        mx = sb("at_mx", [P, GH * TB * NB], F32)
        neg = sb("at_neg", [P, TB * NB], F32)
        zero = sb("at_zero", [P, TB * NB], F32)
        rem = sb("at_rem", [P, TB * NB], F32)
        mp = sb("at_mp", [P, GH * TB * MROWS], BF16)
        ps_k = pb("at_pk", [P, 4 * CHUNK], F32)
        ps_s = pb("at_ps", [P, 2 * CHUNK], F32)
        ps_v = pb("at_pv", [P, CHUNK], F32)
        ps_m = pb("at_pm", [P, CHUNK], F32)
        ps_mb = ps_m[:, :].bitcast(BF16)
        set_up = sem("at_set_up")
        zero_set = sem("at_zero_set")
        in_k = [sem(f"at_in{u}") for u in range(NU)]
        scored = sem("at_scored")
        maxed = sem("at_maxed")
        own = sem("at_own")
        split = sem("at_split")
        rows_turned = sem("at_rows_turned")
        rows_copied = sem("at_rows_copied")
        keyed = sem("at_keyed")
        exp_done = sem("at_exp_done")
        pv_done = sem("at_pv_done")
        pv_copied = sem("at_pv_copied")
        ctx_turned = sem("at_ctx_turned")
        den_ready = sem("at_den_ready")
        ctx_read = sem("at_ctx_read")
        block = ctx.enter_context(nc.Block())
        N_IN = (2 * 6 + 1) * 16
        STEPS = 2 * TB
        UNITS = GH * TB * 2
        FROM = [5 * s for s in range(5)] + [4 * s + 4 for s in range(5, STEPS)] + [UNITS]
        TURN_ROWS = {5: 0, 8: 1, 12: 2, STEPS - 1: GH - 1}
        LOOPS = (GROUPS - 4) // NU

        def over_groups(eng, group):
            group(0, 0)
            with eng.Fori(0, LOOPS) as i:
                for v in (1, 2, 3):
                    group(i, v)
            for v in (1, 2, 3):
                group(LOOPS, v)

        def need(eng, s, i, v, per, c):
            if isinstance(i, int) and per * (NU * i + v) + c <= 0:
                return
            eng.wait_ge(s, i * (per * NU) + (per * v + c))

        def is_first(i, v):
            return isinstance(i, int) and NU * i + v == 0

        def is_last(i, v):
            return isinstance(i, int) and NU * i + v == GROUPS - 1

        @block.sync
        def _(sp):
            for u in range(NU):
                sp.dma_start(ks[u][QROWS:ROWS, :].bitcast(U16), block_rows).then_inc(set_up, 16)
            sp.dma_start(identb[:, :].bitcast(U16), ident_bits).then_inc(set_up, 16)

            def load(i, v):
                if not (isinstance(i, int) and NU * i + v < NU):
                    need(sp, pv_done, i, v, STEPS, -2 * STEPS)
                u, g = v % NU, (i * NU + v)
                for t, i_qk, order in ((qs, 0, (0, 1, 2, 0, 1, 0)), (ks, 1, (0, 0, 0, 1, 1, 2))):
                    for r, p in enumerate(order):
                        src = qk_dram[ds(g, 1), i_qk, p] if not isinstance(g, int) else qk_dram[g:g + 1, i_qk, p]
                        sp.dma_start(t[u][r * HD:(r + 1) * HD, :].rearrange("c (j t) -> c j t", j=GH),
                                     src.rearrange("o (j c) t -> c (o j) t", c=HD)).then_inc(in_k[u], 16)
                src = v_dram[ds(g, 1)] if not isinstance(g, int) else v_dram[g:g + 1]
                sp.dma_start(vs[u][:, :].rearrange("p (n c) -> p n c", c=P),
                             src.rearrange("o (n p) c -> p (o n) c", p=P)).then_inc(in_k[u], 16)

            for v in range(NU):
                load(0, v)
            with sp.Fori(0, LOOPS) as i:
                for v in range(NU, 2 * NU):
                    load(i, v)
            load(LOOPS, NU)

        @block.gpsimd
        def _(pool):
            pool.memset(zero[:, :], 0.0).then_inc(zero_set, 1)
            pool.wait_ge(zero_set, 1)

            def splits(i, v):
                for j in range(GH):
                    base = i * (4 * GH * NU) + 4 * (GH * v + j)
                    m = mx[:, j * TB * NB:(j + 1) * TB * NB]
                    by = mp[:, j * TB * MROWS:(j + 1) * TB * MROWS].rearrange("p (n k) -> p n k", k=PARTS)
                    as3 = lambda a: a.unsqueeze(2)
                    need(pool, maxed, i, v, UNITS, (j + 1) * 2 * TB)
                    need(pool, rows_turned, i, v, GH, j + 1 - GH)
                    need(pool, split, i, v, GH, j)
                    pool.tensor_tensor(neg[:, :], zero[:, :], m, ALU.subtract).then_inc(own, 1)
                    pool.wait_ge(own, base + 1)
                    pool.tensor_tensor(by[:, :, 0:1], as3(neg[:, :]), as3(zero[:, :]), ALU.add).then_inc(own, 1)
                    pool.wait_ge(own, base + 2)
                    pool.tensor_tensor(as3(rem[:, :]), as3(neg[:, :]), by[:, :, 0:1], ALU.subtract).then_inc(own, 1)
                    pool.wait_ge(own, base + 3)
                    pool.tensor_tensor(by[:, :, 1:2], as3(rem[:, :]), as3(zero[:, :]), ALU.add).then_inc(own, 1)
                    pool.wait_ge(own, base + 4)
                    pool.tensor_tensor(by[:, :, 2:3], as3(rem[:, :]), by[:, :, 1:2], ALU.subtract).then_inc(split, 1)

            over_groups(pool, splits)

        @block.tensor
        def _(pe):
            pe.wait_ge(set_up, (NU + 1) * 16)

            def score(i, v, n):
                j, t, half, u = n // (2 * TB), n % (2 * TB) // 2, n % 2, v % NU
                if n == 0:
                    pe.wait_ge(in_k[u], i * N_IN + (v // NU + 1) * N_IN)
                need(pe, maxed, i, v, UNITS, n - 1)
                pe.matmul(ps_s[:, (n % 2) * CHUNK:(n % 2 + 1) * CHUNK], qs[u][0:QROWS, j * S + t * P:j * S + (t + 1) * P],
                          ks[u][0:QROWS, j * S + half * CHUNK:j * S + (half + 1) * CHUNK],
                          start=True, stop=True).then_inc(scored, 1)

            def turn_rows(i, v, j):
                need(pe, split, i, v, GH, j + 1)
                need(pe, rows_copied, i, v, GH, j)
                for t in range(TB):
                    last = pe.transpose(ps_mb[QROWS:ROWS, t * P:(t + 1) * P],
                                        mp[:, (j * TB + t) * MROWS:(j * TB + t + 1) * MROWS], identb[:, :])
                last.then_inc(rows_turned, 1)

            def key_scores(i, v, s, pair):
                half, kt, u = s // TB, s % TB, v % NU
                need(pe, exp_done, i, v, 2 * STEPS, 2 * s + pair - 1)
                for j in (2 * pair, 2 * pair + 1):
                    last = pe.matmul(ps_k[:, j * CHUNK:(j + 1) * CHUNK], ks[u][:, j * S + kt * P:j * S + (kt + 1) * P],
                                     qs[u][:, j * S + half * CHUNK:j * S + (half + 1) * CHUNK], start=True, stop=True)
                last.then_inc(keyed, 1)

            def values(i, v, s):
                half, kt, u = s // TB, s % TB, v % NU
                need(pe, exp_done, i, v, 2 * STEPS, 2 * s + 2)
                if kt == 0:
                    need(pe, pv_copied, i, v, 2, half)
                for j in range(GH):
                    last = pe.matmul(ps_v[32 * j:32 * j + 32, :], vs[u][:, kt * P + 32 * j:kt * P + 32 * j + 32],
                                     ex[:, (s % 2) * GH * CHUNK + j * CHUNK:(s % 2) * GH * CHUNK + (j + 1) * CHUNK],
                                     start=(kt == 0), stop=(kt == TB - 1), skip_group_check=True)
                last.then_inc(pv_done, 1)

            def turn_ctx(i, v, half):
                need(pe, pv_copied, i, v, 2, half + 1)
                need(pe, ctx_read, i, v, 2, half)
                for t in range(CHUNK // P):
                    last = pe.transpose(ps_m[:, t * P:(t + 1) * P], raw[:, t * P:(t + 1) * P], st["ident"][:, :])
                last.then_inc(ctx_turned, 1)

            for n in range(UNITS):
                score(0, 0, n)
                if n % (2 * TB) == 8 and n >= 2 * TB:
                    turn_rows(0, 0, n // (2 * TB) - 1)
            turn_rows(0, 0, GH - 1)

            def group(i, v):
                for s in range(STEPS):
                    more = [] if is_last(i, v) else list(range(FROM[s], FROM[s + 1]))
                    if s == 0:
                        need(pe, rows_copied, i, v, GH, 2)
                    for n in more[:1]:
                        score(i, v + 1, n)
                    key_scores(i, v, s, 0)
                    for n in more[1:-2]:
                        score(i, v + 1, n)
                    if s == 0:
                        need(pe, rows_copied, i, v, GH, GH)
                    key_scores(i, v, s, 1)
                    for n in more[-2:] if len(more) > 2 else more[1:]:
                        score(i, v + 1, n)
                    if s > 0:
                        values(i, v, s - 1)
                    elif not is_first(i, v):
                        values(i, v - 1, STEPS - 1)
                    if s == 2 and not is_first(i, v):
                        turn_ctx(i, v - 1, 1)
                    if s in TURN_ROWS and not is_last(i, v):
                        if s == 5:
                            need(pe, ctx_read, i, v, 2, 0)
                        if s == 12:
                            need(pe, ctx_read, i, v, 2, 1)
                        turn_rows(i, v + 1, TURN_ROWS[s])
                    if s == 10:
                        if not is_last(i, v):
                            need(pe, rows_copied, i, v, GH, GH + 2)
                        turn_ctx(i, v, 0)

            over_groups(pe, group)
            values(LOOPS, NU, STEPS - 1)
            pe.wait_ge(ctx_read, 2 * GROUPS - 1)
            turn_ctx(LOOPS, NU, 1)

        @block.scalar
        def _(act):
            def copy_rows(i, v, j):
                u = v % NU
                need(act, rows_turned, i, v, GH, j + 1)
                act.activation(qs[u][QROWS:ROWS, j * S:(j + 1) * S], ps_mb[QROWS:ROWS, :], ACT.Copy).then_inc(rows_copied, 1)

            def exps(i, v, s, pair):
                need(act, keyed, i, v, 2 * STEPS, 2 * s + pair + 1)
                need(act, pv_done, i, v, STEPS, s - 1)
                at = (s % 2) * GH * CHUNK + pair * 2 * CHUNK
                act.activation(ex[:, at:at + 2 * CHUNK], ps_k[:, pair * 2 * CHUNK:(pair + 1) * 2 * CHUNK],
                               ACT.Exp).then_inc(exp_done, 1)

            def copy_ctx(i, v, half):
                need(act, pv_done, i, v, STEPS, (half + 1) * TB)
                need(act, ctx_turned, i, v, 2, half)
                act.activation(raw[:, :], ps_v[:, :], ACT.Copy).then_inc(pv_copied, 1)

            for j in range(GH):
                copy_rows(0, 0, j)

            def group(i, v):
                for s in range(STEPS):
                    exps(i, v, s, 0)
                    exps(i, v, s, 1)
                    if s == 0 and not is_first(i, v):
                        copy_ctx(i, v - 1, 1)
                    if s == TB:
                        copy_ctx(i, v, 0)
                    if s in TURN_ROWS and not is_last(i, v):
                        copy_rows(i, v + 1, TURN_ROWS[s])

            over_groups(act, group)
            copy_ctx(LOOPS, NU, 1)

        @block.vector
        def _(dve):
            def largest(i, v, n):
                j, t, half = n // (2 * TB), n % (2 * TB) // 2, n % 2
                if n % (2 * TB) == 0:
                    need(dve, split, i, v, GH, j + 1 - GH)
                need(dve, scored, i, v, UNITS, n + 1)
                at = (j * TB + t) * NB + half * 2
                dve.tensor_reduce(mx[:, at:at + 2], ps_s[:, (n % 2) * CHUNK:(n % 2 + 1) * CHUNK]
                                  .rearrange("p (k c) -> p k c", c=KEYS), AX_X, ALU.max).then_inc(maxed, 1)

            def divide(i, v, half):
                need(dve, ctx_turned, i, v, 2, half + 1)
                need(dve, ctx_read, i, v, 2, half)
                strips = ps_m[:, :].rearrange("p (t j c) -> p (t j) c", j=GH, c=32)
                dve.reciprocal(den[:, :].unsqueeze(2), strips[:, :, HD:HD + 1]).then_inc(den_ready, 1)
                need(dve, den_ready, i, v, 2, half + 1)
                at = i * (NU * TB * GCH) + (v * TB + half * TB // 2) * GCH
                dve.tensor_tensor(ctx_all[:, ds(at, CHUNK // P * GCH)].rearrange("p (t c) -> p t c", c=HD),
                                  strips[:, :, 0:HD], den[:, :].unsqueeze(2).to_broadcast([P, GH * GH, HD]),
                                  ALU.mult).then_inc(ctx_read, 1)

            for n in range(UNITS):
                largest(0, 0, n)

            def group(i, v):
                for s in range(STEPS):
                    if not is_last(i, v):
                        for n in range(FROM[s], FROM[s + 1]):
                            largest(i, v + 1, n)
                    if s == 2 and not is_first(i, v):
                        divide(i, v - 1, 1)
                    if s == 10:
                        divide(i, v, 0)

            over_groups(dve, group)
            divide(LOOPS, NU, 1)
            dve.wait_ge(ctx_read, 2 * GROUPS)


def attention_out(nc, st, wo):
    h, ident, ctx_all = (st[x] for x in ("h", "ident", "ctx_all"))
    with ExitStack() as ctx:
        sb, pb, sem = allocators(nc, ctx)
        w_sb = sb("ao_w", [P, C * D], F32)
        stage = sb("ao_stage", [P, TB * D], F32)
        ct = sb("ao_ct", [P, C * S], F32)
        ps_t = pb("ao_pt", [P, 4 * CHUNK], F32)
        ps_o = pb("ao_po", [P, 2 * CHUNK], F32)
        w_in = sem("ao_w_in")
        staged = sem("ao_staged")
        turned = sem("ao_turned")
        ct_ready = sem("ao_ct_ready")
        out_ready = sem("ao_out_ready")
        added = sem("ao_added")
        block = ctx.enter_context(nc.Block())
        Q = C * NC
        G = GROUPS // B

        @block.sync
        def _(sp):
            sp.dma_start(w_sb[:, :].rearrange("p (c n) -> p c n", c=C), wo.rearrange("(c p) n -> p c n", p=P)).then_inc(w_in, 16)

        @block.tensor
        def _(pe):
            pe.wait_ge(w_in, 16)
            with pe.Fori(0, B) as b:
                pe.wait_ge(staged, b + 1)
                for q in range(Q):
                    c, half = q // NC, q % NC
                    for j in range(TB // NC):
                        n = half * (TB // NC) + j
                        last = pe.transpose(ps_t[:, q * CHUNK + j * P:q * CHUNK + (j + 1) * P],
                                            stage[:, n * D + c * P:n * D + (c + 1) * P], ident[:, :])
                    last.then_inc(turned, 1)
                pe.wait_ge(ct_ready, (b + 1) * Q)
                for g in range(TB // 2):
                    if g >= 2:
                        pe.wait_ge(added, b * (TB // 2) + g - 1)
                    for j in range(2):
                        n = 2 * g + j
                        for c in range(C):
                            last = pe.matmul(ps_o[:, (g % 2) * CHUNK + j * D:(g % 2) * CHUNK + (j + 1) * D],
                                             ct[:, c * S + n * P:c * S + (n + 1) * P], w_sb[:, c * D:(c + 1) * D],
                                             start=(c == 0), stop=(c == C - 1))
                    last.then_inc(out_ready, 1)

        @block.scalar
        def _(act):
            with act.Fori(0, B) as b:
                for q in range(Q):
                    c, half = q // NC, q % NC
                    act.wait_ge(turned, b * Q + q + 1)
                    act.activation(ct[:, c * S + half * CHUNK:c * S + (half + 1) * CHUNK],
                                   ps_t[:, q * CHUNK:(q + 1) * CHUNK], ACT.Copy).then_inc(ct_ready, 1)
                act.wait_ge(out_ready, (b + 1) * (TB // 2))

        @block.vector
        def _(dve):
            with dve.Fori(0, B) as b:
                for g in range(G):
                    last = dve.tensor_copy(stage[:, :].rearrange("p (n g c) -> p n g c", g=G, c=GCH)[:, :, g, :],
                                           ctx_all[:, ds((b * G + g) * TB * GCH, TB * GCH)].rearrange("p (n c) -> p n c", c=GCH))
                last.then_inc(staged, 1)
                for g in range(TB // 2):
                    dve.wait_ge(out_ready, b * (TB // 2) + g + 1)
                    hg = h[:, ds((b * TB + 2 * g) * D, 2 * D)]
                    dve.tensor_tensor(hg, hg, ps_o[:, (g % 2) * CHUNK:(g % 2 + 1) * CHUNK], ALU.add).then_inc(added, 1)
            dve.wait_ge(added, B * TB // 2)


CAP = T // E
BITS = 30


def dispatch_capacity(nc, st):
    logits, gates = st["logits"], st["gates"]
    with ExitStack() as ctx:
        sb, pb, sem = allocators(nc, ctx)
        t = routing_tables(sb, "d1", st)
        W = NT * E
        new = lambda name, n, dt=F32: sb("d1_" + name, [P, n], dt)[:, :]
        probs, cmp, sel, eq, onehot, vals = (new(x, W) for x in ("probs", "cmp", "sel", "eq", "onehot", "vals"))
        top, total, cmax = (new(x, NT) for x in ("top", "sum", "cmax"))
        counts, need, keep_f = (new(x, E) for x in ("counts", "need", "keepf"))
        level, trial, keep = (new(x, E, I32) for x in ("level", "trial", "keep"))
        bits_i = new("bits_i", BITS, I32)
        ps_rank = pb("d1_ps", [P, 2 * W], F32)
        ps_cnt = pb("d1_pc", [P, CHUNK], F32)
        own = sem("d1_own")
        shifted = sem("d1_shifted")
        exp_ready = sem("d1_exp_ready")
        counted = sem("d1_counted")
        summed = sem("d1_summed")
        eq_ready = sem("d1_eq_ready")
        ranked = sem("d1_ranked")
        block = ctx.enter_context(nc.Block())
        by = lambda a: a.rearrange("p (n e) -> p n e", e=E)
        over_tiles = lambda a: a.rearrange("p (n e) -> p e n", e=E)
        per_e = lambda a: a.unsqueeze(1).to_broadcast([P, NT, E])
        per_n = lambda a: a.unsqueeze(2).to_broadcast([P, NT, E])
        UNROLL = 5
        BIT_STEPS = 5

        @block.tensor
        def _(pe):
            with pe.Fori(0, BITS // UNROLL) as i:
                for k in range(UNROLL):
                    pe.wait_ge(counted, i * UNROLL + k + 1)
                    pe.matmul(ps_cnt[:, 0:E], st["ones"][:, :], counts, start=True, stop=True).then_inc(summed, 1)
            pe.wait_ge(counted, BITS + 1)
            pe.matmul(ps_cnt[:, 0:E], st["ones"][:, :], counts, start=True, stop=True).then_inc(summed, 1)
            for k in range(2):
                pe.wait_ge(eq_ready, k + 1)
                src = eq if k == 0 else onehot
                pe.matmul(ps_rank[:, 0:W], st["before"][:, :], src, start=True, stop=True)
                pe.matmul(ps_rank[:, W:2 * W], st["ones"][:, :], src, start=True, stop=True).then_inc(ranked, 1)

        @block.scalar
        def _(act):
            act.wait_ge(shifted, 1)
            act.activation(vals, vals, ACT.Exp).then_inc(exp_ready, 1)

        @block.vector
        def _(dve):
            s = Steps(dve, own)
            s.step(dve.tensor_reduce(top, by(logits[:, :]), AX_X, ALU.max))
            dve.tensor_tensor(by(vals), by(logits[:, :]), per_n(top), ALU.subtract).then_inc(shifted, 1)
            s.step(dve.memset(level, 0))
            s.step(dve.tensor_copy(bits_i, st["bits"][:, :]))
            dve.wait_ge(exp_ready, 1)
            s.step(dve.tensor_reduce(total, by(vals), AX_X, ALU.add))
            s.step(dve.reciprocal(cmax, total))
            s.step(dve.tensor_tensor(by(probs), by(vals), per_n(cmax), ALU.mult))
            before = s.n
            with dve.Fori(0, BITS // UNROLL) as i:
                s = Steps(dve, own, i * (UNROLL * BIT_STEPS) + before)
                for k in range(UNROLL):
                    b = i * UNROLL + k
                    s.step(dve.tensor_tensor(trial, level, bits_i[:, ds(b, 1)].to_broadcast([P, E]), ALU.bitwise_or))
                    s.step(dve.tensor_tensor(by(cmp), by(probs), per_e(trial.bitcast(F32)), ALU.is_ge))
                    dve.tensor_reduce(counts, over_tiles(cmp), AX_X, ALU.add).then_inc(counted, 1)
                    dve.wait_ge(summed, b + 1)
                    s.step(dve.tensor_scalar(keep_f, ps_cnt[:, 0:E], CAP - 0.5, None, ALU.is_ge))
                    s.step(dve.tensor_tensor(keep, keep_f, st["bits"][:, ds(b, 1)].to_broadcast([P, E]), ALU.mult))
                    s.step(dve.tensor_tensor(level, level, keep, ALU.bitwise_or))
                assert s.n == UNROLL * BIT_STEPS
            s = Steps(dve, own, before + BITS * BIT_STEPS)
            level_f = level.bitcast(F32)
            s.step(dve.tensor_tensor(by(sel), by(probs), per_e(level_f), ALU.is_gt))
            dve.tensor_reduce(counts, over_tiles(sel), AX_X, ALU.add).then_inc(counted, 1)
            dve.tensor_tensor(by(eq), by(probs), per_e(level_f), ALU.is_equal).then_inc(eq_ready, 1)
            dve.wait_ge(summed, BITS + 1)
            s.step(dve.tensor_scalar(need, ps_cnt[:, 0:E], -1.0, float(CAP), ALU.mult, ALU.add))
            dve.wait_ge(ranked, 1)
            s.mark(dve.tensor_copy(t["rank"], ps_rank[:, 0:W]))
            s.step(dve.tensor_copy(t["total"], ps_rank[:, W:2 * W]))
            for e in range(E):
                s.mark(dve.tensor_tensor_scan(t["incl"][:, e::E], t["one"].to_broadcast([P, NT]), t["total"][:, e::E],
                                              0.0, ALU.mult, ALU.add))
            s.wait()
            s.step(dve.tensor_tensor(t["rank"], t["rank"], t["incl"], ALU.add))
            s.step(dve.tensor_tensor(t["rank"], t["rank"], t["total"], ALU.subtract))
            s.step(dve.tensor_tensor(by(cmp), by(t["rank"]), per_e(need), ALU.is_lt))
            dve.wait_ge(eq_ready, 1)
            s.step(dve.tensor_tensor(cmp, cmp, eq, ALU.mult))
            s.step(dve.tensor_tensor(sel, sel, cmp, ALU.add))
            s.step(dve.tensor_reduce(top, by(sel), AX_X, ALU.max))
            s.step(dve.tensor_scalar(top, top, -1.0, 1.0, ALU.mult, ALU.add))
            s.step(dve.tensor_tensor(by(sel), by(sel), per_n(top), ALU.max))
            s.step(dve.tensor_tensor(cmp, probs, sel, ALU.mult))
            s.step(dve.scalar_tensor_tensor(out=vals, in0=sel, scalar=-1.0, in1=cmp, op0=ALU.add, op1=ALU.add))
            first_of_max(dve, s, by(vals), top, by(cmp), st["rev"][:, :], cmax, by(onehot))
            dve.nop().then_inc(eq_ready, 1)
            s.step(dve.tensor_tensor(cmp, probs, onehot, ALU.mult))
            s.step(dve.tensor_reduce(gates[:, 0:NT], by(cmp), AX_X, ALU.add))
            dve.wait_ge(ranked, 2)
            slots_of(dve, s, t, onehot, ps_rank, T // P + E)
            s.step(dve.tensor_tensor(onehot, onehot, t["rank"], ALU.mult))
            s.step(dve.tensor_reduce(st["pos"][:, 0:NT], by(onehot), AX_X, ALU.add))


CONSTS = (("before", P), ("ones", P), ("rev", E), ("starts", 2 * NT + E), ("bits", BITS), ("count", P),
          ("number", 2 * NT), ("slot_number", 2 * NT + E))


def set_up(nc, st, a):
    with ExitStack() as ctx:
        sb, pb, sem = allocators(nc, ctx)
        const_in = sem("su_const_in")
        block = ctx.enter_context(nc.Block())

        @block.sync
        def _(sp):
            for name, _ in CONSTS:
                sp.dma_start(st[name][:, :], a["c_" + name]).then_inc(const_in, 16)
            sp.wait_ge(const_in, 16 * len(CONSTS))


def tower(nc, a, out):
    TILES0, TILES1 = 2 * NT + E, NT + E
    xn0, xn1 = (nc.dram_tensor(n, [T, D], F32).ap() for n in ("xn0", "xn1"))
    y0 = nc.dram_tensor("y0", [2 * T + TILES0 * P, D], F32).ap()
    y1 = nc.dram_tensor("y1", [T + TILES1 * P, D], F32).ap()
    qk_dram = nc.dram_tensor("qk_groups", [GROUPS, 2, PARTS, GCH, S], BF16).ap()
    v_dram = nc.dram_tensor("v_groups", [GROUPS, S, P], F32).ap()
    with ExitStack() as ctx:
        sb, pb, sem = allocators(nc, ctx)
        st = {"h": sb("h", [P, NT * D], F32), "ident": sb("ident", [P, P], F32), "mv": sb("mv", [P, 2 * NT], F32),
              "rstd": sb("rstd", [P, NT], F32), "logits": sb("logits", [P, NT * E], F32),
              "gates": sb("gates", [P, 2 * NT], F32), "pos": sb("pos", [P, 2 * NT], F32), "slot_rows": sb("slot_rows", [P, 2 * TILES0], I32),
              "tile_ei": sb("tile_ei", [P, 2 * NT + E], I32)}
        for name, n in CONSTS:
            st[name] = sb(name, [P, n], F32)
        experts0_in = sem("experts0_in")
        experts1_in = sem("experts1_in")

        set_up(nc, st, a)
        embed(nc, st, a["tok"], a["L0_tok_emb"], a["c_pos"], a["L0_tok_alpha"], a["L0_tok_beta"])
        layer_norm(nc, st, "n0")
        rwkv(nc, st, *(a["L0_attn_" + n] for n in ("W", "U", "time_mix_k", "time_mix_v", "time_mix_r", "Wk", "Wv", "Wr", "Wo")))
        with ExitStack() as moe:
            for n in ("w1_sb", "w2_sb"):
                st[n] = moe.enter_context(nc.sbuf_tensor("l0_" + n, [P, E * C * HID], F32))
            route(nc, st, "g0", a["L0_ffn_Wr"], a["L0_ffn_br"], xn0, a["L0_ffn_W1"], a["L0_ffn_W2"], experts0_in)
            dispatch_top2(nc, st)
            slot_table(nc, st, "s0", 2, TILES0)
            experts(nc, st, "x0", TILES0, xn0, y0, a["L0_ffn_b1"], a["L0_ffn_b2"], ACT.Relu, experts0_in)
        combine(nc, st, "c0", 2, y0)
        layer_norm(nc, st, "n2")
        with nc.sbuf_tensor("ctx_all", [P, NT * D], F32) as st["ctx_all"]:
            project_qkv(nc, st, a["L1_attn_w_q"], a["L1_attn_w_k"], a["L1_attn_w_v"], a["c_v_ones"], qk_dram, v_dram)
            attention(nc, st, qk_dram, v_dram, a["c_block_rows"], a["c_ident_bits"])
            attention_out(nc, st, a["L1_attn_w_o"])
        with ExitStack() as moe:
            for n in ("w1_sb", "w2_sb"):
                st[n] = moe.enter_context(nc.sbuf_tensor("l1_" + n, [P, E * C * HID], F32))
            route(nc, st, "g1", a["L1_ffn_Wg"], None, xn1, a["L1_ffn_W1"], a["L1_ffn_W2"], experts1_in)
            dispatch_capacity(nc, st)
            slot_table(nc, st, "s1", 1, TILES1)
            experts(nc, st, "x1", TILES1, xn1, y1, None, None, ACT.Gelu, experts1_in)
        combine(nc, st, "c1", 1, y1, out)


def shape_constants():
    position = np.arange(S, dtype=np.float32)[:, None]
    step = np.arange(0, D, 2, dtype=np.float32) * np.float32(-np.log(10000.0) / D)
    angle = (position * np.exp(step.astype(np.float64)).astype(np.float32)).astype(np.float64)
    BF16_ONE = 0x3F80
    rows = np.zeros((MROWS, GH, S), np.uint16)
    for k in range(NB):
        rows[k * PARTS:(k + 1) * PARTS, :, k * KEYS:(k + 1) * KEYS] = BF16_ONE
    ones = np.zeros((HEADS, 32), np.float32)
    ones[:, HD] = 1.0
    spread = lambda v: np.ascontiguousarray(np.broadcast_to(v.astype(np.float32), (P, v.size)))
    return {
        "c_pos": np.stack([np.sin(angle), np.cos(angle)], axis=-1).reshape(S, D).astype(np.float32),
        "c_before": np.triu(np.ones((P, P), np.float32), 1),
        "c_ones": np.ones((P, P), np.float32),
        "c_rev": spread(E - np.arange(E)),
        "c_starts": spread(P * np.arange(2 * NT + E)),
        "c_count": spread(np.arange(P)),
        "c_number": (1.0 + np.arange(2 * T).reshape(2 * NT, P).T).astype(np.float32),
        "c_slot_number": np.arange((2 * NT + E) * P).reshape(2 * NT + E, P).T.astype(np.float32),
        "c_bits": spread(2.0 ** np.arange(BITS - 1, -1, -1)),
        "c_block_rows": rows.reshape(MROWS, GH * S),
        "c_ident_bits": np.eye(P, dtype=np.uint16) * np.uint16(BF16_ONE),
        "c_v_ones": ones.reshape(-1),
    }


def laid_out(inputs):
    a = {n: np.ascontiguousarray(v) for n, v in inputs.items() if n != "x"}
    a["tok"] = np.ascontiguousarray(inputs["x"].reshape(NT, P).T)
    for n in ("Wk", "Wv", "Wr", "Wo"):
        a["L0_attn_" + n] = np.ascontiguousarray(a["L0_attn_" + n].T)
    for n in ("W", "U", "time_mix_k", "time_mix_v", "time_mix_r"):
        a["L0_attn_" + n] = np.ascontiguousarray(a["L0_attn_" + n].reshape(C, P).T)
    a["L0_ffn_b1"] = np.ascontiguousarray(a["L0_ffn_b1"].reshape(E * HC, P).T)
    return a


def kernel(**inputs):
    import concourse.bacc as bacc
    from concourse.bass_utils import run_bass_kernel_spmd

    nc = bacc.Bacc("TRN2", target_bir_lowering=False, num_devices=1)
    arrays = {**laid_out({n: np.asarray(v) for n, v in inputs.items()}), **shape_constants()}
    a = {n: nc.dram_tensor("in_" + n, list(v.shape), mybir.dt.from_np(v.dtype), kind="ExternalInput").ap()
         for n, v in arrays.items()}
    out = nc.dram_tensor("out_h", [B, S, D], F32, kind="ExternalOutput").ap()
    tower(nc, a, out)
    r = run_bass_kernel_spmd(nc, [{"in_" + n: v for n, v in arrays.items()}], core_ids=[0])
    return r.results[0]["out_h"]
```

```python
from contextlib import ExitStack

import concourse.bass as bass
import numpy as np
from concourse import mybir

F32 = mybir.dt.float32
BF16 = mybir.dt.bfloat16
I32 = mybir.dt.int32
U16 = mybir.dt.uint16
ALU = mybir.AluOpType
ACT = mybir.ActivationFunctionType
AX_X = mybir.AxisListType.X

P = 128
B, S, D = 4, 1024, 256
T = B * S
NT = T // P
TB = S // P
C = D // P
CHUNK = 512
NC = S // CHUNK
E = 8
HID = 512
HC = HID // P
FAR = -1e38
LN_EPS = 1e-5
ds = bass.ds


def allocators(nc, ctx):
    sems = []

    def sem(name):
        sems.append(nc.alloc_semaphore(name))
        return sems[-1]

    def clear():
        nc.clear_and_free_semaphores(sems)
        nc.all_engine_barrier()

    ctx.callback(clear)
    return (lambda name, shape, dt: ctx.enter_context(nc.sbuf_tensor(name, shape, dt)),
            lambda name, shape, dt: ctx.enter_context(nc.psum_tensor(name, shape, dt)), sem)


def need(eng, s, count):
    if isinstance(count, int) and count <= 0:
        return
    eng.wait_ge(s, count)


def over_sequences(eng, sequence):
    sequence(0)
    with eng.Fori(1, B) as b:
        sequence(b)


class Steps:

    def __init__(self, eng, sem, base=0):
        self.eng, self.sem, self.base, self.n = eng, sem, base, 0

    def mark(self, ins):
        ins.then_inc(self.sem, 1)
        self.n += 1
        return self.n

    def wait(self, n=None):
        self.eng.wait_ge(self.sem, self.base + (self.n if n is None else n))

    def step(self, ins):
        self.mark(ins)
        self.wait()


def embed(nc, st, tok_ids, emb, pos, alpha, beta, constants):
    h, ident, mv, rstd = st["h"], st["ident"], st["mv"], st["rstd"]
    with ExitStack() as ctx:
        sb, pb, sem = allocators(nc, ctx)
        tok_idx = sb("em_tok_idx", [P, NT], I32)
        pos_sb = sb("em_pos", [P, TB * D], F32)
        alpha_all = sb("em_alpha", [P, D], F32)
        beta_all = sb("em_beta", [P, D], F32)
        stats = sb("em_stats", [P, NT * 6], F32)
        y_mv = sb("em_mv", [P, NT * 2], F32)
        dev = sb("em_dev", [P, NT], F32)
        rec = sb("em_rec", [P, NT], F32)
        var = sb("em_var", [P, NT], F32)
        idx_in = sem("em_idx_in")
        const_in = sem("em_const_in")
        later_in = sem("em_later_in")
        rows_in = [sem(f"em_rows_in{b}") for b in range(B)]
        own = sem("em_own")
        ident_made = sem("em_ident")
        mv_ready = sem("em_mv_ready")
        dev_ready = sem("em_dev_ready")
        shifted = sem("em_shifted")
        h_ready = sem("em_h_ready")
        var_ready = sem("em_var_ready")
        h_dev_ready = sem("em_h_dev_ready")
        block = ctx.enter_context(nc.Block())

        def sequence(b):
            return h[:, b * TB * D:(b + 1) * TB * D]

        def tiles(a):
            return a.rearrange("p (n d) -> p n d", d=D)

        def for_all(v):
            return v[:, :].unsqueeze(1).to_broadcast([P, TB, D])

        @block.sync
        def _(sp):
            sp.dma_start(tok_idx[:, :], tok_ids).then_inc(idx_in, 16)
            sp.dma_start(tiles(pos_sb[:, :]), pos.rearrange("(n p) d -> p n d", p=P)).then_inc(const_in, 16)
            sp.dma_start(alpha_all[:, :], alpha.partition_broadcast(P)).then_inc(const_in, 16)
            sp.dma_start(beta_all[:, :], beta.partition_broadcast(P)).then_inc(const_in, 16)
            for name, values in constants:
                sp.dma_start(st[name][:, :], values).then_inc(later_in, 16)
            sp.wait_ge(later_in, 16 * len(constants))

        @block.gpsimd
        def _(pool):
            pool.wait_ge(idx_in, 16)
            for n in range(NT):
                pool.indirect_dma_start(out=h[:, n * D:(n + 1) * D], out_offset=None, in_=emb,
                                        in_offset=bass.IndirectOffsetOnAxis(ap=tok_idx[:, n:n + 1], axis=0),
                                        ).then_inc(rows_in[n // TB], 16)
            pool.memset(ident[:, :], 0.0).then_inc(ident_made, 1)
            pool.wait_ge(ident_made, 1)
            pool.affine_select(out=ident[:, :], in_=ident[:, :], compare_op=ALU.not_equal, fill=1.0, base=0,
                               pattern=[[-1, P]], channel_multiplier=1).then_inc(ident_made, 1)
            for b in range(B):
                pool.wait_ge(shifted, b + 1)
                pool.tensor_tensor(tiles(sequence(b)), tiles(sequence(b)), for_all(alpha_all), ALU.mult).then_inc(h_ready, 1)
            pool.wait_ge(ident_made, 2)

        @block.scalar
        def _(act):
            for b in range(B):
                act.wait_ge(mv_ready, b + 1)
                act.activation(dev[:, b * TB:(b + 1) * TB], y_mv[:, 2 * b * TB + 1:2 * (b + 1) * TB:2], ACT.Sqrt,
                               scale=D / (D - 1.0)).then_inc(dev_ready, 1)
            act.wait_ge(var_ready, 1)
            act.activation(dev[:, :], var[:, :], ACT.Sqrt).then_inc(h_dev_ready, 1)

        @block.vector
        def _(dve):
            s = Steps(dve, own)

            def statistics(b, to):
                for n in range(b * TB, (b + 1) * TB):
                    last = dve.bn_stats(stats[:, n * 6:(n + 1) * 6], h[:, n * D:(n + 1) * D])
                s.step(last)
                for n in range(b * TB, (b + 1) * TB):
                    last = dve.bn_aggr(to[:, n * 2:(n + 1) * 2], stats[:, n * 6:(n + 1) * 6])
                return last

            def place(b):
                dve.wait_ge(rows_in[b], 16 * TB)
                s.step(dve.tensor_tensor(sequence(b), sequence(b), pos_sb[:, :], ALU.add))
                statistics(b, y_mv).then_inc(mv_ready, 1)

            def standardise(b):
                dve.wait_ge(dev_ready, b + 1)
                cols = slice(b * TB, (b + 1) * TB)
                s.step(dve.tensor_scalar_add(rec[:, cols], dev[:, cols], 1e-6))
                s.step(dve.reciprocal(rec[:, cols], rec[:, cols]))
                for n in range(b * TB, (b + 1) * TB):
                    hn = h[:, n * D:(n + 1) * D]
                    last = dve.tensor_scalar(hn, hn, y_mv[:, n * 2:n * 2 + 1], rec[:, n:n + 1], ALU.subtract, ALU.mult)
                s.step(last)
                dve.tensor_tensor(tiles(sequence(b)), tiles(sequence(b)), for_all(beta_all), ALU.add).then_inc(shifted, 1)

            dve.wait_ge(const_in, 48)
            place(0)
            for b in range(B):
                if b < B - 1:
                    place(b + 1)
                dve.wait_ge(mv_ready, b + 1)
                standardise(b)
            for b in range(B):
                dve.wait_ge(h_ready, b + 1)
                s.step(statistics(b, mv))
            dve.tensor_scalar_add(var[:, :], mv[:, 1::2], LN_EPS).then_inc(var_ready, 1)
            dve.wait_ge(h_dev_ready, 1)
            s.step(dve.reciprocal(rstd[:, :], dev[:, :]))


def rwkv(nc, st, decay, bonus, mix_k, mix_v, mix_r, wk, wv, wr, wo):
    h, mv, rstd, ident = st["h"], st["mv"], st["rstd"], st["ident"]
    with ExitStack() as ctx:
        sb, pb, sem = allocators(nc, ctx)
        w_sb = sb("rw_w", [P, 4 * C * D], F32)
        cols = sb("rw_cols", [P, 5 * C], F32)
        neg_w = sb("rw_nw", [P, C], F32)
        xn = sb("rw_xn", [P, TB * D], F32)
        xt = sb("rw_xt", [P, C * (S + 1)], F32)
        dif = sb("rw_dif", [P, C * S], F32)
        mix = sb("rw_mix", [P, 3 * C * S], F32)
        kvr = sb("rw_kvr", [P, 3 * C * S], F32)
        run_max = sb("rw_max", [P, S + 1], F32)
        aa = sb("rw_aa", [P, S + 1], F32)
        bb = sb("rw_bb", [P, S + 1], F32)
        expo = sb("rw_f", [P, 4 * S], F32)
        ex = sb("rw_e", [P, 4 * S], F32)
        tmp = sb("rw_t", [P, 3 * S], F32)
        numer = sb("rw_numer", [P, 2 * S], F32)
        gated = sb("rw_out", [P, C * S], F32)
        ps_t = pb("rw_pt", [P, 2 * CHUNK], F32)
        ps_p = pb("rw_pp", [P, 2 * CHUNK], F32)
        ps_o = pb("rw_po", [P, 4 * CHUNK], F32)
        w_in = sem("rw_in")
        zeroed = sem("rw_zero")
        decay_ready = sem("rw_decay")
        own = sem("rw_own")
        xn_ready = sem("rw_xn_ready")
        turned = sem("rw_turned")
        xt_ready = sem("rw_xt_ready")
        dif_ready = sem("rw_dif_ready")
        mix_ready = sem("rw_mix_ready")
        projected = sem("rw_proj")
        kvr_ready = sem("rw_kvr_ready")
        max_ready = sem("rw_max_ready")
        new_ready = sem("rw_new_arg")
        arg_ready = sem("rw_arg")
        exp_ready = sem("rw_exp")
        relu_ready = sem("rw_relu")
        aa_ready = sem("rw_aa_ready")
        products = sem("rw_products")
        numer_ready = sem("rw_numer_ready")
        gated_ready = sem("rw_gated")
        out_ready = sem("rw_outp")
        added = sem("rw_added")
        block = ctx.enter_context(nc.Block())
        W = C * D
        Q = C * NC
        U = 3 * NC
        G = TB // 2

        def over_turns(eng, turn):
            turn(0, False)
            with eng.Fori(1, B - 1) as b:
                turn(b, False)
            turn(B - 1, True)

        def weight(i, c, lo, n):
            return w_sb[:, i * W + c * D + lo:i * W + c * D + lo + n]

        def col(i, c):
            return cols[:, i * C + c:i * C + c + 1]

        def xt_now(c):
            return xt[:, c * (S + 1) + 1:(c + 1) * (S + 1)]

        def xt_before(c):
            return xt[:, c * (S + 1):(c + 1) * (S + 1) - 1]

        def mixed(i, c, lo=0, n=S):
            return mix[:, (i * C + c) * S + lo:(i * C + c) * S + lo + n]

        def chan(i, d, lo=0, n=S):
            return kvr[:, (i * C + d) * S + lo:(i * C + d) * S + lo + n]

        def row(t, i, n=S):
            return t[:, i * S:i * S + n]

        def wkv_exps(act, b, d):
            at = b * (3 * C) + 3 * d
            act.wait_ge(arg_ready, at + 1)
            act.activation(row(ex, 0), row(expo, 0), ACT.Exp).then_inc(exp_ready, 1)
            act.wait_ge(new_ready, b * C + d + 1)
            act.activation(row(ex, 1), row(expo, 1), ACT.Exp).then_inc(exp_ready, 1)
            act.wait_ge(arg_ready, at + 3)
            act.activation(row(tmp, 2), row(expo, 2), ACT.Relu).then_inc(relu_ready, 1)
            act.wait_ge(relu_ready, b * C + d + 1)
            act.activation(row(ex, 2), row(tmp, 2), ACT.Exp, scale=-1.0).then_inc(exp_ready, 1)
            act.activation(row(ex, 3), row(expo, 3), ACT.Exp).then_inc(exp_ready, 1)

        @block.sync
        def _(sp):
            for i, w in enumerate((wk, wv, wr, wo)):
                sp.dma_start(w_sb[:, i * W:(i + 1) * W].rearrange("p (c n) -> p c n", c=C),
                             w.rearrange("(c p) n -> p c n", p=P)).then_inc(w_in, 16)
            for i, v in enumerate((mix_k, mix_v, mix_r, bonus, decay)):
                sp.dma_start(cols[:, i * C:(i + 1) * C], v.rearrange("p c -> p c")).then_inc(w_in, 16)

        @block.gpsimd
        def _(pool):
            for c in range(C):
                pool.memset(xt[:, c * (S + 1):c * (S + 1) + 1], 0.0).then_inc(zeroed, 1)
            pool.memset(run_max[:, 0:1], FAR).then_inc(zeroed, 1)
            pool.memset(aa[:, 0:1], 0.0).then_inc(zeroed, 1)
            pool.memset(bb[:, 0:1], 0.0).then_inc(zeroed, 1)
            pool.wait_ge(zeroed, C + 3)

            def difference(b):
                need(pool, mix_ready, b * 3)
                pool.wait_ge(xt_ready, (b + 1) * Q)
                pool.tensor_tensor(dif[:, 0:S], xt_now(0), xt_before(0), ALU.subtract).then_inc(dif_ready, 1)

            def new_argument(b, d):
                pool.wait_ge(max_ready, b * C + d + 1)
                pool.tensor_tensor(row(expo, 1), chan(0, d), run_max[:, 1:S + 1], ALU.subtract).then_inc(new_ready, 1)

            def numerator(b, d):
                pool.wait_ge(exp_ready, b * (4 * C) + 4 * d + 4)
                pool.tensor_tensor(row(numer, 0), row(ex, 3), chan(1, d), ALU.mult).then_inc(products, 1)
                pool.wait_ge(aa_ready, b * C + d + 1)
                pool.tensor_tensor(row(numer, 1), row(ex, 2), aa[:, 0:S], ALU.mult).then_inc(products, 1)
                need(pool, out_ready, b * G)
                pool.wait_ge(products, b * (2 * C) + 2 * d + 2)
                pool.tensor_tensor(row(gated, d), row(numer, 0), row(numer, 1), ALU.add).then_inc(numer_ready, 1)

            difference(0)

            def turn(b, last):
                new_argument(b, 0)
                numerator(b, 0)
                if not last:
                    difference(b + 1)
                new_argument(b, 1)
                numerator(b, 1)

            over_turns(pool, turn)

        @block.tensor
        def _(pe):
            def turn_in(b):
                pe.wait_ge(xn_ready, b + 1)
                for q in range(Q):
                    c, half = q // NC, q % NC
                    need(pe, xt_ready, b * Q + q - 1)
                    for j in range(TB // NC):
                        n = half * (TB // NC) + j
                        last = pe.transpose(ps_t[:, (q % 2) * CHUNK + j * P:(q % 2) * CHUNK + (j + 1) * P],
                                            xn[:, n * D + c * P:n * D + (c + 1) * P], ident[:, :])
                    last.then_inc(turned, 1)

            def project(b, d):
                for i in range(3):
                    if d == 0:
                        pe.wait_ge(mix_ready, b * 3 + i + 1)
                    for m in range(NC):
                        k = d * U + i * NC + m
                        need(pe, kvr_ready, b * (C * U) + k - 1)
                        for c in range(C):
                            last = pe.matmul(ps_p[:, (k % 2) * CHUNK:(k % 2 + 1) * CHUNK], weight(i, c, d * P, P),
                                             mixed(i, c, m * CHUNK, CHUNK), start=(c == 0), stop=(c == C - 1))
                        last.then_inc(projected, 1)

            def output(b):
                pe.wait_ge(gated_ready, (b + 1) * C)
                for g in range(G):
                    for j in range(2):
                        n = 2 * g + j
                        for d in range(C):
                            last = pe.matmul(ps_o[:, g * CHUNK + j * D:g * CHUNK + (j + 1) * D],
                                             gated[:, d * S + n * P:d * S + (n + 1) * P], weight(3, d, 0, D),
                                             start=(d == 0), stop=(d == C - 1))
                    last.then_inc(out_ready, 1)

            turn_in(0)
            pe.wait_ge(w_in, 16 * 9)
            project(0, 0)

            def turn(b, last):
                if not (isinstance(b, int) and b == 0):
                    output(b - 1)
                if not last:
                    turn_in(b + 1)
                project(b, 1)
                if not last:
                    project(b + 1, 0)

            over_turns(pe, turn)
            output(B - 1)

        @block.scalar
        def _(act):
            act.wait_ge(zeroed, C + 3)

            def take_turned(b):
                need(act, mix_ready, b * 3)
                for q in range(Q):
                    c, half = q // NC, q % NC
                    act.wait_ge(turned, b * Q + q + 1)
                    act.activation(xt[:, c * (S + 1) + 1 + half * CHUNK:c * (S + 1) + 1 + (half + 1) * CHUNK],
                                   ps_t[:, (q % 2) * CHUNK:(q % 2 + 1) * CHUNK], ACT.Copy).then_inc(xt_ready, 1)

            def take_projected(b, d, kinds):
                need(act, gated_ready, (b - 1) * C + d + 1)
                for i in kinds:
                    for m in range(NC):
                        k = d * U + i * NC + m
                        act.wait_ge(projected, b * (C * U) + k + 1)
                        src = ps_p[:, (k % 2) * CHUNK:(k % 2 + 1) * CHUNK]
                        if i < 2:
                            act.activation(chan(i, d, m * CHUNK, CHUNK), src, ACT.Copy).then_inc(kvr_ready, 1)
                        else:
                            act.activation(chan(i, d, m * CHUNK, CHUNK), src, ACT.Exp, scale=-1.0).then_inc(kvr_ready, 1)

            take_turned(0)
            act.wait_ge(w_in, 16 * 9)
            act.activation(neg_w[:, :], cols[:, 4 * C:5 * C], ACT.Exp).then_inc(decay_ready, 1)
            take_projected(0, 0, (0, 1, 2))

            def turn(b, last):
                wkv_exps(act, b, 0)
                if not last:
                    take_turned(b + 1)
                take_projected(b, 1, (0, 1, 2))
                if not last:
                    take_projected(b + 1, 0, (0, 1))
                wkv_exps(act, b, 1)
                if not last:
                    take_projected(b + 1, 0, (2,))

            over_turns(act, turn)

        @block.vector
        def _(dve):
            STEPS = 1 + 7 * C

            def normalise(b):
                for n in range(TB):
                    t = b * TB + n
                    last = dve.tensor_scalar(xn[:, n * D:(n + 1) * D], h[:, ds(t * D, D)], mv[:, ds(t * 2, 1)],
                                             rstd[:, ds(t, 1)], ALU.subtract, ALU.mult)
                last.then_inc(xn_ready, 1)

            def mix_in(s, b):
                dve.wait_ge(xt_ready, (b + 1) * Q)
                s.step(dve.tensor_tensor(dif[:, S:2 * S], xt_now(1), xt_before(1), ALU.subtract))
                dve.wait_ge(dif_ready, b + 1)
                need(dve, projected, b * (C * U))
                for i in range(3):
                    for c in range(C):
                        last = dve.scalar_tensor_tensor(out=mixed(i, c), in0=dif[:, c * S:(c + 1) * S], scalar=col(i, c),
                                                        in1=xt_before(c), op0=ALU.mult, op1=ALU.add)
                    last.then_inc(mix_ready, 1)

            def recurrence(s, b, d):
                k, v, er = chan(0, d), chan(1, d), chan(2, d)
                w1, u1 = neg_w[:, d:d + 1], col(3, d)
                ex_at = b * (4 * C) + 4 * d
                dve.wait_ge(kvr_ready, b * (C * U) + d * U + 2 * NC)
                dve.tensor_tensor_scan(run_max[:, 1:S + 1], w1.to_broadcast([P, S]), k, FAR, ALU.add, ALU.max).then_inc(max_ready, 1)
                dve.wait_ge(max_ready, b * C + d + 1)
                dve.scalar_tensor_tensor(out=row(expo, 0), in0=run_max[:, 0:S], scalar=w1, in1=run_max[:, 1:S + 1],
                                         op0=ALU.add, op1=ALU.subtract).then_inc(arg_ready, 1)
                s.step(dve.scalar_tensor_tensor(out=row(expo, 2), in0=k, scalar=u1, in1=run_max[:, 0:S],
                                                op0=ALU.add, op1=ALU.subtract))
                dve.tensor_scalar_min(row(expo, 3), row(expo, 2), 0.0).then_inc(arg_ready, 2)
                dve.wait_ge(exp_ready, ex_at + 2)
                s.step(dve.tensor_tensor(row(tmp, 0), row(ex, 1), v, ALU.mult))
                dve.tensor_tensor_scan(aa[:, 1:S + 1], row(ex, 0), row(tmp, 0), 0.0, ALU.mult, ALU.add).then_inc(aa_ready, 1)
                s.step(dve.tensor_tensor_scan(bb[:, 1:S + 1], row(ex, 0), row(ex, 1), 0.0, ALU.mult, ALU.add))
                dve.wait_ge(exp_ready, ex_at + 4)
                s.step(dve.tensor_tensor(row(tmp, 1), row(ex, 2), bb[:, 0:S], ALU.mult))
                s.step(dve.tensor_tensor(row(tmp, 1), row(tmp, 1), row(ex, 3), ALU.add))
                dve.wait_ge(kvr_ready, b * (C * U) + (d + 1) * U)
                dve.wait_ge(aa_ready, b * C + d + 1)
                s.step(dve.scalar_tensor_tensor(out=row(tmp, 0), in0=er, scalar=1.0, in1=row(tmp, 1),
                                                op0=ALU.add, op1=ALU.mult))
                s.step(dve.reciprocal(row(tmp, 1), row(tmp, 0)))
                dve.wait_ge(numer_ready, b * C + d + 1)
                dve.tensor_tensor(row(gated, d), row(gated, d), row(tmp, 1), ALU.mult).then_inc(gated_ready, 1)

            def add_output(b):
                for g in range(G):
                    dve.wait_ge(out_ready, b * G + g + 1)
                    hg = h[:, ds((b * TB + 2 * g) * D, 2 * D)]
                    dve.tensor_tensor(hg, hg, ps_o[:, g * CHUNK:(g + 1) * CHUNK], ALU.add).then_inc(added, 1)

            normalise(0)
            dve.wait_ge(zeroed, C + 3)
            dve.wait_ge(decay_ready, 1)
            dve.tensor_scalar_mul(neg_w[:, :], neg_w[:, :], -1.0).then_inc(decay_ready, 1)
            dve.wait_ge(decay_ready, 2)
            mix_in(Steps(dve, own), 0)

            def turn(b, last):
                s = Steps(dve, own, b * STEPS + 1)
                if not last:
                    normalise(b + 1)
                recurrence(s, b, 0)
                if not (isinstance(b, int) and b == 0):
                    add_output(b - 1)
                if not last:
                    mix_in(s, b + 1)
                recurrence(s, b, 1)
                assert last or s.n == STEPS, s.n

            over_turns(dve, turn)
            add_output(B - 1)
            dve.wait_ge(added, B * G)


def first_of_max(dve, s, vals, top, eq, rev, cmax, onehot):
    s.step(dve.tensor_reduce(top, vals, AX_X, ALU.max))
    s.step(dve.tensor_tensor(eq, vals, top.unsqueeze(2).to_broadcast([P, NT, E]), ALU.is_equal))
    s.step(dve.tensor_tensor(eq, eq, rev.unsqueeze(1).to_broadcast([P, NT, E]), ALU.mult))
    s.step(dve.tensor_reduce(cmax, eq, AX_X, ALU.max))
    s.step(dve.tensor_tensor(onehot, eq, cmax.unsqueeze(2).to_broadcast([P, NT, E]), ALU.is_equal))


def slots_of(dve, s, t, ps_rank, n_slot_tiles):
    rank, total = t["rank"], t["total"]
    s.mark(dve.tensor_copy(rank, ps_rank[:, 0:NT * E]))
    s.step(dve.tensor_copy(total, ps_rank[:, NT * E:2 * NT * E]))
    by = lambda a: a.rearrange("p (n e) -> p n e", e=E)
    for e in range(E):
        s.mark(dve.tensor_tensor_scan(t["incl"][:, e::E], t["one"].to_broadcast([P, NT]), total[:, e::E],
                                      0.0, ALU.mult, ALU.add))
    s.wait()
    s.mark(dve.tensor_tensor(rank, rank, t["incl"], ALU.add))
    s.step(dve.tensor_scalar_add(t["cnt_i"], t["incl"][:, (NT - 1) * E:], float(P - 1)))
    s.step(dve.tensor_single_scalar(t["cnt_i"], t["cnt_i"], -P, ALU.bitwise_and))
    s.step(dve.tensor_copy(t["padded"], t["cnt_i"]))
    s.step(dve.tensor_tensor_scan(t["ends"], t["one"].to_broadcast([P, E]), t["padded"], 0.0, ALU.mult, ALU.add))
    s.step(dve.tensor_tensor(t["base"], t["ends"], t["padded"], ALU.subtract))
    s.step(dve.tensor_tensor(rank, rank, total, ALU.subtract))
    s.step(dve.tensor_tensor(by(rank), by(rank), t["base"].unsqueeze(1).to_broadcast([P, NT, E]), ALU.add))
    J = n_slot_tiles
    ge = t["ge"][0:1, 0:J * E].rearrange("p (j e) -> p j e", e=E)
    s.step(dve.tensor_tensor(ge, t["starts"][0:1, 0:J].unsqueeze(2).to_broadcast([1, J, E]),
                             t["ends"][0:1, :].unsqueeze(1).to_broadcast([1, J, E]), ALU.is_ge))
    s.step(dve.tensor_reduce(t["tile_e"][0:1, 0:J], ge, AX_X, ALU.add))
    s.step(dve.tensor_scalar_min(t["tile_ei"][0:1, 0:J], t["tile_e"][0:1, 0:J], float(E - 1)))


def routing_tables(sb, tag, st):
    t = {}
    for name, n, dt in (("rank", NT * E, F32), ("total", NT * E, F32), ("incl", NT * E, F32), ("padded", E, F32),
                        ("ends", E, F32), ("base", E, F32), ("cnt_i", E, I32), ("ge", (2 * NT + E) * E, F32), ("tile_e", 2 * NT + E, F32)):
        t[name] = sb(tag + "_" + name, [P, n], dt)[:, :]
    t["one"] = st["ones"][:, 0:1]
    t["starts"] = st["starts"][:, :]
    t["tile_ei"] = st["tile_ei"][:, :]
    return t


def load_experts(sp, st, w1, w2, arrived):
    for e in range(E):
        sp.dma_start(st["w1_sb"][:, e * C * HID:(e + 1) * C * HID].rearrange("p (c n) -> p c n", c=C),
                     w1[e].rearrange("(c p) n -> p c n", p=P)).then_inc(arrived, 16)
        sp.dma_start(st["w2_sb"][:, e * HC * D:(e + 1) * HC * D].rearrange("p (c n) -> p c n", c=HC),
                     w2[e].rearrange("(c p) n -> p c n", p=P)).then_inc(arrived, 16)


def route(nc, st, tag, w_router, bias, xn_dram, w1, w2, experts_in):
    h, ident, logits = (st[k] for k in ("h", "ident", "logits"))
    with ExitStack() as ctx:
        sb, pb, sem = allocators(nc, ctx)
        w_sb = sb(tag + "_w", [P, C * E], F32)
        b_sb = sb(tag + "_b", [P, E], F32)
        stats = sb(tag + "_stats", [P, NT * 6], F32)
        mv = sb(tag + "_mv", [P, NT * 2], F32)
        var = sb(tag + "_var", [P, NT], F32)
        dev = sb(tag + "_dev", [P, NT], F32)
        rstd = sb(tag + "_rstd", [P, NT], F32)
        xn = sb(tag + "_xn", [P, NT * D], F32)
        xt = sb(tag + "_xt", [P, 2 * C * S], F32)
        ps_t = pb(tag + "_pt", [P, 4 * CHUNK], F32)
        ps_l = pb(tag + "_pl", [P, CHUNK], F32)
        w_in = sem(tag + "_in")
        own = sem(tag + "_own")
        var_ready = sem(tag + "_var_ready")
        dev_ready = sem(tag + "_dev_ready")
        xn_ready = sem(tag + "_xn_ready")
        xn_stored = sem(tag + "_xn_stored")
        turned = sem(tag + "_turned")
        xt_ready = sem(tag + "_xt_ready")
        logit_done = sem(tag + "_logit_done")
        block = ctx.enter_context(nc.Block())
        Q = C * NC
        n_in = 32 if bias is not None else 16

        def turned_to(b, c, lo, n):
            return xt[:, (b % 2 * C + c) * S + lo:(b % 2 * C + c) * S + lo + n]

        @block.sync
        def _(sp):
            sp.dma_start(w_sb[:, :].rearrange("p (c n) -> p c n", c=C), w_router.rearrange("(c p) n -> p c n", p=P)).then_inc(w_in, 16)
            if bias is not None:
                sp.dma_start(b_sb[:, :], bias.partition_broadcast(P)).then_inc(w_in, 16)
            for b in range(B):
                sp.wait_ge(xn_ready, b + 1)
                sp.dma_start(xn_dram[b * S:(b + 1) * S, :].rearrange("(n p) d -> p n d", p=P),
                             xn[:, b * TB * D:(b + 1) * TB * D].rearrange("p (n d) -> p n d", d=D)).then_inc(xn_stored, 16)
            load_experts(sp, st, w1, w2, experts_in)
            sp.wait_ge(xn_stored, B * 16)

        @block.vector
        def _(dve):
            s = Steps(dve, own)

            def statistics(b):
                for n in range(b * TB, (b + 1) * TB):
                    last = dve.bn_stats(stats[:, n * 6:(n + 1) * 6], h[:, n * D:(n + 1) * D])
                s.step(last)
                for n in range(b * TB, (b + 1) * TB):
                    last = dve.bn_aggr(mv[:, n * 2:(n + 1) * 2], stats[:, n * 6:(n + 1) * 6])
                s.step(last)
                dve.tensor_scalar_add(var[:, b * TB:(b + 1) * TB], mv[:, b * TB * 2 + 1:(b + 1) * TB * 2:2],
                                      LN_EPS).then_inc(var_ready, 1)

            def normalise(b):
                dve.wait_ge(dev_ready, b + 1)
                s.step(dve.reciprocal(rstd[:, b * TB:(b + 1) * TB], dev[:, b * TB:(b + 1) * TB]))
                for n in range(b * TB, (b + 1) * TB):
                    last = dve.tensor_scalar(xn[:, n * D:(n + 1) * D], h[:, n * D:(n + 1) * D], mv[:, 2 * n:2 * n + 1],
                                             rstd[:, n:n + 1], ALU.subtract, ALU.mult)
                last.then_inc(xn_ready, 1)

            for b in range(B):
                statistics(b)
                normalise(b)
            dve.wait_ge(w_in, n_in)
            dve.wait_ge(logit_done, B)
            if bias is not None:
                s.step(dve.tensor_tensor(logits[:, :].rearrange("p (n e) -> p n e", e=E),
                                         ps_l[:, 0:NT * E].rearrange("p (n e) -> p n e", e=E),
                                         b_sb[:, :].unsqueeze(1).to_broadcast([P, NT, E]), ALU.add))
            else:
                s.step(dve.tensor_copy(logits[:, :], ps_l[:, 0:NT * E]))

        @block.scalar
        def _(act):
            def deviation(b):
                act.wait_ge(var_ready, b + 1)
                act.activation(dev[:, b * TB:(b + 1) * TB], var[:, b * TB:(b + 1) * TB], ACT.Sqrt).then_inc(dev_ready, 1)

            deviation(0)
            for b in range(B):
                if b < B - 1:
                    deviation(b + 1)
                if b >= 2:
                    act.wait_ge(logit_done, b - 1)
                for q in range(Q):
                    c, half = q // NC, q % NC
                    act.wait_ge(turned, b * Q + q + 1)
                    act.activation(turned_to(b, c, half * CHUNK, CHUNK), ps_t[:, q * CHUNK:(q + 1) * CHUNK],
                                   ACT.Copy).then_inc(xt_ready, 1)

        @block.tensor
        def _(pe):
            def turn(b):
                pe.wait_ge(xn_ready, b + 1)
                for q in range(Q):
                    c, half = q // NC, q % NC
                    if b >= 1:
                        pe.wait_ge(xt_ready, (b - 1) * Q + q + 1)
                    for j in range(TB // NC):
                        n = b * TB + half * (TB // NC) + j
                        last = pe.transpose(ps_t[:, q * CHUNK + j * P:q * CHUNK + (j + 1) * P],
                                            xn[:, n * D + c * P:n * D + (c + 1) * P], ident[:, :])
                    last.then_inc(turned, 1)

            pe.wait_ge(w_in, n_in)
            turn(0)
            for b in range(B):
                if b < B - 1:
                    turn(b + 1)
                pe.wait_ge(xt_ready, (b + 1) * Q)
                for n in range(TB):
                    for c in range(C):
                        last = pe.matmul(ps_l[:, (b * TB + n) * E:(b * TB + n + 1) * E], turned_to(b, c, n * P, P),
                                         w_sb[:, c * E:(c + 1) * E], start=(c == 0), stop=(c == C - 1))
                last.then_inc(logit_done, 1)


def slot_table(nc, st, tag, choices, n_slot_tiles):
    pos, number, slot_rows = st["pos"], st["number"], st["slot_rows"]
    with ExitStack() as ctx:
        sb, pb, sem = allocators(nc, ctx)
        W, J, R = choices * NT, n_slot_tiles, 8
        pos_i = sb(tag + "_pos_i", [P, W], I32)
        part_i = sb(tag + "_part_i", [P, 2 * W], I32)
        low = sb(tag + "_low", [P, W], F32)
        high = sb(tag + "_high", [P, W], F32)
        at_low = sb(tag + "_at_low", [P, R * P], F32)
        at_high = sb(tag + "_at_high", [P, R * J], F32)
        empty = sb(tag + "_empty", [P, J], F32)
        row = sb(tag + "_row", [P, J], F32)
        row_i = sb(tag + "_row_i", [P, J], I32)
        ps = pb(tag + "_ps", [P, CHUNK], F32)
        own = sem(tag + "_own")
        high_marked = sem(tag + "_high_marked")
        marked = sem(tag + "_marked")
        placed = sem(tag + "_placed")
        block = ctx.enter_context(nc.Block())
        FREE = 2
        F = R // FREE

        def over_rings(eng, ring):
            ring(0)
            with eng.Fori(1, W // R - 1) as i:
                ring(i)
            ring(W // R - 1)

        @block.vector
        def _(dve):
            s = Steps(dve, own)
            s.step(dve.tensor_copy(pos_i[:, :], pos[:, 0:W]))
            s.mark(dve.tensor_single_scalar(part_i[:, 0:W], pos_i[:, :], P - 1, ALU.bitwise_and))
            s.step(dve.tensor_single_scalar(part_i[:, W:2 * W], pos_i[:, :], P.bit_length() - 1, ALU.arith_shift_right))
            s.mark(dve.tensor_copy(low[:, :], part_i[:, 0:W]))
            s.step(dve.tensor_copy(high[:, :], part_i[:, W:2 * W]))

            def ring(i):
                for f in range(FREE):
                    need(dve, placed, i * FREE + f + 1 - FREE)
                    count = lambda n: st["count"][:, 0:n].unsqueeze(1).to_broadcast([P, F, n])
                    of_token = lambda a, n: a[:, ds(i * R + f * F, F)].unsqueeze(2).to_broadcast([P, F, n])
                    by_high = at_high[:, f * F * J:(f + 1) * F * J].rearrange("p (k n) -> p k n", n=J)
                    dve.tensor_tensor(by_high, count(J), of_token(high, J), ALU.is_equal).then_inc(high_marked, 1)
                    dve.tensor_tensor(at_low[:, f * F * P:(f + 1) * F * P].rearrange("p (k n) -> p k n", n=P), count(P),
                                      of_token(low, P), ALU.is_equal).then_inc(marked, 1)
                    dve.wait_ge(high_marked, i * FREE + f + 1)
                    dve.tensor_tensor(by_high, by_high, of_token(number, J), ALU.mult).then_inc(marked, 1)

            over_rings(dve, ring)
            dve.wait_ge(placed, W // R * FREE)
            s.mark(dve.tensor_single_scalar(empty[:, :], ps[:, 0:J], 0.0, ALU.is_equal))
            s.step(dve.tensor_scalar_add(row[:, :], ps[:, 0:J], -1.0))
            s.mark(dve.tensor_copy(row_i[:, :], row[:, :]))
            s.step(dve.scalar_tensor_tensor(out=empty[:, :], in0=st["slot_number"][:, 0:J], scalar=choices * T + 1.0,
                                            in1=empty[:, :], op0=ALU.add, op1=ALU.mult))
            s.mark(dve.tensor_single_scalar(slot_rows[:, 0:2 * J:2], row_i[:, :], T - 1, ALU.bitwise_and))
            s.step(dve.tensor_tensor(slot_rows[:, 1:2 * J:2], row[:, :], empty[:, :], ALU.add))

        @block.tensor
        def _(pe):
            def ring(i):
                for k in range(R):
                    if k % F == 0:
                        pe.wait_ge(marked, i * (2 * FREE) + 2 * (k // F) + 2)
                    n = i * R + k if isinstance(i, int) else None
                    last = pe.matmul(ps[:, 0:J], at_low[:, k * P:(k + 1) * P], at_high[:, k * J:(k + 1) * J],
                                     start=(n == 0), stop=(n == W - 1))
                    if k % F == F - 1:
                        last.then_inc(placed, 1)

            over_rings(pe, ring)


def dispatch_top2(nc, st):
    logits, gates, pos = (st[k] for k in ("logits", "gates", "pos"))
    with ExitStack() as ctx:
        sb, pb, sem = allocators(nc, ctx)
        t = routing_tables(sb, "d0", st)
        rev = st["rev"][:, :]
        vals2 = sb("d0_vals2", [P, NT * E], F32)[:, :]
        eq = sb("d0_eq", [P, NT * E], F32)[:, :]
        oh1 = sb("d0_oh1", [P, NT * E], F32)[:, :]
        oh2 = sb("d0_oh2", [P, NT * E], F32)[:, :]
        marks = sb("d0_marks", [P, NT * E], F32)[:, :]
        top1 = sb("d0_top1", [P, NT], F32)[:, :]
        top2 = sb("d0_top2", [P, NT], F32)[:, :]
        cmax = sb("d0_cmax", [P, NT], F32)[:, :]
        dif = sb("d0_dif", [P, NT], F32)[:, :]
        ps_rank = pb("d0_ps", [P, 2 * NT * E], F32)
        own = sem("d0_own")
        dif_ready = sem("d0_dif_ready")
        exp_ready = sem("d0_exp_ready")
        marks_ready = sem("d0_marks_ready")
        ranked = sem("d0_ranked")
        block = ctx.enter_context(nc.Block())
        by = lambda a: a.rearrange("p (n e) -> p n e", e=E)

        @block.vector
        def _(dve):
            s = Steps(dve, own)
            first_of_max(dve, s, by(logits[:, :]), top1, by(eq), rev, cmax, by(oh1))
            s.step(dve.scalar_tensor_tensor(out=vals2, in0=oh1, scalar=-3e38, in1=logits[:, :], op0=ALU.mult, op1=ALU.add))
            first_of_max(dve, s, by(vals2), top2, by(eq), rev, cmax, by(oh2))
            dve.tensor_tensor(marks, oh1, oh2, ALU.add).then_inc(marks_ready, 1)
            dve.tensor_tensor(dif, top2, top1, ALU.subtract).then_inc(dif_ready, 1)
            dve.wait_ge(exp_ready, 1)
            s.step(dve.tensor_scalar_add(top2, dif, 1.0))
            s.step(dve.reciprocal(gates[:, 0:NT], top2))
            s.step(dve.tensor_tensor(gates[:, NT:2 * NT], gates[:, 0:NT], dif, ALU.mult))
            dve.wait_ge(ranked, 1)
            slots_of(dve, s, t, ps_rank, 2 * T // P + E)
            for w, oh in enumerate((oh1, oh2)):
                s.step(dve.tensor_tensor(oh, oh, t["rank"], ALU.mult))
                s.step(dve.tensor_reduce(pos[:, w * NT:(w + 1) * NT], by(oh), AX_X, ALU.add))

        @block.scalar
        def _(act):
            act.wait_ge(dif_ready, 1)
            act.activation(dif, dif, ACT.Exp).then_inc(exp_ready, 1)

        @block.tensor
        def _(pe):
            pe.wait_ge(marks_ready, 1)
            pe.matmul(ps_rank[:, 0:NT * E], st["before"][:, :], marks, start=True, stop=True)
            pe.matmul(ps_rank[:, NT * E:2 * NT * E], st["ones"][:, :], marks, start=True, stop=True).then_inc(ranked, 1)


def experts(nc, st, tag, n_tiles, xn_dram, y_dram, b1, b2, func, weights_in):
    ident, w1_sb, w2_sb, tile_ei, slot_rows = (st[k] for k in ("ident", "w1_sb", "w2_sb", "tile_ei", "slot_rows"))
    X4, X8 = 4, 8
    with ExitStack() as ctx:
        sb, pb, sem = allocators(nc, ctx)
        rows_now = sb(tag + "_rows_now", [P, X8 * 2], I32)
        xin = sb(tag + "_xin", [P, X4 * D], F32)
        xt = sb(tag + "_xt", [P, 2 * D], F32)
        w1_now = sb(tag + "_w1_now", [P, 2 * C * HID], F32)
        hid = sb(tag + "_hid", [P, 2 * HID], F32) if b1 is not None else None
        hidt = sb(tag + "_hidt", [P, 2 * HID], F32)
        yout = sb(tag + "_yout", [P, X4 * D], F32)
        b1_all = sb(tag + "_b1", [P, E * HC], F32) if b1 is not None else None
        b2_all = sb(tag + "_b2", [P, E * D], F32) if b2 is not None else None
        ps_x = pb(tag + "_px", [P, 2 * CHUNK], F32)
        ps_h = pb(tag + "_ph", [P, 2 * HID], F32)
        ps_y = pb(tag + "_py", [P, 2 * CHUNK], F32)
        bias_in = sem(tag + "_bias_in")
        rows_ready = sem(tag + "_rows_ready")
        x_in = [sem(f"{tag}_x_in{k}") for k in range(X4)]
        y_out = [sem(f"{tag}_y_out{k}") for k in range(X4)]
        x_turned = sem(tag + "_x_turned")
        xt_ready = sem(tag + "_xt_ready")
        w1_ready = sem(tag + "_w1_ready")
        first_done = sem(tag + "_first_done")
        hid_ready = sem(tag + "_hid_ready")
        hidt_ready = sem(tag + "_hidt_ready")
        second_done = sem(tag + "_second_done")
        y_ready = sem(tag + "_y_ready")
        passed = sem(tag + "_passed")
        block = ctx.enter_context(nc.Block())
        LOOPS = n_tiles // 8 - 1
        assert n_tiles == 8 * LOOPS + 8

        def over_tiles(eng, step):
            for c in range(5):
                step(0, c)
            with eng.Fori(0, LOOPS) as i:
                for c in range(5, 13):
                    step(i, c)
            for c in range(5, 8):
                step(LOOPS, c)

        def tile_need(eng, s, i, c):
            need(eng, s, i * 8 + c)

        def y_stored(eng, i, c):
            need(eng, y_out[c % X4], i * (8 // X4 * 16) + (c // X4 + 1) * 16)

        def slot(t, c, n, w):
            return t[:, (c % n) * w:(c % n + 1) * w]

        def pick(eng, i, c):
            return eng.value_load(tile_ei[0:1, ds(i * 8 + c, 1)], min_val=0, max_val=E - 1)

        @block.sync
        def _(sp):
            if b1 is not None:
                sp.dma_start(b1_all[:, :], b1).then_inc(bias_in, 16)
                sp.dma_start(b2_all[:, :], b2.rearrange("e n -> (e n)").partition_broadcast(P)).then_inc(bias_in, 16)

        @block.gpsimd
        def _(pool):
            def gather(i, c):
                pool.wait_ge(rows_ready, i * 8 + c + 1)
                tile_need(pool, x_turned, i, c + 1 - X4)
                pool.sem_inc(passed, 1)
                pool.indirect_dma_start(out=slot(xin, c, X4, D), out_offset=None, in_=xn_dram,
                                        in_offset=bass.IndirectOffsetOnAxis(ap=rows_now[:, 2 * (c % X8):2 * (c % X8) + 1], axis=0),
                                        ).then_inc(x_in[c % X4], 16)

            def scatter(i, c):
                pool.wait_ge(y_ready, i * 8 + c + 1)
                pool.sem_inc(passed, 1)
                pool.indirect_dma_start(out=y_dram, out_offset=bass.IndirectOffsetOnAxis(
                    ap=rows_now[:, 2 * (c % X8) + 1:2 * (c % X8) + 2], axis=0),
                                        in_=slot(yout, c, X4, D), in_offset=None).then_inc(y_out[c % X4], 16)

            for c in range(X4):
                gather(0, c)
            with pool.Fori(0, LOOPS) as i:
                for c in range(8):
                    gather(i, c + X4)
                    scatter(i, c)
            for c in range(8):
                if c + X4 < 8:
                    gather(LOOPS, c + X4)
                scatter(LOOPS, c)
            for c in range(X4):
                pool.wait_ge(y_out[c], 16 * (n_tiles // X4))

        @block.tensor
        def _(pe):
            pe.wait_ge(weights_in, 2 * E * 16)

            def turn_x(i, c):
                pe.wait_ge(x_in[c % X4], i * 32 + (c // X4 + 1) * 16)
                tile_need(pe, xt_ready, i, c - 1)
                for k in range(C):
                    last = pe.transpose(ps_x[:, (c % 2) * CHUNK + k * P:(c % 2) * CHUNK + (k + 1) * P],
                                        xin[:, (c % X4) * D + k * P:(c % X4) * D + (k + 1) * P], ident[:, :])
                last.then_inc(x_turned, 1)

            def first(i, c):
                tile_need(pe, xt_ready, i, c + 1)
                tile_need(pe, w1_ready, i, c + 1)
                tile_need(pe, hid_ready if b1 is not None else hidt_ready, i, c - 1)
                for m in range(HC):
                    for k in range(C):
                        at = (c % 2) * C * HID + k * HID + m * P
                        last = pe.matmul(ps_h[:, (c % 2) * HID + m * P:(c % 2) * HID + (m + 1) * P], w1_now[:, at:at + P],
                                         xt[:, (c % 2) * D + k * P:(c % 2) * D + (k + 1) * P], start=(k == 0), stop=(k == C - 1))
                last.then_inc(first_done, 1)

            def second(i, c):
                e = pick(pe, i, c)
                tile_need(pe, hidt_ready, i, c + 1)
                tile_need(pe, y_ready, i, c - 1)
                for k in range(HC):
                    last = pe.matmul(ps_y[:, (c % 2) * CHUNK:(c % 2) * CHUNK + D],
                                     hidt[:, (c % 2) * HID + k * P:(c % 2) * HID + (k + 1) * P],
                                     w2_sb[:, ds(e * (HC * D) + k * D, D)], start=(k == 0), stop=(k == HC - 1))
                last.then_inc(second_done, 1)

            turn_x(0, 0)

            def tile(i, c):
                if not (isinstance(i, int) and 8 * i + c == n_tiles - 1):
                    turn_x(i, c + 1)
                first(i, c)
                if not (isinstance(i, int) and 8 * i + c == 0):
                    second(i, c - 1)

            over_tiles(pe, tile)
            second(LOOPS, 7)

        @block.vector
        def _(dve):
            if b1 is not None:
                dve.wait_ge(bias_in, 32)

            def take_rows(i, c):
                if not (isinstance(i, int) and 8 * i + c < X8):
                    y_stored(dve, i, c - X8)
                dve.tensor_copy(slot(rows_now, c, X8, 2), slot_rows[:, ds((i * 8 + c) * 2, 2)]).then_inc(rows_ready, 1)

            def take_x(i, c):
                tile_need(dve, x_turned, i, c + 1)
                tile_need(dve, first_done, i, c - 1)
                dve.tensor_copy(slot(xt, c, 2, D), ps_x[:, (c % 2) * CHUNK:(c % 2) * CHUNK + D]).then_inc(xt_ready, 1)

            def add_bias(i, c):
                e = pick(dve, i, c)
                tile_need(dve, first_done, i, c + 1)
                tile_need(dve, hidt_ready, i, c - 1)
                by = lambda a: a.rearrange("p (m t) -> p m t", t=P)
                dve.tensor_tensor(by(slot(hid, c, 2, HID)), by(slot(ps_h, c, 2, HID)),
                                  b1_all[:, ds(e * HC, HC)].unsqueeze(2).to_broadcast([P, HC, P]), ALU.add).then_inc(hid_ready, 1)

            def take_y(i, c):
                if b2 is not None:
                    e = pick(dve, i, c)
                tile_need(dve, second_done, i, c + 1)
                if not (isinstance(i, int) and 8 * i + c < X4):
                    y_stored(dve, i, c - X4)
                y = ps_y[:, (c % 2) * CHUNK:(c % 2) * CHUNK + D]
                if b2 is not None:
                    dve.tensor_tensor(slot(yout, c, X4, D), y, b2_all[:, ds(e * D, D)], ALU.add).then_inc(y_ready, 1)
                else:
                    dve.tensor_copy(slot(yout, c, X4, D), y).then_inc(y_ready, 1)

            AHEAD = 3
            for c in range(AHEAD):
                take_rows(0, c)
            take_x(0, 0)

            def tile(i, c):
                if not (isinstance(i, int) and 8 * i + c + AHEAD >= n_tiles):
                    take_rows(i, c + AHEAD)
                if not (isinstance(i, int) and 8 * i + c == n_tiles - 1):
                    take_x(i, c + 1)
                if b1 is not None:
                    add_bias(i, c)
                if not (isinstance(i, int) and 8 * i + c == 0):
                    take_y(i, c - 1)

            over_tiles(dve, tile)
            take_y(LOOPS, 7)

        @block.scalar
        def _(act):
            act.wait_ge(weights_in, 2 * E * 16)

            def take_w1(i, c):
                e = pick(act, i, c)
                tile_need(act, first_done, i, c - 1)
                act.activation(slot(w1_now, c, 2, C * HID), w1_sb[:, ds(e * (C * HID), C * HID)], ACT.Copy).then_inc(w1_ready, 1)

            take_w1(0, 0)

            def tile(i, c):
                if not (isinstance(i, int) and 8 * i + c == n_tiles - 1):
                    take_w1(i, c + 1)
                tile_need(act, second_done, i, c - 1)
                if b1 is not None:
                    tile_need(act, hid_ready, i, c + 1)
                    act.activation(slot(hidt, c, 2, HID), slot(hid, c, 2, HID), func).then_inc(hidt_ready, 1)
                else:
                    tile_need(act, first_done, i, c + 1)
                    act.activation(slot(hidt, c, 2, HID), slot(ps_h, c, 2, HID), func).then_inc(hidt_ready, 1)

            over_tiles(act, tile)


def load_results(eng, y, y_dram, b, w, arrived):
    eng.dma_start(y[:, (w * NT + b * TB) * D:(w * NT + (b + 1) * TB) * D].rearrange("p (n d) -> p n d", d=D),
                  y_dram[w * T + b * S:w * T + (b + 1) * S, :].rearrange("(n p) d -> p n d", p=P)).then_inc(arrived, 16)


def add_gated(dve, h, y, gates, b):
    for n in range(b * TB, (b + 1) * TB):
        hn = h[:, n * D:(n + 1) * D]
        last = dve.scalar_tensor_tensor(out=hn, in0=y[:, n * D:(n + 1) * D], scalar=gates[:, n:n + 1], in1=hn,
                                        op0=ALU.mult, op1=ALU.add)
    return last


def combine_top2(nc, st, y_dram):
    h, gates, mv, rstd = (st[k] for k in ("h", "gates", "mv", "rstd"))
    with ExitStack() as ctx:
        sb, pb, sem = allocators(nc, ctx)
        y = sb("c0_y", [P, 2 * NT * D], F32)
        stats = sb("c0_stats", [P, NT * 6], F32)
        var = sb("c0_var", [P, NT], F32)
        dev = sb("c0_dev", [P, NT], F32)
        y_in = [[sem(f"c0_y{w}_in{b}") for b in range(B)] for w in range(2)]
        own = sem("c0_own")
        first_added = sem("c0_first_added")
        scaled = sem("c0_scaled")
        second_added = sem("c0_second_added")
        var_ready = sem("c0_var_ready")
        dev_ready = sem("c0_dev_ready")
        block = ctx.enter_context(nc.Block())

        @block.sync
        def _(sp):
            for b in range(B):
                for w in (1, 0):
                    load_results(sp, y, y_dram, b, w, y_in[w][b])

        @block.scalar
        def _(act):
            for b in range(B):
                act.wait_ge(y_in[1][b], 16)
                for n in range(NT + b * TB, NT + (b + 1) * TB):
                    last = act.activation(y[:, n * D:(n + 1) * D], y[:, n * D:(n + 1) * D], ACT.Copy, scale=gates[:, n:n + 1])
                last.then_inc(scaled, 1)
            act.wait_ge(var_ready, 1)
            act.activation(dev[:, :], var[:, :], ACT.Sqrt).then_inc(dev_ready, 1)

        @block.gpsimd
        def _(pool):
            for b in range(B):
                pool.wait_ge(first_added, b + 1)
                pool.wait_ge(scaled, b + 1)
                hb = h[:, b * TB * D:(b + 1) * TB * D]
                pool.tensor_tensor(hb, hb, y[:, (NT + b * TB) * D:(NT + (b + 1) * TB) * D], ALU.add).then_inc(second_added, 1)

        @block.vector
        def _(dve):
            s = Steps(dve, own)

            def add_first(b):
                dve.wait_ge(y_in[0][b], 16)
                add_gated(dve, h, y, gates, b).then_inc(first_added, 1)

            add_first(0)
            for b in range(B):
                if b < B - 1:
                    add_first(b + 1)
                dve.wait_ge(second_added, b + 1)
                for n in range(b * TB, (b + 1) * TB):
                    last = dve.bn_stats(stats[:, n * 6:(n + 1) * 6], h[:, n * D:(n + 1) * D])
                s.step(last)
                for n in range(b * TB, (b + 1) * TB):
                    last = dve.bn_aggr(mv[:, n * 2:(n + 1) * 2], stats[:, n * 6:(n + 1) * 6])
            s.step(last)
            dve.tensor_scalar_add(var[:, :], mv[:, 1::2], LN_EPS).then_inc(var_ready, 1)
            dve.wait_ge(dev_ready, 1)
            s.step(dve.reciprocal(rstd[:, :], dev[:, :]))


def combine_top1(nc, st, y_dram, out):
    h, gates = st["h"], st["gates"]
    with ExitStack() as ctx:
        sb, pb, sem = allocators(nc, ctx)
        y = sb("c1_y", [P, NT * D], F32)
        y_in = [sem(f"c1_y_in{b}") for b in range(B)]
        added = sem("c1_added")
        stored = sem("c1_stored")
        block = ctx.enter_context(nc.Block())

        @block.sync
        def _(sp):
            for b in range(B):
                load_results(sp, y, y_dram, b, 0, y_in[b])
            for b in range(B):
                sp.wait_ge(added, b + 1)
                sp.dma_start(out[b].rearrange("(n p) d -> p n d", p=P),
                             h[:, b * TB * D:(b + 1) * TB * D].rearrange("p (n d) -> p n d", d=D)).then_inc(stored, 16)
            sp.wait_ge(stored, 16 * B)

        @block.vector
        def _(dve):
            for b in range(B):
                dve.wait_ge(y_in[b], 16)
                add_gated(dve, h, y, gates, b).then_inc(added, 1)


HEADS, HD = 16, 16
GH = 4
GROUPS = B * HEADS // GH
GCH = GH * HD
KEYS = 256
NB = S // KEYS
PARTS = 3
QROWS = 6 * HD
MROWS = PARTS * NB
ROWS = QROWS + MROWS


PART_ORDER = ((0, 1, 2, 0, 1, 0), (0, 0, 0, 1, 1, 2))


def load_rows(sp, rows, src, i, arrived):
    for r, p in enumerate(PART_ORDER[i]):
        sp.dma_start(rows[r * HD:(r + 1) * HD, :].rearrange("c (j t) -> c j t", j=GH),
                     src[:, p].rearrange("o (j c) t -> c (o j) t", c=HD)).then_inc(arrived, 16)


def project_qkv(nc, st, wq, wk, wv, v_ones, qk_dram, v_dram):
    h, mv, rstd, ident = (st[x] for x in ("h", "mv", "rstd", "ident"))
    with ExitStack() as ctx:
        sb, pb, sem = allocators(nc, ctx)
        VW = GROUPS // B * P
        wqk_sb = sb("qk_w", [P, 2 * C * D], F32)
        wv_sb = sb("v_w", [P, C * D], F32)
        xn = sb("qk_xn", [P, TB * D], F32)
        xt = sb("qk_xt", [P, C * S], F32)
        parts = sb("qk_parts", [P, 2 * PARTS * S], BF16)
        rest = sb("qk_rest", [P, 2 * CHUNK], F32)
        v_sb = sb("v_sb", [P, 4 * VW], F32)
        ps_t = pb("qk_pt", [P, 2 * CHUNK], F32)
        ps_q = pb("qk_pq", [P, 2 * CHUNK], F32)
        ps_v = pb("qk_pv", [P, 2 * CHUNK], F32)
        q0 = sb("qk_q0", [QROWS, GH * S], BF16)
        k0 = sb("qk_k0", [QROWS, GH * S], BF16)
        ps_s = pb("qk_ps", [P, 2 * CHUNK], F32)
        group_in = sem("qk_group_in")
        scored = sem("qk_scored")
        maxed = sem("qk_maxed")
        w_in = sem("qk_w_in")
        xn_ready = sem("qk_xn_ready")
        turned = sem("qk_turned")
        xt_ready = sem("qk_xt_ready")
        projected = sem("qk_projected")
        high_ready = sem("qk_high")
        rest_ready = sem("qk_rest_ready")
        mid_ready = sem("qk_mid")
        low_ready = sem("qk_low")
        parts_out = [sem(f"qk_parts_out{k}") for k in range(2)]
        v_done = sem("qk_v_done")
        v_ready = sem("qk_v_ready")
        v_out = [sem(f"qk_v_out{k}") for k in range(4)]
        block = ctx.enter_context(nc.Block())
        Q = C * NC
        U = 2 * C * NC
        SCALE = HD ** -0.5
        SLOT0 = U + 2
        UNITS, SLOTS = GH * TB * 2, B * U - SLOT0

        def score_units(b, u):
            slot = b * U + u - SLOT0
            return range(0) if slot < 0 else range(slot * UNITS // SLOTS, (slot + 1) * UNITS // SLOTS)

        def part(k, p, lo, n):
            return parts[:, (k % 2 * PARTS + p) * S + lo:(k % 2 * PARTS + p) * S + lo + n]

        @block.sync
        def _(sp):
            for i, w in enumerate((wq, wk)):
                sp.dma_start(wqk_sb[:, i * C * D:(i + 1) * C * D].rearrange("p (c n) -> p c n", c=C),
                             w.rearrange("(c p) n -> p c n", p=P)).then_inc(w_in, 16)
            sp.dma_start(wv_sb[:, :].rearrange("p (c n) -> p c n", c=C), wv.rearrange("(c p) n -> p c n", p=P)).then_inc(w_in, 16)
            for k in range(4):
                sp.dma_start(v_sb[:, k * VW:(k + 1) * VW], v_ones.partition_broadcast(P)).then_inc(w_in, 16)
            for b in range(B):
                for k in range(2 * C):
                    i, d = k // C, k % C
                    sp.wait_ge(low_ready, b * U + (k + 1) * NC)
                    for half in range(2):
                        sp.dma_start(qk_dram[ds(b * (GROUPS // B) + d * 2 + half, 1), i].rearrange("o p c t -> c (o p) t"),
                                     parts[half * GCH:(half + 1) * GCH, (k % 2) * PARTS * S:(k % 2 + 1) * PARTS * S]
                                     .rearrange("c (p t) -> c p t", p=PARTS)).then_inc(parts_out[k % 2], 16)
                if b == 0:
                    sp.wait_ge(parts_out[0], 2 * 32)
                    for t, i in ((q0, 0), (k0, 1)):
                        load_rows(sp, t, qk_dram[0:1, i], i, group_in)
            for k in range(2):
                sp.wait_ge(parts_out[k], B * C * 32)

        @block.gpsimd
        def _(pool):
            with pool.Fori(0, B) as b:
                for n in range(TB):
                    pool.wait_ge(v_ready, b * TB + n + 1)
                    pool.dma_start(v_dram[ds(b * (GROUPS // B), GROUPS // B), n * P:(n + 1) * P, :].rearrange("g t c -> t g c"),
                                   v_sb[:, (n % 4) * VW:(n % 4 + 1) * VW].rearrange("p (g c) -> p g c", g=GROUPS // B)
                                   ).then_inc(v_out[n % 4], 16)
            for k in range(4):
                pool.wait_ge(v_out[k], B * TB // 4 * 16)

        @block.tensor
        def _(pe):
            def score(n):
                j, t, half = n // (2 * TB), n % (2 * TB) // 2, n % 2
                if n == 0:
                    pe.wait_ge(group_in, 2 * 6 * 16)
                need(pe, maxed, n - 1)
                pe.matmul(ps_s[:, (n % 2) * CHUNK:(n % 2 + 1) * CHUNK], q0[:, j * S + t * P:j * S + (t + 1) * P],
                          k0[:, j * S + half * CHUNK:j * S + (half + 1) * CHUNK], start=True, stop=True).then_inc(scored, 1)

            for b in range(B):
                pe.wait_ge(xn_ready, b + 1)
                for q in range(Q):
                    c, half = q // NC, q % NC
                    if q >= 2:
                        pe.wait_ge(xt_ready, b * Q + q - 1)
                    for j in range(TB // NC):
                        n = half * (TB // NC) + j
                        last = pe.transpose(ps_t[:, (q % 2) * CHUNK + j * P:(q % 2) * CHUNK + (j + 1) * P],
                                            xn[:, n * D + c * P:n * D + (c + 1) * P], ident[:, :])
                    last.then_inc(turned, 1)
                pe.wait_ge(xt_ready, (b + 1) * Q)
                pe.wait_ge(w_in, 7 * 16)
                for u in range(U):
                    i, d, m = u // (C * NC), u // NC % C, u % NC
                    for n in score_units(b, u)[:1]:
                        score(n)
                    need(pe, rest_ready, b * U + u - 1)
                    for c in range(C):
                        last = pe.matmul(ps_q[:, (u % 2) * CHUNK:(u % 2 + 1) * CHUNK],
                                         wqk_sb[:, (i * C + c) * D + d * P:(i * C + c) * D + (d + 1) * P],
                                         xt[:, c * S + m * CHUNK:c * S + (m + 1) * CHUNK], start=(c == 0), stop=(c == C - 1))
                    last.then_inc(projected, 1)
                    for n in score_units(b, u)[1:2]:
                        score(n)
                    n = u
                    need(pe, v_ready, b * TB + n - 1)
                    for c in range(C):
                        last = pe.matmul(ps_v[:, (n % 2) * CHUNK:(n % 2) * CHUNK + D], xt[:, c * S + n * P:c * S + (n + 1) * P],
                                         wv_sb[:, c * D:(c + 1) * D], start=(c == 0), stop=(c == C - 1))
                    last.then_inc(v_done, 1)
                    for n in score_units(b, u)[2:]:
                        score(n)

        @block.scalar
        def _(act):
            def sequence(b):
                for q in range(Q):
                    c, half = q // NC, q % NC
                    act.wait_ge(turned, b * Q + q + 1)
                    act.activation(xt[:, c * S + half * CHUNK:c * S + (half + 1) * CHUNK],
                                   ps_t[:, (q % 2) * CHUNK:(q % 2 + 1) * CHUNK], ACT.Copy).then_inc(xt_ready, 1)
                for u in range(U):
                    k, m = u // NC, u % NC
                    if m == 0:
                        need(act, parts_out[k % 2], b * (C * 32) + k // 2 * 32)
                    act.wait_ge(projected, b * U + u + 1)
                    act.activation(part(k, 0, m * CHUNK, CHUNK), ps_q[:, (u % 2) * CHUNK:(u % 2 + 1) * CHUNK], ACT.Copy,
                                   scale=SCALE if k < C else 1.0).then_inc(high_ready, 1)
                    n = u
                    act.wait_ge(v_done, b * TB + n + 1)
                    if isinstance(b, int):
                        act.wait_ge(w_in, 7 * 16)
                    need(act, v_out[n % 4], b * 32 + n // 4 * 16)
                    act.activation(v_sb[:, (n % 4) * VW:(n % 4 + 1) * VW].rearrange("p (j c) -> p j c", j=HEADS)[:, :, 0:HD],
                                   ps_v[:, (n % 2) * CHUNK:(n % 2) * CHUNK + D].rearrange("p (j c) -> p j c", j=HEADS),
                                   ACT.Copy).then_inc(v_ready, 1)
                    act.wait_ge(rest_ready, b * U + u + 1)
                    act.activation(part(k, 1, m * CHUNK, CHUNK), rest[:, (u % 2) * CHUNK:(u % 2 + 1) * CHUNK],
                                   ACT.Copy).then_inc(mid_ready, 1)
                act.wait_ge(v_done, (b + 1) * TB)

            over_sequences(act, sequence)

        @block.vector
        def _(dve):
            def normalise(b):
                dve.wait_ge(turned, b * Q)
                for n in range(TB):
                    t = b * TB + n
                    last = dve.tensor_scalar(xn[:, n * D:(n + 1) * D], h[:, ds(t * D, D)], mv[:, ds(t * 2, 1)],
                                             rstd[:, ds(t, 1)], ALU.subtract, ALU.mult)
                last.then_inc(xn_ready, 1)

            def largest(n):
                j, t, half = n // (2 * TB), n % (2 * TB) // 2, n % 2
                dve.wait_ge(scored, n + 1)
                at = (j * TB + t) * NB + half * 2
                dve.tensor_reduce(st["mx"][:, at:at + 2], ps_s[:, (n % 2) * CHUNK:(n % 2 + 1) * CHUNK]
                                  .rearrange("p (k c) -> p k c", c=KEYS), AX_X, ALU.max).then_inc(maxed, 1)

            def sequence(b):
                for u in range(U):
                    if u == 2 and b < B - 1:
                        normalise(b + 1)
                    for n in score_units(b, u)[:1]:
                        largest(n)
                    k, m = u // NC, u % NC
                    r = rest[:, (u % 2) * CHUNK:(u % 2 + 1) * CHUNK]
                    dve.wait_ge(high_ready, b * U + u + 1)
                    if u > 0:
                        dve.wait_ge(low_ready, b * U + u)
                    dve.scalar_tensor_tensor(out=r, in0=ps_q[:, (u % 2) * CHUNK:(u % 2 + 1) * CHUNK],
                                             scalar=SCALE if k < C else 1.0, in1=part(k, 0, m * CHUNK, CHUNK),
                                             op0=ALU.mult, op1=ALU.subtract).then_inc(rest_ready, 1)
                    for n in score_units(b, u)[1:2]:
                        largest(n)
                    dve.wait_ge(rest_ready, b * U + u + 1)
                    dve.wait_ge(mid_ready, b * U + u + 1)
                    dve.tensor_tensor(part(k, 2, m * CHUNK, CHUNK), r, part(k, 1, m * CHUNK, CHUNK),
                                      ALU.subtract).then_inc(low_ready, 1)
                    for n in score_units(b, u)[2:]:
                        largest(n)
                dve.wait_ge(low_ready, (b + 1) * U)

            for n in range(TB):
                last = dve.tensor_scalar(xn[:, n * D:(n + 1) * D], h[:, n * D:(n + 1) * D], mv[:, n * 2:n * 2 + 1],
                                         rstd[:, n:n + 1], ALU.subtract, ALU.mult)
            last.then_inc(xn_ready, 1)
            for b in range(B):
                sequence(b)
            dve.wait_ge(maxed, UNITS)


def attention(nc, st, qk_dram, v_dram, block_rows, ident_bits):
    ctx_all, mx = st["ctx_all"], st["mx"]
    with ExitStack() as ctx:
        sb, pb, sem = allocators(nc, ctx)
        NU = 3
        qs = [sb(f"at_q{u}", [ROWS, GH * S], BF16) for u in range(NU)]
        ks = [sb(f"at_k{u}", [ROWS, GH * S], BF16) for u in range(NU)]
        vs = [sb(f"at_v{u}", [P, TB * P], F32) for u in range(NU)]
        identb = sb("at_identb", [P, P], BF16)
        ex = sb("at_ex", [P, 2 * GH * CHUNK], F32)
        raw = sb("at_raw", [P, CHUNK], F32)
        den = sb("at_den", [P, GH * GH], F32)
        neg = sb("at_neg", [P, TB * NB], F32)
        zero = sb("at_zero", [P, TB * NB], F32)
        rem = sb("at_rem", [P, TB * NB], F32)
        mp = sb("at_mp", [P, GH * TB * MROWS], BF16)
        ps_k = pb("at_pk", [P, 4 * CHUNK], F32)
        ps_s = pb("at_ps", [P, 2 * CHUNK], F32)
        ps_v = pb("at_pv", [P, CHUNK], F32)
        ps_m = pb("at_pm", [P, CHUNK], F32)
        ps_mb = ps_m[:, :].bitcast(BF16)
        set_up = sem("at_set_up")
        zero_set = sem("at_zero_set")
        in_k = [sem(f"at_in{u}") for u in range(NU)]
        scored = sem("at_scored")
        maxed = sem("at_maxed")
        own = sem("at_own")
        split = sem("at_split")
        rows_turned = sem("at_rows_turned")
        rows_copied = sem("at_rows_copied")
        keyed = sem("at_keyed")
        exp_done = sem("at_exp_done")
        pv_done = sem("at_pv_done")
        pv_copied = sem("at_pv_copied")
        ctx_turned = sem("at_ctx_turned")
        den_ready = sem("at_den_ready")
        ctx_read = sem("at_ctx_read")
        block = ctx.enter_context(nc.Block())
        N_IN = (2 * 6 + 1) * 16
        STEPS = 2 * TB
        UNITS = GH * TB * 2
        FROM = [5 * s for s in range(5)] + [4 * s + 4 for s in range(5, STEPS)] + [UNITS]
        TURN_ROWS = {5: 0, 8: 1, 12: 2, STEPS - 1: GH - 1}
        LOOPS = (GROUPS - 4) // NU

        def over_groups(eng, group):
            group(0, 0)
            with eng.Fori(0, LOOPS) as i:
                for v in (1, 2, 3):
                    group(i, v)
            for v in (1, 2, 3):
                group(LOOPS, v)

        def need(eng, s, i, v, per, c):
            if isinstance(i, int) and per * (NU * i + v) + c <= 0:
                return
            eng.wait_ge(s, i * (per * NU) + (per * v + c))

        def is_first(i, v):
            return isinstance(i, int) and NU * i + v == 0

        def is_last(i, v):
            return isinstance(i, int) and NU * i + v == GROUPS - 1

        @block.sync
        def _(sp):
            for u in range(NU):
                sp.dma_start(ks[u][QROWS:ROWS, :].bitcast(U16), block_rows).then_inc(set_up, 16)
            sp.dma_start(identb[:, :].bitcast(U16), ident_bits).then_inc(set_up, 16)

            def load(i, v):
                if not (isinstance(i, int) and NU * i + v < NU):
                    need(sp, pv_done, i, v, STEPS, -2 * STEPS)
                u, g = v % NU, (i * NU + v)
                for rows, i_qk in ((qs[u], 0), (ks[u], 1)):
                    load_rows(sp, rows, qk_dram[ds(g, 1), i_qk], i_qk, in_k[u])
                src = v_dram[ds(g, 1)] if not isinstance(g, int) else v_dram[g:g + 1]
                sp.dma_start(vs[u][:, :].rearrange("p (n c) -> p n c", c=P),
                             src.rearrange("o (n p) c -> p (o n) c", p=P)).then_inc(in_k[u], 16)

            for v in range(NU):
                load(0, v)
            with sp.Fori(0, LOOPS) as i:
                for v in range(NU, 2 * NU):
                    load(i, v)
            load(LOOPS, NU)

        @block.gpsimd
        def _(pool):
            pool.memset(zero[:, :], 0.0).then_inc(zero_set, 1)
            pool.wait_ge(zero_set, 1)

            def splits(i, v):
                for j in range(GH):
                    base = i * (4 * GH * NU) + 4 * (GH * v + j)
                    m = mx[:, j * TB * NB:(j + 1) * TB * NB]
                    by = mp[:, j * TB * MROWS:(j + 1) * TB * MROWS].rearrange("p (n k) -> p n k", k=PARTS)
                    as3 = lambda a: a.unsqueeze(2)
                    if not is_first(i, v):
                        need(pool, maxed, i, v - 1, UNITS, (j + 1) * 2 * TB)
                    need(pool, rows_turned, i, v, GH, j + 1 - GH)
                    need(pool, split, i, v, GH, j)
                    pool.tensor_tensor(neg[:, :], zero[:, :], m, ALU.subtract).then_inc(own, 1)
                    pool.wait_ge(own, base + 1)
                    pool.tensor_tensor(by[:, :, 0:1], as3(neg[:, :]), as3(zero[:, :]), ALU.add).then_inc(own, 1)
                    pool.wait_ge(own, base + 2)
                    pool.tensor_tensor(as3(rem[:, :]), as3(neg[:, :]), by[:, :, 0:1], ALU.subtract).then_inc(own, 1)
                    pool.wait_ge(own, base + 3)
                    pool.tensor_tensor(by[:, :, 1:2], as3(rem[:, :]), as3(zero[:, :]), ALU.add).then_inc(own, 1)
                    pool.wait_ge(own, base + 4)
                    pool.tensor_tensor(by[:, :, 2:3], as3(rem[:, :]), by[:, :, 1:2], ALU.subtract).then_inc(split, 1)

            over_groups(pool, splits)

        @block.tensor
        def _(pe):
            pe.wait_ge(set_up, (NU + 1) * 16)

            def score(i, v, n):
                j, t, half, u = n // (2 * TB), n % (2 * TB) // 2, n % 2, v % NU
                if n == 0:
                    pe.wait_ge(in_k[u], i * N_IN + (v // NU + 1) * N_IN)
                need(pe, maxed, i, v - 1, UNITS, n - 1)
                pe.matmul(ps_s[:, (n % 2) * CHUNK:(n % 2 + 1) * CHUNK], qs[u][0:QROWS, j * S + t * P:j * S + (t + 1) * P],
                          ks[u][0:QROWS, j * S + half * CHUNK:j * S + (half + 1) * CHUNK],
                          start=True, stop=True).then_inc(scored, 1)

            def turn_rows(i, v, j):
                need(pe, split, i, v, GH, j + 1)
                need(pe, rows_copied, i, v, GH, j)
                for t in range(TB):
                    last = pe.transpose(ps_mb[QROWS:ROWS, t * P:(t + 1) * P],
                                        mp[:, (j * TB + t) * MROWS:(j * TB + t + 1) * MROWS], identb[:, :])
                last.then_inc(rows_turned, 1)

            def key_scores(i, v, s, pair):
                half, kt, u = s // TB, s % TB, v % NU
                need(pe, exp_done, i, v, 2 * STEPS, 2 * s + pair - 1)
                for j in (2 * pair, 2 * pair + 1):
                    last = pe.matmul(ps_k[:, j * CHUNK:(j + 1) * CHUNK], ks[u][:, j * S + kt * P:j * S + (kt + 1) * P],
                                     qs[u][:, j * S + half * CHUNK:j * S + (half + 1) * CHUNK], start=True, stop=True)
                last.then_inc(keyed, 1)

            def values(i, v, s):
                half, kt, u = s // TB, s % TB, v % NU
                need(pe, exp_done, i, v, 2 * STEPS, 2 * s + 2)
                if kt == 0:
                    need(pe, pv_copied, i, v, 2, half)
                for j in range(GH):
                    last = pe.matmul(ps_v[32 * j:32 * j + 32, :], vs[u][:, kt * P + 32 * j:kt * P + 32 * j + 32],
                                     ex[:, (s % 2) * GH * CHUNK + j * CHUNK:(s % 2) * GH * CHUNK + (j + 1) * CHUNK],
                                     start=(kt == 0), stop=(kt == TB - 1), skip_group_check=True)
                last.then_inc(pv_done, 1)

            def turn_ctx(i, v, half):
                need(pe, pv_copied, i, v, 2, half + 1)
                need(pe, ctx_read, i, v, 2, half)
                for t in range(CHUNK // P):
                    last = pe.transpose(ps_m[:, t * P:(t + 1) * P], raw[:, t * P:(t + 1) * P], st["ident"][:, :])
                last.then_inc(ctx_turned, 1)

            for j in range(GH):
                turn_rows(0, 0, j)
            pe.wait_ge(in_k[0], N_IN)

            def group(i, v):
                for s in range(STEPS):
                    more = [] if is_last(i, v) else list(range(FROM[s], FROM[s + 1]))
                    if s == 0:
                        need(pe, rows_copied, i, v, GH, 2)
                    for n in more[:1]:
                        score(i, v + 1, n)
                    key_scores(i, v, s, 0)
                    for n in more[1:-2]:
                        score(i, v + 1, n)
                    if s == 0:
                        need(pe, rows_copied, i, v, GH, GH)
                    key_scores(i, v, s, 1)
                    for n in more[-2:] if len(more) > 2 else more[1:]:
                        score(i, v + 1, n)
                    if s > 0:
                        values(i, v, s - 1)
                    elif not is_first(i, v):
                        values(i, v - 1, STEPS - 1)
                    if s == 2 and not is_first(i, v):
                        turn_ctx(i, v - 1, 1)
                    if s in TURN_ROWS and not is_last(i, v):
                        if s == 5:
                            need(pe, ctx_read, i, v, 2, 0)
                        if s == 12:
                            need(pe, ctx_read, i, v, 2, 1)
                        turn_rows(i, v + 1, TURN_ROWS[s])
                    if s == 10:
                        if not is_last(i, v):
                            need(pe, rows_copied, i, v, GH, GH + 2)
                        turn_ctx(i, v, 0)

            over_groups(pe, group)
            values(LOOPS, NU, STEPS - 1)
            pe.wait_ge(ctx_read, 2 * GROUPS - 1)
            turn_ctx(LOOPS, NU, 1)

        @block.scalar
        def _(act):
            def copy_rows(i, v, j):
                u = v % NU
                need(act, rows_turned, i, v, GH, j + 1)
                act.activation(qs[u][QROWS:ROWS, j * S:(j + 1) * S], ps_mb[QROWS:ROWS, :], ACT.Copy).then_inc(rows_copied, 1)

            def exps(i, v, s, pair):
                need(act, keyed, i, v, 2 * STEPS, 2 * s + pair + 1)
                need(act, pv_done, i, v, STEPS, s - 1)
                at = (s % 2) * GH * CHUNK + pair * 2 * CHUNK
                act.activation(ex[:, at:at + 2 * CHUNK], ps_k[:, pair * 2 * CHUNK:(pair + 1) * 2 * CHUNK],
                               ACT.Exp).then_inc(exp_done, 1)

            def copy_ctx(i, v, half):
                need(act, pv_done, i, v, STEPS, (half + 1) * TB)
                need(act, ctx_turned, i, v, 2, half)
                act.activation(raw[:, :], ps_v[:, :], ACT.Copy).then_inc(pv_copied, 1)

            for j in range(GH):
                copy_rows(0, 0, j)

            def group(i, v):
                for s in range(STEPS):
                    exps(i, v, s, 0)
                    exps(i, v, s, 1)
                    if s == 0 and not is_first(i, v):
                        copy_ctx(i, v - 1, 1)
                    if s == TB:
                        copy_ctx(i, v, 0)
                    if s in TURN_ROWS and not is_last(i, v):
                        copy_rows(i, v + 1, TURN_ROWS[s])

            over_groups(act, group)
            copy_ctx(LOOPS, NU, 1)

        @block.vector
        def _(dve):
            def largest(i, v, n):
                j, t, half = n // (2 * TB), n % (2 * TB) // 2, n % 2
                if n % (2 * TB) == 0:
                    need(dve, split, i, v, GH, j + 1 - GH)
                need(dve, scored, i, v - 1, UNITS, n + 1)
                at = (j * TB + t) * NB + half * 2
                dve.tensor_reduce(mx[:, at:at + 2], ps_s[:, (n % 2) * CHUNK:(n % 2 + 1) * CHUNK]
                                  .rearrange("p (k c) -> p k c", c=KEYS), AX_X, ALU.max).then_inc(maxed, 1)

            def divide(i, v, half):
                need(dve, ctx_turned, i, v, 2, half + 1)
                need(dve, ctx_read, i, v, 2, half)
                strips = ps_m[:, :].rearrange("p (t j c) -> p (t j) c", j=GH, c=32)
                dve.reciprocal(den[:, :].unsqueeze(2), strips[:, :, HD:HD + 1]).then_inc(den_ready, 1)
                need(dve, den_ready, i, v, 2, half + 1)
                at = i * (NU * TB * GCH) + (v * TB + half * TB // 2) * GCH
                dve.tensor_tensor(ctx_all[:, ds(at, CHUNK // P * GCH)].rearrange("p (t c) -> p t c", c=HD),
                                  strips[:, :, 0:HD], den[:, :].unsqueeze(2).to_broadcast([P, GH * GH, HD]),
                                  ALU.mult).then_inc(ctx_read, 1)

            def group(i, v):
                for s in range(STEPS):
                    if not is_last(i, v):
                        for n in range(FROM[s], FROM[s + 1]):
                            largest(i, v + 1, n)
                    if s == 2 and not is_first(i, v):
                        divide(i, v - 1, 1)
                    if s == 10:
                        divide(i, v, 0)

            over_groups(dve, group)
            divide(LOOPS, NU, 1)
            dve.wait_ge(ctx_read, 2 * GROUPS)


def attention_out(nc, st, wo):
    h, ident, ctx_all = (st[x] for x in ("h", "ident", "ctx_all"))
    with ExitStack() as ctx:
        sb, pb, sem = allocators(nc, ctx)
        w_sb = sb("ao_w", [P, C * D], F32)
        stage = sb("ao_stage", [P, TB * D], F32)
        ct = sb("ao_ct", [P, 2 * C * S], F32)
        ps_t = pb("ao_pt", [P, 4 * CHUNK], F32)
        ps_o = pb("ao_po", [P, 2 * CHUNK], F32)
        w_in = sem("ao_w_in")
        staged = sem("ao_staged")
        turned = sem("ao_turned")
        ct_ready = sem("ao_ct_ready")
        out_ready = sem("ao_out_ready")
        added = sem("ao_added")
        block = ctx.enter_context(nc.Block())
        Q = C * NC
        G = TB // 2

        def ct_of(b, c, lo, n):
            return ct[:, (b % 2 * C + c) * S + lo:(b % 2 * C + c) * S + lo + n]

        @block.sync
        def _(sp):
            sp.dma_start(w_sb[:, :].rearrange("p (c n) -> p c n", c=C), wo.rearrange("(c p) n -> p c n", p=P)).then_inc(w_in, 16)

        @block.tensor
        def _(pe):
            def turn(b):
                pe.wait_ge(staged, b + 1)
                for q in range(Q):
                    c, half = q // NC, q % NC
                    need(pe, ct_ready, (b - 1) * Q + q + 1)
                    for j in range(TB // NC):
                        n = half * (TB // NC) + j
                        last = pe.transpose(ps_t[:, q * CHUNK + j * P:q * CHUNK + (j + 1) * P],
                                            stage[:, n * D + c * P:n * D + (c + 1) * P], ident[:, :])
                    last.then_inc(turned, 1)

            def project(b):
                pe.wait_ge(ct_ready, (b + 1) * Q)
                for g in range(G):
                    need(pe, added, b * G + g - 1)
                    for j in range(2):
                        n = 2 * g + j
                        for c in range(C):
                            last = pe.matmul(ps_o[:, (g % 2) * CHUNK + j * D:(g % 2) * CHUNK + (j + 1) * D],
                                             ct_of(b, c, n * P, P), w_sb[:, c * D:(c + 1) * D],
                                             start=(c == 0), stop=(c == C - 1))
                    last.then_inc(out_ready, 1)

            turn(0)
            pe.wait_ge(w_in, 16)
            for b in range(B):
                if b < B - 1:
                    turn(b + 1)
                project(b)

        @block.scalar
        def _(act):
            for b in range(B):
                if b >= 2:
                    act.wait_ge(out_ready, (b - 1) * G)
                for q in range(Q):
                    c, half = q // NC, q % NC
                    act.wait_ge(turned, b * Q + q + 1)
                    act.activation(ct_of(b, c, half * CHUNK, CHUNK), ps_t[:, q * CHUNK:(q + 1) * CHUNK],
                                   ACT.Copy).then_inc(ct_ready, 1)

        @block.vector
        def _(dve):
            def gather(b):
                need(dve, turned, b * Q)
                for k in range(GROUPS // B):
                    at = (b * (GROUPS // B) + k) * TB * GCH
                    last = dve.tensor_copy(stage[:, :].rearrange("p (n g c) -> p n g c", g=GROUPS // B, c=GCH)[:, :, k, :],
                                           ctx_all[:, at:at + TB * GCH].rearrange("p (n c) -> p n c", c=GCH))
                last.then_inc(staged, 1)

            gather(0)
            for b in range(B):
                if b < B - 1:
                    gather(b + 1)
                for g in range(G):
                    dve.wait_ge(out_ready, b * G + g + 1)
                    at = (b * TB + 2 * g) * D
                    dve.tensor_tensor(h[:, at:at + 2 * D], h[:, at:at + 2 * D], ps_o[:, (g % 2) * CHUNK:(g % 2 + 1) * CHUNK],
                                      ALU.add).then_inc(added, 1)
            dve.wait_ge(added, B * G)


CAP = T // E
BITS = 30


def dispatch_capacity(nc, st):
    logits, gates = st["logits"], st["gates"]
    with ExitStack() as ctx:
        sb, pb, sem = allocators(nc, ctx)
        t = routing_tables(sb, "d1", st)
        W = NT * E
        new = lambda name, n, dt=F32: sb("d1_" + name, [P, n], dt)[:, :]
        probs, cmp, sel, eq, onehot, vals = (new(x, W) for x in ("probs", "cmp", "sel", "eq", "onehot", "vals"))
        top, total, cmax = (new(x, NT) for x in ("top", "sum", "cmax"))
        counts, need = (new(x, E) for x in ("counts", "need"))
        level, trial, keep = (new(x, E, I32) for x in ("level", "trial", "keep"))
        bits_i = new("bits_i", BITS, I32)
        ps_rank = pb("d1_ps", [P, 2 * W], F32)
        ps_cnt = pb("d1_pc", [P, CHUNK], F32)
        own = sem("d1_own")
        shifted = sem("d1_shifted")
        exp_ready = sem("d1_exp_ready")
        counted = sem("d1_counted")
        summed = sem("d1_summed")
        eq_ready = sem("d1_eq_ready")
        ranked = sem("d1_ranked")
        block = ctx.enter_context(nc.Block())
        by = lambda a: a.rearrange("p (n e) -> p n e", e=E)
        over_tiles = lambda a: a.rearrange("p (n e) -> p e n", e=E)
        per_e = lambda a: a.unsqueeze(1).to_broadcast([P, NT, E])
        per_n = lambda a: a.unsqueeze(2).to_broadcast([P, NT, E])
        UNROLL = 5
        BIT_STEPS = 4

        @block.tensor
        def _(pe):
            with pe.Fori(0, BITS // UNROLL) as i:
                for k in range(UNROLL):
                    pe.wait_ge(counted, i * UNROLL + k + 1)
                    pe.matmul(ps_cnt[:, 0:E], st["ones"][:, :], counts, start=True, stop=True).then_inc(summed, 1)
            pe.wait_ge(counted, BITS + 1)
            pe.matmul(ps_cnt[:, 0:E], st["ones"][:, :], counts, start=True, stop=True).then_inc(summed, 1)
            for k in range(2):
                pe.wait_ge(eq_ready, k + 1)
                src = eq if k == 0 else onehot
                pe.matmul(ps_rank[:, 0:W], st["before"][:, :], src, start=True, stop=True)
                pe.matmul(ps_rank[:, W:2 * W], st["ones"][:, :], src, start=True, stop=True).then_inc(ranked, 1)

        @block.scalar
        def _(act):
            act.wait_ge(shifted, 1)
            act.activation(vals, vals, ACT.Exp).then_inc(exp_ready, 1)

        @block.vector
        def _(dve):
            s = Steps(dve, own)
            s.step(dve.tensor_reduce(top, by(logits[:, :]), AX_X, ALU.max))
            dve.tensor_tensor(by(vals), by(logits[:, :]), per_n(top), ALU.subtract).then_inc(shifted, 1)
            s.step(dve.memset(level, 0))
            s.step(dve.tensor_copy(bits_i, st["bits"][:, :]))
            dve.wait_ge(exp_ready, 1)
            s.step(dve.tensor_reduce(total, by(vals), AX_X, ALU.add))
            s.step(dve.reciprocal(cmax, total))
            s.step(dve.tensor_tensor(by(probs), by(vals), per_n(cmax), ALU.mult))
            before = s.n
            with dve.Fori(0, BITS // UNROLL) as i:
                s = Steps(dve, own, i * (UNROLL * BIT_STEPS) + before)
                for k in range(UNROLL):
                    b = i * UNROLL + k
                    s.step(dve.tensor_tensor(trial, level, bits_i[:, ds(b, 1)].to_broadcast([P, E]), ALU.bitwise_or))
                    s.step(dve.tensor_tensor(by(cmp), by(probs), per_e(trial.bitcast(F32)), ALU.is_ge))
                    dve.tensor_reduce(counts, over_tiles(cmp), AX_X, ALU.add).then_inc(counted, 1)
                    dve.wait_ge(summed, b + 1)
                    s.step(dve.scalar_tensor_tensor(out=keep, in0=ps_cnt[:, 0:E], scalar=CAP - 0.5,
                                                    in1=st["bits"][:, ds(b, 1)].to_broadcast([P, E]), op0=ALU.is_ge, op1=ALU.mult))
                    s.step(dve.tensor_tensor(level, level, keep, ALU.bitwise_or))
                assert s.n == UNROLL * BIT_STEPS
            s = Steps(dve, own, before + BITS * BIT_STEPS)
            level_f = level.bitcast(F32)
            s.step(dve.tensor_tensor(by(sel), by(probs), per_e(level_f), ALU.is_gt))
            dve.tensor_reduce(counts, over_tiles(sel), AX_X, ALU.add).then_inc(counted, 1)
            dve.tensor_tensor(by(eq), by(probs), per_e(level_f), ALU.is_equal).then_inc(eq_ready, 1)
            dve.wait_ge(summed, BITS + 1)
            s.step(dve.tensor_scalar(need, ps_cnt[:, 0:E], -1.0, float(CAP), ALU.mult, ALU.add))
            dve.wait_ge(ranked, 1)
            s.mark(dve.tensor_copy(t["rank"], ps_rank[:, 0:W]))
            s.step(dve.tensor_copy(t["total"], ps_rank[:, W:2 * W]))
            for e in range(E):
                s.mark(dve.tensor_tensor_scan(t["incl"][:, e::E], t["one"].to_broadcast([P, NT]), t["total"][:, e::E],
                                              0.0, ALU.mult, ALU.add))
            s.wait()
            s.step(dve.tensor_tensor(t["rank"], t["rank"], t["incl"], ALU.add))
            s.step(dve.tensor_tensor(t["rank"], t["rank"], t["total"], ALU.subtract))
            s.step(dve.tensor_tensor(by(cmp), by(t["rank"]), per_e(need), ALU.is_lt))
            dve.wait_ge(eq_ready, 1)
            s.step(dve.tensor_tensor(cmp, cmp, eq, ALU.mult))
            s.step(dve.tensor_tensor(sel, sel, cmp, ALU.add))
            s.step(dve.tensor_reduce(top, by(sel), AX_X, ALU.max))
            s.step(dve.tensor_scalar(top, top, -1.0, 1.0, ALU.mult, ALU.add))
            s.step(dve.tensor_tensor(by(sel), by(sel), per_n(top), ALU.max))
            s.step(dve.tensor_tensor(cmp, probs, sel, ALU.mult))
            s.step(dve.scalar_tensor_tensor(out=vals, in0=sel, scalar=-1.0, in1=cmp, op0=ALU.add, op1=ALU.add))
            first_of_max(dve, s, by(vals), top, by(cmp), st["rev"][:, :], cmax, by(onehot))
            dve.nop().then_inc(eq_ready, 1)
            s.step(dve.tensor_tensor(cmp, probs, onehot, ALU.mult))
            s.step(dve.tensor_reduce(gates[:, 0:NT], by(cmp), AX_X, ALU.add))
            dve.wait_ge(ranked, 2)
            slots_of(dve, s, t, ps_rank, T // P + E)
            s.step(dve.tensor_tensor(onehot, onehot, t["rank"], ALU.mult))
            s.step(dve.tensor_reduce(st["pos"][:, 0:NT], by(onehot), AX_X, ALU.add))


CONSTS = (("before", P), ("ones", P), ("rev", E), ("starts", 2 * NT + E), ("bits", BITS), ("count", P),
          ("number", 2 * NT), ("slot_number", 2 * NT + E))


def tower(nc, a, out):
    TILES0, TILES1 = 2 * NT + E, NT + E
    xn0, xn1 = (nc.dram_tensor(n, [T, D], F32).ap() for n in ("xn0", "xn1"))
    y0 = nc.dram_tensor("y0", [2 * T + TILES0 * P, D], F32).ap()
    y1 = nc.dram_tensor("y1", [T + TILES1 * P, D], F32).ap()
    qk_dram = nc.dram_tensor("qk_groups", [GROUPS, 2, PARTS, GCH, S], BF16).ap()
    v_dram = nc.dram_tensor("v_groups", [GROUPS, S, P], F32).ap()
    with ExitStack() as ctx:
        sb, pb, sem = allocators(nc, ctx)
        st = {"h": sb("h", [P, NT * D], F32), "ident": sb("ident", [P, P], F32), "mv": sb("mv", [P, 2 * NT], F32),
              "rstd": sb("rstd", [P, NT], F32), "logits": sb("logits", [P, NT * E], F32),
              "gates": sb("gates", [P, 2 * NT], F32), "pos": sb("pos", [P, 2 * NT], F32), "slot_rows": sb("slot_rows", [P, 2 * TILES0], I32),
              "tile_ei": sb("tile_ei", [P, 2 * NT + E], I32)}
        for name, n in CONSTS:
            st[name] = sb(name, [P, n], F32)
        experts0_in = sem("experts0_in")
        experts1_in = sem("experts1_in")

        embed(nc, st, a["tok"], a["L0_tok_emb"], a["c_pos"], a["L0_tok_alpha"], a["L0_tok_beta"],
              [(name, a["c_" + name]) for name, _ in CONSTS])
        rwkv(nc, st, *(a["L0_attn_" + n] for n in ("W", "U", "time_mix_k", "time_mix_v", "time_mix_r", "Wk", "Wv", "Wr", "Wo")))
        with ExitStack() as moe:
            for n in ("w1_sb", "w2_sb"):
                st[n] = moe.enter_context(nc.sbuf_tensor("l0_" + n, [P, E * C * HID], F32))
            route(nc, st, "g0", a["L0_ffn_Wr"], a["L0_ffn_br"], xn0, a["L0_ffn_W1"], a["L0_ffn_W2"], experts0_in)
            dispatch_top2(nc, st)
            slot_table(nc, st, "s0", 2, TILES0)
            experts(nc, st, "x0", TILES0, xn0, y0, a["L0_ffn_b1"], a["L0_ffn_b2"], ACT.Relu, experts0_in)
        combine_top2(nc, st, y0)
        with nc.sbuf_tensor("ctx_all", [P, NT * D], F32) as st["ctx_all"], \
                nc.sbuf_tensor("mx", [P, GH * TB * NB], F32) as st["mx"]:
            project_qkv(nc, st, a["L1_attn_w_q"], a["L1_attn_w_k"], a["L1_attn_w_v"], a["c_v_ones"], qk_dram, v_dram)
            attention(nc, st, qk_dram, v_dram, a["c_block_rows"], a["c_ident_bits"])
            attention_out(nc, st, a["L1_attn_w_o"])
        with ExitStack() as moe:
            for n in ("w1_sb", "w2_sb"):
                st[n] = moe.enter_context(nc.sbuf_tensor("l1_" + n, [P, E * C * HID], F32))
            route(nc, st, "g1", a["L1_ffn_Wg"], None, xn1, a["L1_ffn_W1"], a["L1_ffn_W2"], experts1_in)
            dispatch_capacity(nc, st)
            slot_table(nc, st, "s1", 1, TILES1)
            experts(nc, st, "x1", TILES1, xn1, y1, None, None, ACT.Gelu, experts1_in)
        combine_top1(nc, st, y1, out)


def shape_constants():
    position = np.arange(S, dtype=np.float32)[:, None]
    step = np.arange(0, D, 2, dtype=np.float32) * np.float32(-np.log(10000.0) / D)
    angle = (position * np.exp(step.astype(np.float64)).astype(np.float32)).astype(np.float64)
    BF16_ONE = 0x3F80
    rows = np.zeros((MROWS, GH, S), np.uint16)
    for k in range(NB):
        rows[k * PARTS:(k + 1) * PARTS, :, k * KEYS:(k + 1) * KEYS] = BF16_ONE
    ones = np.zeros((HEADS, 32), np.float32)
    ones[:, HD] = 1.0
    spread = lambda v: np.ascontiguousarray(np.broadcast_to(v.astype(np.float32), (P, v.size)))
    return {
        "c_pos": np.stack([np.sin(angle), np.cos(angle)], axis=-1).reshape(S, D).astype(np.float32),
        "c_before": np.triu(np.ones((P, P), np.float32), 1),
        "c_ones": np.ones((P, P), np.float32),
        "c_rev": spread(E - np.arange(E)),
        "c_starts": spread(P * np.arange(2 * NT + E)),
        "c_count": spread(np.arange(P)),
        "c_number": (1.0 + np.arange(2 * T).reshape(2 * NT, P).T).astype(np.float32),
        "c_slot_number": np.arange((2 * NT + E) * P).reshape(2 * NT + E, P).T.astype(np.float32),
        "c_bits": spread(2.0 ** np.arange(BITS - 1, -1, -1)),
        "c_block_rows": rows.reshape(MROWS, GH * S),
        "c_ident_bits": np.eye(P, dtype=np.uint16) * np.uint16(BF16_ONE),
        "c_v_ones": ones.reshape(-1),
    }


def laid_out(inputs):
    a = {n: np.ascontiguousarray(v) for n, v in inputs.items() if n != "x"}
    a["tok"] = np.ascontiguousarray(inputs["x"].reshape(NT, P).T)
    for n in ("Wk", "Wv", "Wr", "Wo"):
        a["L0_attn_" + n] = np.ascontiguousarray(a["L0_attn_" + n].T)
    for n in ("W", "U", "time_mix_k", "time_mix_v", "time_mix_r"):
        a["L0_attn_" + n] = np.ascontiguousarray(a["L0_attn_" + n].reshape(C, P).T)
    a["L0_ffn_b1"] = np.ascontiguousarray(a["L0_ffn_b1"].reshape(E * HC, P).T)
    return a


def kernel(**inputs):
    import concourse.bacc as bacc
    from concourse.bass_utils import run_bass_kernel_spmd

    nc = bacc.Bacc("TRN2", target_bir_lowering=False, num_devices=1)
    arrays = {**laid_out({n: np.asarray(v) for n, v in inputs.items()}), **shape_constants()}
    a = {n: nc.dram_tensor("in_" + n, list(v.shape), mybir.dt.from_np(v.dtype), kind="ExternalInput").ap()
         for n, v in arrays.items()}
    out = nc.dram_tensor("out_h", [B, S, D], F32, kind="ExternalOutput").ap()
    tower(nc, a, out)
    r = run_bass_kernel_spmd(nc, [{"in_" + n: v for n, v in arrays.items()}], core_ids=[0])
    return r.results[0]["out_h"]
```
